# Optimizing a Trainium2 kernel written in Bass

```python
import numpy as np
import jax
import jax.numpy as jnp

def _softmax(x, axis=-1):
    return jax.nn.softmax(x, axis=axis)

def _gelu(x):
    return jax.nn.gelu(x, approximate=True)

def _silu(x):
    return jax.nn.silu(x)

def _sigmoid(x):
    return jax.nn.sigmoid(x)

def _layernorm(x, axis=-1, eps=1e-05):
    m = jnp.mean(x, axis=axis, keepdims=True)
    v = jnp.var(x, axis=axis, keepdims=True)
    return (x - m) / jnp.sqrt(v + eps)

def _scatter_add(tgt, idx, src, axis=0):
    return tgt.at[idx].add(src)

def _segment_sum(src, seg, n):
    return jax.ops.segment_sum(src, seg, n)
kernel_name = 'mk_xattn_ffn_d2_seqx_r4_6a32d1'

def setup_inputs(seed: int=0):
    np.random.seed(seed)
    _w = jnp.asarray

    def _rec_inputs():
        import jax
        import jax.numpy as jnp
        _rk = jax.random.key(seed)
        x = -0.0002928 + 1 * jax.random.normal(jax.random.fold_in(_rk, 1), (2, 1024, 256), jnp.float32)
        _lenS = 1024 - jax.random.randint(jax.random.fold_in(_rk, 7), (2,), 0, max(1, 1024 // 4) + 1, jnp.int32)
        _lenS2 = 154 - jax.random.randint(jax.random.fold_in(_rk, 8), (2,), 0, max(1, 154 // 4) + 1, jnp.int32)
        _ctx_1024P = jax.random.normal(jax.random.fold_in(_rk, 11), (2, 16, 256), jnp.float32)
        _ctx_1024c = jax.random.dirichlet(jax.random.fold_in(_rk, 511), 0.3 * jnp.ones((16,), jnp.float32), (2, 154))
        _ctx_1024t = jnp.einsum('bsk,bkd->bsd', _ctx_1024c, _ctx_1024P)
        _ctx_1024t = _ctx_1024t * jax.lax.rsqrt(jnp.mean(jnp.square(_ctx_1024t)) + 1e-12) * 0.953939
        ctx_1024 = -1.39393e-06 + 0.999914 * (_ctx_1024t + 0.3 * jax.random.normal(jax.random.fold_in(_rk, 611), (2, 154, 256), jnp.float32))
        fside_BxSxS2_0 = -1.47943e-05 + 1.00017 * jax.random.normal(jax.random.fold_in(_rk, 13), (2, 1024, 154), jnp.float32)
        _validS = jnp.arange(1024)[None, :] < _lenS[:, None]
        _validS2 = jnp.arange(154)[None, :] < _lenS2[:, None]
        _causal = jnp.tril(jnp.ones((1024, 1024), dtype=bool))
        mask_BxSxS2_ik0 = jnp.where(jnp.broadcast_to(_validS2[:, None, :], (2, 1024, 154)), 0, 1).astype(jnp.int32)
        return (x, ctx_1024, fside_BxSxS2_0, mask_BxSxS2_ik0)
    x, ctx_1024, fside_BxSxS2_0, mask_BxSxS2_ik0 = _rec_inputs()

    def _L0_xattn_setup():
        import jax, jax.numpy as jnp
        import numpy as np
        D_MODEL = 256
        N_HEADS = 16
        D_K = D_MODEL // N_HEADS
        B, S = (2, 512)
        NEG = -1000000000.0
        key = jax.random.key(seed)
        ks = jax.random.split(key, 12)
        sc = 1.0 / np.sqrt(D_MODEL)
        inp = {'query': jax.random.normal(ks[0], (B, S, D_MODEL), jnp.float32), 'key': jax.random.normal(ks[1], (B, S, D_MODEL), jnp.float32), 'value': jax.random.normal(ks[2], (B, S, D_MODEL), jnp.float32), 'mask': jnp.broadcast_to(jnp.tril(jnp.ones((S, S), jnp.int32)), (B, S, S)), 'wq': jax.random.normal(ks[3], (D_MODEL, D_MODEL), jnp.float32) * sc, 'bq': jnp.zeros((D_MODEL,), jnp.float32), 'wk': jax.random.normal(ks[4], (D_MODEL, D_MODEL), jnp.float32) * sc, 'bk': jnp.zeros((D_MODEL,), jnp.float32), 'wv': jax.random.normal(ks[5], (D_MODEL, D_MODEL), jnp.float32) * sc, 'bv': jnp.zeros((D_MODEL,), jnp.float32), 'wo': jax.random.normal(ks[6], (D_MODEL, D_MODEL), jnp.float32) * sc, 'bo': jnp.zeros((D_MODEL,), jnp.float32)}
        return inp
    _L0_xattn_all = _L0_xattn_setup()
    _L0_xattn_in = {k: v for k, v in _L0_xattn_all.items() if k in ('wq', 'bq', 'wk', 'bk', 'wv', 'bv', 'wo', 'bo')}
    del _L0_xattn_all

    def _L0_ffn_setup():
        import jax, jax.numpy as jnp
        import numpy as np
        B, S, H = (2, 512, 256)
        E, I, K = (8, 1024, 2)

        def _moe_forward(x, gate_w, wg, wu, wd):
            b, s, h = x.shape
            x_flat = x.reshape(-1, h)
            logits = x_flat @ gate_w.T
            top_v, top_i = jax.lax.top_k(logits, K)
            probs = jax.nn.softmax(top_v.astype(jnp.float32), axis=-1).astype(logits.dtype)
            one_hot = jax.nn.one_hot(top_i, E, dtype=probs.dtype)
            combine = jnp.einsum('tk,tke->et', probs, one_hot)

            def body(acc, ws):
                wge, wue, wde, we = ws
                hidden = jax.nn.silu(x_flat @ wge.T) * (x_flat @ wue.T)
                return (acc + we[:, None] * (hidden @ wde.T), None)
            out, _ = jax.lax.scan(body, jnp.zeros_like(x_flat), (wg, wu, wd, combine))
            return out.reshape(b, s, h)
        key = jax.random.key(seed)
        ks = jax.random.split(key, 5)
        scale_h = 1.0 / np.sqrt(H)
        scale_i = 1.0 / np.sqrt(I)
        x = jax.random.normal(ks[0], (B, S, H), dtype=jnp.float32)
        gate_w = jax.random.normal(ks[1], (E, H), dtype=jnp.float32) * scale_h
        wg = jax.random.normal(ks[2], (E, I, H), dtype=jnp.float32) * scale_h
        wu = jax.random.normal(ks[3], (E, I, H), dtype=jnp.float32) * scale_h
        wd = jax.random.normal(ks[4], (E, H, I), dtype=jnp.float32) * scale_i
        return {'x': x, 'gate_w': gate_w, 'wg': wg, 'wu': wu, 'wd': wd}
    _L0_ffn_all = _L0_ffn_setup()
    _L0_ffn_in = {k: v for k, v in _L0_ffn_all.items() if k in ('gate_w', 'wg', 'wu', 'wd')}
    del _L0_ffn_all

    def _L1_xattn_setup():
        import jax, jax.numpy as jnp
        import numpy as np
        D = 256
        key = jax.random.key(seed)
        ks = jax.random.split(key, 13)
        B, S, d = (4, 512, D)
        inp = {'q_in': jax.random.normal(ks[0], (B, S, d), jnp.float32), 'k_in': jax.random.normal(ks[1], (B, S, d), jnp.float32), 'v_in': jax.random.normal(ks[2], (B, S, d), jnp.float32), 'phi_risk': jax.random.normal(ks[3], (B, S, S), jnp.float32), 'phi_prio': jax.random.normal(ks[4], (B, S, S), jnp.float32), 'phi_impl': jax.random.normal(ks[5], (B, S, S), jnp.float32), 'Wq': jax.random.normal(ks[6], (d, d), jnp.float32) / np.sqrt(d), 'bq': jax.random.normal(ks[7], (d,), jnp.float32) * 0.01, 'Wk': jax.random.normal(ks[8], (d, d), jnp.float32) / np.sqrt(d), 'bk': jax.random.normal(ks[9], (d,), jnp.float32) * 0.01, 'Wv': jax.random.normal(ks[10], (d, d), jnp.float32) / np.sqrt(d), 'bv': jax.random.normal(ks[11], (d,), jnp.float32) * 0.01, 'beta_risk': jnp.float32(0.1), 'beta_prio': jnp.float32(0.1), 'beta_impl': jnp.float32(0.1)}
        return inp
    _L1_xattn_all = _L1_xattn_setup()
    _L1_xattn_in = {k: v for k, v in _L1_xattn_all.items() if k in ('Wq', 'bq', 'Wk', 'bk', 'Wv', 'bv', 'beta_risk', 'beta_prio', 'beta_impl')}
    del _L1_xattn_all

    def _L1_ffn_setup():
        import jax, jax.numpy as jnp
        import numpy as np
        B, C, D = (2, 512, 256)
        I = 512
        E, K = (8, 2)
        CF = 1.25
        key = jax.random.key(seed)
        k1, k2, k3, k4 = jax.random.split(key, 4)
        scale = 0.02
        return {'hidden_states': jax.random.normal(k1, (B, C, D), jnp.float32), 'Wg': jax.random.normal(k2, (E, D), jnp.float32) * scale, 'W1': jax.random.normal(k3, (E, D, 2 * I), jnp.float32) * scale, 'W2': jax.random.normal(k4, (E, I, D), jnp.float32) * scale}
    _L1_ffn_all = _L1_ffn_setup()
    _L1_ffn_in = {k: v for k, v in _L1_ffn_all.items() if k in ('Wg', 'W1', 'W2')}
    del _L1_ffn_all
    return {'x': x, 'ctx_1024': ctx_1024, 'fside_BxSxS2_0': fside_BxSxS2_0, 'mask_BxSxS2_ik0': mask_BxSxS2_ik0, 'L0_xattn_wq': _L0_xattn_in['wq'], 'L0_xattn_bq': _L0_xattn_in['bq'], 'L0_xattn_wk': _L0_xattn_in['wk'], 'L0_xattn_bk': _L0_xattn_in['bk'], 'L0_xattn_wv': _L0_xattn_in['wv'], 'L0_xattn_bv': _L0_xattn_in['bv'], 'L0_xattn_wo': _L0_xattn_in['wo'], 'L0_xattn_bo': _L0_xattn_in['bo'], 'L0_ffn_gate_w': _L0_ffn_in['gate_w'], 'L0_ffn_wg': _L0_ffn_in['wg'], 'L0_ffn_wu': _L0_ffn_in['wu'], 'L0_ffn_wd': _L0_ffn_in['wd'], 'L1_xattn_Wq': _L1_xattn_in['Wq'], 'L1_xattn_bq': _L1_xattn_in['bq'], 'L1_xattn_Wk': _L1_xattn_in['Wk'], 'L1_xattn_bk': _L1_xattn_in['bk'], 'L1_xattn_Wv': _L1_xattn_in['Wv'], 'L1_xattn_bv': _L1_xattn_in['bv'], 'L1_xattn_beta_risk': _L1_xattn_in['beta_risk'], 'L1_xattn_beta_prio': _L1_xattn_in['beta_prio'], 'L1_xattn_beta_impl': _L1_xattn_in['beta_impl'], 'L1_ffn_Wg': _L1_ffn_in['Wg'], 'L1_ffn_W1': _L1_ffn_in['W1'], 'L1_ffn_W2': _L1_ffn_in['W2']}

def reference(x, ctx_1024, fside_BxSxS2_0, mask_BxSxS2_ik0, L0_xattn_wq, L0_xattn_bq, L0_xattn_wk, L0_xattn_bk, L0_xattn_wv, L0_xattn_bv, L0_xattn_wo, L0_xattn_bo, L0_ffn_gate_w, L0_ffn_wg, L0_ffn_wu, L0_ffn_wd, L1_xattn_Wq, L1_xattn_bq, L1_xattn_Wk, L1_xattn_bk, L1_xattn_Wv, L1_xattn_bv, L1_xattn_beta_risk, L1_xattn_beta_prio, L1_xattn_beta_impl, L1_ffn_Wg, L1_ffn_W1, L1_ffn_W2):
    import jax
    import jax.numpy as jnp

    def _L0_xattn_ref(query, key, value, mask, wq, bq, wk, bk, wv, bv, wo, bo):
        import jax, jax.numpy as jnp
        import numpy as np
        D_MODEL = 256
        N_HEADS = 16
        D_K = D_MODEL // N_HEADS
        B, S = (2, 512)
        NEG = -1000000000.0
        b, sq, _ = query.shape
        sk = key.shape[1]

        def proj(x, w, bias, s):
            return (x @ w + bias).reshape(b, s, N_HEADS, D_K).transpose(0, 2, 1, 3)
        Q = proj(query, wq, bq, sq)
        K = proj(key, wk, bk, sk)
        V = proj(value, wv, bv, sk)
        scores = jnp.einsum('bhqd,bhkd->bhqk', Q, K) / np.sqrt(D_K)
        scores = jnp.where(mask[:, None, :, :] == 0, NEG, scores)
        attn = jax.nn.softmax(scores, axis=-1)
        ctx = jnp.einsum('bhqk,bhkd->bhqd', attn, V)
        ctx = ctx.transpose(0, 2, 1, 3).reshape(b, sq, D_MODEL)
        return ctx @ wo + bo

    def _L0_ffn_ref(x, gate_w, wg, wu, wd):
        import jax, jax.numpy as jnp
        import numpy as np
        B, S, H = (2, 512, 256)
        E, I, K = (8, 1024, 2)

        def _moe_forward(x, gate_w, wg, wu, wd):
            b, s, h = x.shape
            x_flat = x.reshape(-1, h)
            logits = x_flat @ gate_w.T
            top_v, top_i = jax.lax.top_k(logits, K)
            probs = jax.nn.softmax(top_v.astype(jnp.float32), axis=-1).astype(logits.dtype)
            one_hot = jax.nn.one_hot(top_i, E, dtype=probs.dtype)
            combine = jnp.einsum('tk,tke->et', probs, one_hot)

            def body(acc, ws):
                wge, wue, wde, we = ws
                hidden = jax.nn.silu(x_flat @ wge.T) * (x_flat @ wue.T)
                return (acc + we[:, None] * (hidden @ wde.T), None)
            out, _ = jax.lax.scan(body, jnp.zeros_like(x_flat), (wg, wu, wd, combine))
            return out.reshape(b, s, h)
        return _moe_forward(x, gate_w, wg, wu, wd)

    def _L1_xattn_ref(q_in, k_in, v_in, phi_risk, phi_prio, phi_impl, Wq, bq, Wk, bk, Wv, bv, beta_risk, beta_prio, beta_impl):
        import jax, jax.numpy as jnp
        import numpy as np
        D = 256
        d = q_in.shape[-1]
        scale = jnp.asarray(d, q_in.dtype) ** (-0.5)
        Q = q_in @ Wq.T + bq
        K = k_in @ Wk.T + bk
        V = v_in @ Wv.T + bv
        att = jnp.einsum('bsd,btd->bst', Q, K) * scale
        att = att + beta_risk * phi_risk + beta_prio * phi_prio - beta_impl * phi_impl
        w = jax.nn.softmax(att, axis=-1)
        return jnp.einsum('bst,btd->bsd', w, V)

    def _L1_ffn_ref(hidden_states, Wg, W1, W2):
        import jax, jax.numpy as jnp
        import numpy as np
        B, C, D = (2, 512, 256)
        I = 512
        E, K = (8, 2)
        CF = 1.25
        Bx, Cx, d = hidden_states.shape
        N = Bx * Cx
        cap = int(N * K * CF / E)
        x = hidden_states.reshape(N, d)
        logits = x @ Wg.T
        top_v, top_i = jax.lax.top_k(logits, K)
        gates = jax.nn.softmax(top_v, axis=-1)
        flat_e = top_i.reshape(N * K)
        gates_f = gates.reshape(N * K)
        tok = jnp.repeat(jnp.arange(N), K)
        onehot = jax.nn.one_hot(flat_e, E, dtype=jnp.int32)
        pos = jnp.cumsum(onehot, axis=0) - 1
        pos_f = jnp.take_along_axis(pos, flat_e[:, None], axis=1)[:, 0]
        keep = pos_f < cap
        pos_safe = jnp.where(keep, pos_f, cap)
        exp_batches = jnp.zeros((E, cap, d), x.dtype).at[flat_e, pos_safe].set(x[tok], mode='drop')
        h = jnp.einsum('ecd,edf->ecf', exp_batches, W1)
        inp, gate = jnp.split(h, 2, axis=-1)
        h = jax.nn.gelu(inp, approximate=False) * gate
        exp_out = jnp.einsum('eci,eid->ecd', h, W2)
        gathered = exp_out[flat_e, jnp.minimum(pos_safe, cap - 1)]
        contrib = jnp.where(keep, gates_f, 0.0)[:, None] * gathered
        out = jax.ops.segment_sum(contrib, tok, num_segments=N)
        return out.reshape(Bx, Cx, d)
    x = x + _L0_xattn_ref(_layernorm(x, axis=-1), ctx_1024, ctx_1024, mask_BxSxS2_ik0, L0_xattn_wq, L0_xattn_bq, L0_xattn_wk, L0_xattn_bk, L0_xattn_wv, L0_xattn_bv, L0_xattn_wo, L0_xattn_bo)
    x = x + _L0_ffn_ref(_layernorm(x, axis=-1), L0_ffn_gate_w, L0_ffn_wg, L0_ffn_wu, L0_ffn_wd)
    x = x + _L1_xattn_ref(_layernorm(x, axis=-1), ctx_1024, ctx_1024, fside_BxSxS2_0, fside_BxSxS2_0, fside_BxSxS2_0, L1_xattn_Wq, L1_xattn_bq, L1_xattn_Wk, L1_xattn_bk, L1_xattn_Wv, L1_xattn_bv, L1_xattn_beta_risk, L1_xattn_beta_prio, L1_xattn_beta_impl)
    x = x + _L1_ffn_ref(_layernorm(x, axis=-1), L1_ffn_Wg, L1_ffn_W1, L1_ffn_W2)
    return x

_drawn_inputs = setup_inputs


def setup_inputs(seed=0):
    import zlib

    import numpy as np

    out = dict(_drawn_inputs(seed))
    spreads = {'L0_xattn_bq': (0.0, 0.1),
     'L0_xattn_bk': (0.0, 0.8),
     'L0_xattn_bv': (0.0, 0.1),
     'L0_xattn_bo': (0.0, 0.1)}
    factors = {'fside_BxSxS2_0': 6.761,
     'L1_xattn_bq': 8.0,
     'L1_xattn_bk': 8.0,
     'L1_xattn_bv': 7.549,
     'L1_ffn_Wg': 5.08,
     'L1_ffn_W1': 4.457,
     'L1_ffn_W2': 4.377}
    for name, (base, spread) in spreads.items():
        noise = np.random.default_rng([zlib.crc32(name.encode()), seed]).standard_normal(out[name].shape)
        drawn = base * np.exp(spread * noise) if base else spread * noise
        out[name] = jnp.asarray(drawn.astype(out[name].dtype))
    for name, factor in factors.items():
        out[name] = (out[name] * factor).astype(out[name].dtype)
    return out
```

```python
from contextlib import ExitStack

import concourse.bass as bass
from concourse import mybir

ALU = mybir.AluOpType
ACT = mybir.ActivationFunctionType
AX = mybir.AxisListType.X
F32, F16, BF16 = mybir.dt.float32, mybir.dt.float16, mybir.dt.bfloat16
I32, U32 = mybir.dt.int32, mybir.dt.uint32

P = 128
D = 256
KC = D // P
H = 16
DK = D // H
B = 2
E = 8
TOP = 2
N = 2048
NT = N // P
GT = 4
NG = NT // GT
GW = GT * P
SK = 154
KM = P
KR = SK - KM
QW = 32
VW = 2 * DK + 1
PENALTY = -1e30
BLK = 256
REGION = N + BLK
MAXBLK = N * TOP // BLK + E
FAR = 1 << 20
EPS = 1e-5


class Chain:

    def __init__(self, eng, sem):
        self.eng, self.sem, self.n = eng, sem, 0

    def __call__(self, ins):
        self.n += 1
        ins.then_inc(self.sem, 1)

    def settle(self):
        self.eng.wait_ge(self.sem, self.n)


def two_layers(nc, a, out):
    with ExitStack() as ctx:
        def sb(name, shape, dt=F32):
            return ctx.enter_context(nc.sbuf_tensor(name, shape, dt))

        sems = {}

        def S(name):
            if name not in sems:
                sems[name] = ctx.enter_context(nc.semaphore(name))
            return sems[name]

        ps = ctx.enter_context(nc.psum_tensor("ps", [P, 8, 512], F32))
        psh = ps[:, :, :].bitcast(F16)
        psb = ps[:, :, :].bitcast(BF16)

        rows = nc.dram_tensor("rows", (E * REGION, 2 * D), F16, kind="Internal").ap()
        results = nc.dram_tensor("results", (MAXBLK * BLK, D), F32, kind="Internal").ap()

        WS = 6144
        probs = sb("probs", [P, 2 * 20 * GW], F16)
        keys = sb("keys", [P, B * 2 * H * SK], F16)
        expo = sb("expo", [P, 2 * 4 * GW], F16)
        queries = sb("queries", [P, 2 * KC * GW], F16)
        inbox = sb("inbox", [P, 2 * 2 * 1664], F16)
        heads = sb("heads", [P, 2 * 2048], F16)
        def part(arena, at, shape, dt=F32, rows=P):
            size = 1
            for n in shape[1:]:
                size *= n
            width = size * (1 if dt in (F16, BF16) else 2)
            v = arena[0:rows, at:at + width]
            if dt != F16:
                v = v.bitcast(dt)
            if len(shape) > 2:
                names = "abcdef"[:len(shape) - 1]
                v = v.rearrange("p (" + " ".join(names) + ") -> p " + " ".join(names), **dict(zip(names[1:], shape[2:])))
            return v, at + width

        ident = sb("ident", [P, P])
        identb = sb("identb", [P, P], BF16)
        identh = sb("identh", [P, P], F16)
        earlier = sb("earlier", [P, P], BF16)
        onesb = sb("onesb", [P, P], BF16)
        iota_i = sb("iota_i", [P, 8], I32)
        iota8 = sb("iota8", [P, 8])
        head_of = sb("head_of", [P, 8], F16)
        quad_of = sb("quad_of", [P, 4], F16)
        m16 = sb("m16", [32, H], BF16)
        msel = sb("msel", [32, H, P], BF16)
        mselr = sb("mselr", [32, H, QW], BF16)
        esel = sb("esel", [32, 4, QW], BF16)
        zeros = sb("zeros", [P, 512])
        thr = sb("thr", [P, 7])
        le = sb("le", [P, 8, 8])

        x = sb("x", [P, NT, D])
        ctxT, at = part(probs, 0, [P, B, KC, SK])
        ctxR, at = part(probs, at, [P, B, KC, 4, QW])
        w_sb = {n: sb("w_" + n, [P, KC, D]) for n in ("wq", "wo", "Wq")}
        for n in ("wk", "wv", "Wk", "Wv"):
            w_sb[n], at = part(probs, at, [P, KC, D])
        v_tmp, at = part(probs, at, [P, D])
        v_hl, at = part(probs, at, [P, 2, D], F16)
        k_tmp, at = part(probs, at, [P, 2, SK], F16)
        bcol = {n: sb("b_" + n, [P, KC]) for n in ("bq", "bk", "Bq", "Bk")}
        brow = {n: sb("b_" + n, [P, D]) for n in ("bv", "bo", "Bv")}
        gate = [sb("gate0", [P, KC, E]), sb("gate1", [P, KC, E])]
        betas = sb("betas", [P, 4])
        phi, keys_at = part(keys, 0, [P, NT, SK])

        mask_raw, at = part(inbox, 0, [P, GT, SK], I32)
        maskT_raw, at = part(inbox, at, [P, GW], I32)
        maskR_raw, at = part(inbox, at, [QW, GW], I32, rows=QW)
        pen = sb("pen", [P, NT, SK], BF16)
        penT = sb("penT", [P, NG, GW], BF16)
        penR = sb("penR", [QW, NG, GW], BF16)

        k_blk, _ = part(keys, 0, [P, B, 2, H, SK], F16)
        k_rem = sb("k_rem", [P, B, 2, H, QW], F16)
        v_ext = sb("v_ext", [P, B, H, VW], F16)
        v_rem = sb("v_rem", [P, B, 4, 4, VW], F16)
        k1T = sb("k1T", [P, B, KC, SK])
        v1m = sb("v1m", [P, B, D])
        v1r = sb("v1r", [QW, B, D])

        stats = sb("stats", [P, GT, 6])
        mv = sb("mv", [P, GT, 2])
        ve = sb("ve", [P, GT])
        ry = sb("ry", [P, GT])
        rt = sb("rt", [P, GT])
        xln = sb("xln", [P, GT, D])
        xlr = sb("xlr", [P, GT, D])
        xT = sb("xT", [P, KC, GW])
        xTr = sb("xTr", [P, KC, GW])
        q_hi, at = part(queries, 0, [P, KC, GW], F16)
        q_lo, at = part(queries, at, [P, KC, GW], F16)
        mx = sb("mx", [P, GT, H])
        nm = sb("nm", [P, GT, 2 * H], BF16)
        nmT = sb("nmT", [2 * H, GW], BF16)
        e_ring, _ = part(expo, 0, [P, 4, GW])
        p_hi, at = part(probs, 0, [P, 20, GW], F16)
        p_lo, _ = part(probs, at, [P, 20, GW], F16)
        o_lo, at = part(heads, 0, [P, 2, 8, DK])
        o_sum, at = part(heads, at, [P, 2, 8, DK])
        o_n, at = part(heads, at, [P, 2, D])
        rden = sb("rden", [P, 2, 8])
        oT = sb("oT", [P, 2, D])
        xo = sb("xo", [P, D])

        att, at = part(expo, 0, [P, GT, SK])
        pT, at = part(expo, at, [P, GW])
        pTr, at = part(expo, at, [QW, GW], rows=QW)
        mx1 = sb("mx1", [P, GT])
        den1 = sb("den1", [P, GT])
        rd1 = sb("rd1", [P, GT])
        q1T, _ = part(queries, 0, [P, KC, GW])

        xp = sb("xp", [P, GT, 2 * D], F16)
        lg = sb("lg", [P, GT, E])
        mx8 = sb("mx8", [P, GT, 8])
        ix8 = sb("ix8", [P, GT, 8], U32)
        dv = sb("dv", [P, GT])
        ev = sb("ev", [P, GT])
        dn = sb("dn", [P, GT])
        sel = sb("sel", [P, GT, E])
        selb = sb("selb", [P, GT, E], BF16)
        cum = sb("cum", [P, GT + 1, E])
        cumb = sb("cumb", [P, GT + 1, E], BF16)
        ohp = sb("ohp", [P, NT, TOP, E])
        posk = sb("posk", [P, GT, TOP])
        drop = sb("drop", [P, GT, TOP])
        slotf = sb("slotf", [P, NT, TOP])
        idxf = sb("idxf", [P, NT, TOP])
        oh = sb("oh", [P, NT, TOP, E])
        pos_kept = sb("pos_kept", [P, NT, TOP])
        weight = sb("weight", [P, NT, TOP])
        slot_s = sb("slot_s", [P, NT, TOP], I32)
        slot_g = sb("slot_g", [P, NT, TOP], I32)
        cnt = sb("cnt", [P, E])
        over = sb("over", [P, E, 7])
        nblk = sb("nblk", [P, E])
        lem = sb("lem", [P, E, E])
        blk_end = sb("blk_end", [P, E])
        blk_row = sb("blk_row", [P, E])
        table = [sb("table0", [1, 16], I32), sb("table1", [1, 16], I32)]

        stage, _ = part(inbox, 0, [P, 2, 1024])
        slot0 = sb("slot0", [P, 2, WS], F16)
        slot1, at = part(probs, 0, [P, 2, WS], F16)
        w_hl = [slot0, slot1]
        h_hi, at = part(probs, at, [P, 8, BLK], F16)
        h_lo, at = part(probs, at, [P, 8, BLK], F16)
        s_act, at = part(probs, at, [P, 2, 2 * BLK])
        x_raw, at = part(probs, at, [P, 2, 2 * D], F16)
        h32, keys_at = part(keys, keys_at, [P, 2, 2 * BLK])
        xbT, keys_at = part(keys, keys_at, [P, 2, KC, BLK], F16)
        yb, keys_at = part(keys, keys_at, [P, 2, D])
        gb, _ = part(heads, 0, [P, 2, TOP, D])

        class Layer:
            pass

        L = [Layer(), Layer()]
        for n, l in enumerate(L):
            l.n, l.r = n, f"r{n}"
            l.I = (1024, 512)[n]
            l.hc = l.I // P
            l.pairs = l.hc // 2
            l.cap = (N, N * TOP * 5 // 4 // E)[n]
            l.act = (ACT.Silu, ACT.Gelu)[n]
            l.gate_col = lambda kc, c, n=n: (kc * 1024 + c * P)
            l.up_col = lambda kc, c, n=n: ((2048, 512)[n] + kc * 1024 + c * P)
            l.down_at = (4096, 2048)[n]
        L[0].chunks = [(a[w], 1024 * i, 2048 * n + 1024 * i) for n, w in enumerate(("wg", "wu", "wd")) for i in range(2)]
        L[1].chunks = [(a["W1"], 0, 0), (a["W1"], 1024, 1024), (a["W2"], 0, 2048)]

        def wait_counted(eng, sem, value):
            eng.wait_ge(sem, value)
            eng.sem_inc(S("counted"), 1)

        block = ctx.enter_context(nc.Block())

        @block.sync
        def _(sp):
            for b in range(B):
                sp.dma_start(ctxT[:, b], a["ctxT"][b].rearrange("(k p) s -> p k s", p=P)).then_inc(S("ld_kv"), 16)
            for n in ("wk", "wv", "Wk", "Wv"):
                sp.dma_start(w_sb[n][:, :, :], a[n].rearrange("(k p) n -> p k n", p=P)).then_inc(S("ld_kv"), 16)
            for n in ("bq", "bk", "Bq", "Bk"):
                sp.dma_start(bcol[n][:, :], a[n]).then_inc(S("ld_kv"), 16)
            for n in ("bv", "bo", "Bv"):
                sp.dma_start(brow[n][:, :], a[n].unsqueeze(0).broadcast_to([P, D])).then_inc(S("ld_kv"), 16)
            for g in range(NG):
                sp.dma_start(x[:, g * GT:(g + 1) * GT, :],
                             a["x"][g * GW:(g + 1) * GW, :].rearrange("(t p) d -> p t d", p=P)).then_inc(S(f"ld_x{g}"), 16)
                if g == 0:
                    for n in ("wq", "wo", "Wq"):
                        sp.dma_start(w_sb[n][:, :, :], a[n].rearrange("(k p) n -> p k n", p=P)).then_inc(S("ld_w"), 16)
                    for n in range(2):
                        sp.dma_start(gate[n][:, :, :], a[f"gate{n}"].rearrange("(k p) e -> p k e", p=P)).then_inc(S("ld_w"), 16)
            for g in range(NG):
                if g:
                    sp.wait_ge(S("mask_used"), 3 * g)
                b, q0 = g // 2, (g % 2) * GW
                sp.dma_start(mask_raw[:, :, :], a["mask"][g * GW:(g + 1) * GW, :].rearrange("(t p) s -> p t s", p=P)).then_inc(S("ld_mask"), 16)
                sp.dma_start(maskT_raw[:, :], a["maskT"][b, 0:KM, q0:q0 + GW]).then_inc(S("ld_mask"), 16)
                sp.dma_start(maskR_raw[0:KR, :], a["maskT"][b, KM:SK, q0:q0 + GW]).then_inc(S("ld_mask"), 16)
            for n in range(3):
                sp.dma_start(betas[:, n:n + 1], a["betas"][n].unsqueeze(0).broadcast_to([P, 1])).then_inc(S("ld_phi"), 16)
            sp.wait_ge(S("zeros_set"), 1)
            rz = rows.rearrange("(n p r s) d -> n p r (s d)", p=P, r=4, s=2)
            for n in range(E * REGION // (P * 8)):
                sp.dma_start(rz[n], zeros[:, :].bitcast(F16).unsqueeze(1).broadcast_to([P, 4, 1024])).then_inc(S("rows_zero"), 16)
            yz = results.rearrange("(n p r s) d -> n p r (s d)", p=P, r=4, s=2)
            for n in range(MAXBLK * BLK // (P * 8)):
                sp.dma_start(yz[n], zeros[:, :].unsqueeze(1).broadcast_to([P, 4, 512])).then_inc(S("results_zero"), 16)

            sp.wait_ge(S("a0_st"), 20 * NG)
            sp.dma_start(phi[:, :, :], a["phi"].rearrange("(t p) s -> p t s", p=P)).then_inc(S("ld_phi"), 16)

            def load_blocks(l):
                r, tb = l.r, table[l.n]
                sp.wait_ge(S(r + "_table"), 1)
                sp.wait_ge(S(r + "_scattered"), 16 * NT * TOP)

                def load(row):
                    sp.dma_start(x_raw[:, :, :], rows[bass.ds(row, BLK), :].rearrange("(h p) d -> p h d", p=P)).then_inc(S(r + "_xraw"), 16)

                with sp.Fori(0, E) as e:
                    first = sp.value_load(tb[0:1, bass.ds(e, 1)], min_val=0, max_val=MAXBLK - 1)
                    end = sp.value_load(tb[0:1, bass.ds(e + 1, 1)], min_val=1, max_val=MAXBLK)
                    with sp.Fori(first, end) as g:
                        sp.wait_ge(S(r + "_xbT_ps"), g + 1)
                        row = nc.s_assert_within(e * REGION + (g - first) * BLK, 0, E * REGION - BLK)
                        load(row)
                total = sp.value_load(tb[0:1, 8:9], min_val=1, max_val=MAXBLK)
                sp.wait_ge(S(r + "_xbT_ps"), total + 1)
                load(0)

            load_blocks(L[0])
            load_blocks(L[1])
            for t in range(NT):
                sp.wait_ge(S("r1_x"), t + 1)
                sp.dma_start(out[t * P:(t + 1) * P, :], x[:, t, :]).then_inc(S("stored"), 16)
            sp.wait_ge(S("stored"), 16 * NT)

        @block.gpsimd
        def _(pool):
            ch = Chain(pool, S("pool_step"))
            ch(pool.memset(ident[:, :], 0.0))
            ch(pool.memset(identb[:, :], 1.0))
            ch.settle()
            ch(pool.affine_select(out=ident[:, :], in_=ident[:, :], compare_op=ALU.not_equal, fill=1.0, base=0,
                                  pattern=[[-1, P]], channel_multiplier=1))
            ch(pool.affine_select(out=earlier[:, :], in_=identb[:, :], compare_op=ALU.is_gt, fill=0.0, base=0,
                                  pattern=[[1, P]], channel_multiplier=-1))
            ch.settle()
            ch(pool.tensor_copy(identb[:, :], ident[:, :]))
            ch(pool.tensor_copy(identh[:, :], ident[:, :]))
            ch(pool.memset(onesb[:, :], 1.0))
            ch(pool.iota(iota_i[:, :], pattern=[[1, 8]], base=0, channel_multiplier=0))
            ch.settle()
            ch(pool.tensor_copy(iota8[:, :], iota_i[:, :]))
            ch.settle()
            ch(pool.tensor_scalar(thr[:, :], iota8[:, 1:8], float(BLK), None, ALU.mult))
            pool.memset(penR[:, :, :], PENALTY).then_inc(S("consts"), 1)
            ch(pool.memset(ctxR[:, :, :, :, :], 0.0))
            ch(pool.memset(k_rem[:, :, :, :, :], 0.0))
            ch(pool.memset(v_ext[:, :, :, :], 1.0))
            ch.settle()
            pool.memset(v_rem[:, :, :, :, :], 0.0).then_inc(S("blanks"), 1)
            pool.memset(zeros[:, :], 0.0).then_inc(S("zeros_set"), 1)

            for g in range(NG):
                pool.wait_ge(S("ld_mask"), 48 * (g + 1))
                if g == 0:
                    pool.wait_ge(S("consts"), 1)
                pool.tensor_scalar(pen[:, g * GT:(g + 1) * GT, :], mask_raw[:, :, :], 0.0, PENALTY, ALU.is_equal, ALU.mult).then_inc(S("mask_used"), 1)
                pool.tensor_scalar(penT[:, g, :], maskT_raw[:, :], 0.0, PENALTY, ALU.is_equal, ALU.mult).then_inc(S("mask_used"), 1)
                pool.tensor_scalar(penR[0:KR, g, :], maskR_raw[0:KR, :], 0.0, PENALTY, ALU.is_equal, ALU.mult).then_inc(S("mask_used"), 1)

            def expert(l, e, slot, seen):
                k = len(l.chunks)

                def fetch(n):
                    src, col, _ = l.chunks[n]
                    pool.dma_start(stage[:, n % 2, :], src[bass.ds(e, 1), :, col:col + 1024].rearrange("e p n -> (e p) n")).then_inc(S(f"staged{l.n}_{n}"), 16)

                def split(n):
                    at, st = l.chunks[n][2], stage[:, n % 2, :]
                    wait_counted(pool, S(f"staged{l.n}_{n}"), (seen + 1) * 16)
                    pool.tensor_copy(w_hl[slot][:, 0, at:at + 1024], st).then_inc(S(f"w_hi{l.n}"), 1)
                    wait_counted(pool, S(f"w_hi{l.n}"), seen * k + n + 1)
                    pool.tensor_tensor(w_hl[slot][:, 1, at:at + 1024], st, w_hl[slot][:, 0, at:at + 1024], ALU.subtract).then_inc(S(f"w_ready{l.n}"), 1)

                for n in range(2):
                    fetch(n)
                for n in range(k):
                    split(n)
                    wait_counted(pool, S(f"w_ready{l.n}"), seen * k + n + 1)
                    if n + 2 < k:
                        fetch(n + 2)

            def rest_of_experts(l):
                tb = table[l.n]
                pool.wait_ge(S(l.r + "_table"), 1)
                with pool.Fori(1, E // 2) as pr:
                    for slot in range(2):
                        e = pr * 2 + slot
                        freed = pool.value_load(tb[0:1, bass.ds(e - 1, 1)], min_val=0, max_val=MAXBLK)
                        wait_counted(pool, S(l.r + "_down"), freed + 1)
                        expert(l, e, slot, e)

            def scatter(l, g):
                r = l.r
                pool.wait_ge(S(r + "_xp"), g + 1)
                pool.wait_ge(S(r + "_slot"), g + 1)
                if g == 0:
                    pool.wait_ge(S("rows_zero"), 16 * (E * REGION // (P * 8)))
                for t in range(GT):
                    for k in range(TOP):
                        pool.indirect_dma_start(
                            out=rows, out_offset=bass.IndirectOffsetOnAxis(ap=slot_s[:, g * GT + t, k:k + 1], axis=0),
                            in_=xp[:, t, :], in_offset=None, bounds_check=E * REGION - 1,
                            oob_is_err=False).then_inc(S(r + "_scattered"), 16)

            def results_stored(l):
                r = l.r
                total = pool.value_load(table[l.n][0:1, 8:9], min_val=1, max_val=MAXBLK)
                wait_counted(pool, S(r + "_stored"), total * 16 + 16)
                if l.n == 0:
                    pool.wait_ge(S("results_zero"), 16 * (MAXBLK * BLK // (P * 8)))

            def gather(l, g):
                r = l.r
                for t in range(g * GT, (g + 1) * GT):
                    if t >= 2:
                        pool.wait_ge(S(r + "_x"), t - 1)
                    for k in range(TOP):
                        pool.indirect_dma_start(
                            out=gb[:, t % 2, k, :], out_offset=None, in_=results,
                            in_offset=bass.IndirectOffsetOnAxis(ap=slot_g[:, t, k:k + 1], axis=0),
                            bounds_check=MAXBLK * BLK - 1, oob_is_err=False).then_inc(S(f"{r}_gathered{t % 2}"), 16)

            pool.wait_ge(S("mask_used"), 3 * NG)
            expert(L[0], 0, 0, 0)
            for g in range(NG):
                scatter(L[0], g)
            pool.wait_ge(S("a0_o_ps"), NT)
            expert(L[0], 1, 1, 1)
            pool.wait_ge(S("ld_phi"), 64)
            ch(pool.tensor_tensor(betas[:, 3:4], betas[:, 0:1], betas[:, 1:2], ALU.add))
            ch.settle()
            ch(pool.tensor_tensor(betas[:, 3:4], betas[:, 3:4], betas[:, 2:3], ALU.subtract))
            ch.settle()
            pool.tensor_scalar(phi[:, :, :], phi[:, :, :], betas[:, 3:4], None, ALU.mult).then_inc(S("phi_set"), 1)
            rest_of_experts(L[0])
            wait_counted(pool, S("r0_down"), pool.value_load(table[0][0:1, 7:8], min_val=1, max_val=MAXBLK) + 1)
            expert(L[1], 0, 0, 0)
            results_stored(L[0])
            gather(L[0], 0)
            for g in range(1, NG):
                gather(L[0], g)
                scatter(L[1], g - 1)
            expert(L[1], 1, 1, 1)
            scatter(L[1], NG - 1)
            rest_of_experts(L[1])
            results_stored(L[1])
            for g in range(NG):
                gather(L[1], g)

        @block.tensor
        def _(pe):
            def mm(o, l, r, start, stop, **kw):
                return pe.matmul(o, l, r, start=start, stop=stop, **kw)

            pe.wait_ge(S("ld_kv"), 13 * 16)
            pe.wait_ge(S("ctx_rep"), 1)
            for b in range(B):
                for oc in range(KC):
                    for kc in range(KC):
                        mm(ps[:, 2 * b + oc, 0:SK], w_sb["wk"][:, kc, oc * P:(oc + 1) * P], ctxT[:, b, kc, :], kc == 0, kc == 1)
                for kc in range(KC):
                    mm(ps[:, 4 + b, 0:D], ctxT[:, b, kc, 0:KM], w_sb["wv"][:, kc, :], kc == 0, kc == 1)
                for kc in range(KC):
                    last = mm(ps[:, 6 + b, 0:D], ctxR[:, b, kc, :, :].rearrange("p a j -> p (a j)"), w_sb["wv"][:, kc, :], kc == 0, kc == 1)
            last.then_inc(S("kv_ps"), 1)
            pe.wait_ge(S("kv_done"), 1)
            for b in range(B):
                for oc in range(KC):
                    for kc in range(KC):
                        mm(ps[:, 2 * b + oc, 0:SK], w_sb["Wk"][:, kc, oc * P:(oc + 1) * P], ctxT[:, b, kc, :], kc == 0, kc == 1)
                for kc in range(KC):
                    mm(ps[:, 4 + b, 0:D], ctxT[:, b, kc, 0:KM], w_sb["Wv"][:, kc, :], kc == 0, kc == 1)
                for kc in range(KC):
                    last = mm(ps[0:KR, 6 + b, 0:D], ctxT[:, b, kc, KM:SK], w_sb["Wv"][:, kc, :], kc == 0, kc == 1)
            last.then_inc(S("kv_ps"), 1)
            pe.wait_ge(S("kv_done"), 2)
            pe.wait_ge(S("ld_w"), 5 * 16)

            def turn(c, g, src):
                pe.wait_ge(S(c + "_ln"), g + 1)
                for kc in range(KC):
                    for t in range(GT):
                        last = pe.transpose(ps[:, kc, t * P:(t + 1) * P], src[:, t, kc * P:(kc + 1) * P], ident[:, :])
                last.then_inc(S(c + "_xT_ps"), 1)

            def project_q(c, g, w):
                pe.wait_ge(S(c + "_xT"), g + 1)
                for oc in range(KC):
                    for kc in range(KC):
                        last = mm(ps[:, 2 + oc, :], w[:, kc, oc * P:(oc + 1) * P], xT[:, kc, :], kc == 0, kc == 1)
                last.then_inc(S(c + "_q_ps"), 1)

            def score_max(g):
                b = g // 2
                pe.wait_ge(S("a0_qlo"), 2 * (g + 1))
                pe.wait_ge(S("mask_used"), 3 * (g + 1))
                for n in range(12):
                    t, h0 = n // 3, (n % 3) * 6
                    if n >= 2:
                        pe.wait_ge(S("a0_mx"), 12 * g + n - 1)
                    for j in range(2):
                        heads = range(h0 + 3 * j, min(h0 + 3 * j + 3, H))
                        o = ps[:, 2 * (n % 2) + j, 0:len(heads) * SK].rearrange("p (h s) -> p h s", s=SK)
                        mm(o, identb[:, :], pen[:, g * GT + t, :].unsqueeze(1).broadcast_to([P, len(heads), SK]), True, False)
                        for oc in range(KC):
                            part = [h for h in heads if h // 8 == oc]
                            if part:
                                last = mm(o[:, part[0] - heads[0]:part[-1] - heads[0] + 1, :], q_hi[:, oc, t * P:(t + 1) * P],
                                          k_blk[:, b, 0, part[0]:part[-1] + 1, :], False, part[-1] == heads[-1])
                    last.then_inc(S("a0_s_ps"), 1)

            def turn_max(g):
                pe.wait_ge(S("a0_nm"), g + 1)
                for t in range(GT):
                    last = pe.transpose(psb[0:32, 0, t * P:(t + 1) * P], nm[:, t, :], identb[:, :])
                last.then_inc(S("a0_mT_ps"), 1)

            def scores(g):
                b = g // 2
                pe.wait_ge(S("a0_mT"), g + 1)
                if g:
                    pe.wait_ge(S("a0_oev"), 4 * g)
                for u in range(20):
                    if u >= 2:
                        pe.wait_ge(S("a0_exp"), 20 * g + u - 1)
                    o = ps[:, 4 + u % 2, :]
                    if u < H:
                        kh, kl = (k_blk[:, b, i, u, 0:KM] for i in range(2))
                        oc, who, lp, rp = u // 8, msel[:, u, :], identb[:, :], penT[:, g, :]
                    else:
                        r = u - H
                        kh, kl = (k_rem[:, b, i, 4 * r:4 * r + 4, :].rearrange("p h j -> p (h j)") for i in range(2))
                        oc, who = r // 2, mselr[:, 4 * r:4 * r + 4, :].rearrange("p h j -> p (h j)")
                        lp, rp = esel[:, :, :].rearrange("p a j -> p (a j)"), penR[:, g, :]
                    mm(o, kh, q_hi[:, oc, :], True, False)
                    mm(o, kl, q_hi[:, oc, :], False, False)
                    mm(o, kh, q_lo[:, oc, :], False, False)
                    mm(o, lp, rp, False, False)
                    mm(o, who, nmT[:, :], False, True).then_inc(S("a0_st"), 1)

            def weigh_values(g, t):
                b, at = g // 2, 6 - 2 * (t % 2)
                pe.wait_ge(S("a0_plo"), 20 * (g + 1))
                if t >= 2:
                    pe.wait_ge(S("a0_oev"), 4 * g + t - 1)
                elif t == 0 and g:
                    pe.wait_ge(S("a0_oev"), 4 * g - 1)
                tk = slice(t * P, (t + 1) * P)
                for j in range(2):
                    o = ps[:, at + j, 0:8 * VW].rearrange("p (h v) -> p h v", v=VW)
                    for h in range(8):
                        mm(o[:, h, :], p_hi[:, 8 * j + h, tk], v_ext[:, b, 8 * j + h, :], h == 0, False, skip_group_check=True)
                        mm(o[:, h, 0:DK + 1], p_lo[:, 8 * j + h, tk], v_ext[:, b, 8 * j + h, 0:DK + 1], False, False, skip_group_check=True)
                    for r in range(2):
                        q = 2 * j + r
                        mm(o[:, 4 * r:4 * r + 4, :], p_hi[:, H + q, tk], v_rem[:, b, q, :, :], False, False, skip_group_check=True)
                        last = mm(o[:, 4 * r:4 * r + 4, 0:DK + 1], p_lo[:, H + q, tk], v_rem[:, b, q, :, 0:DK + 1], False, r == 1, skip_group_check=True)
                last.then_inc(S("a0_o_ps"), 1)

            def turn_out(g, t):
                n = 4 * g + t
                pe.wait_ge(S("a0_on"), n + 1)
                if t == 0:
                    pe.wait_ge(S("a0_mx"), 12 * min(g + 2, NG))
                if n >= 2:
                    pe.wait_ge(S("a0_oT"), n - 1)
                for kc in range(KC):
                    last = pe.transpose(ps[:, t % 2, kc * P:(kc + 1) * P], o_n[:, t % 2, kc * P:(kc + 1) * P], ident[:, :])
                last.then_inc(S("a0_oT_ps"), 1)

            def project_out(g, t):
                n = 4 * g + t
                pe.wait_ge(S("a0_oT"), n + 1)
                if n >= 2:
                    pe.wait_ge(S("a0_x"), n - 1)
                for kc in range(KC):
                    last = mm(ps[:, 2 + t % 2, 0:D], oT[:, t % 2, kc * P:(kc + 1) * P], w_sb["wo"][:, kc, :], kc == 0, kc == 1)
                last.then_inc(S("a0_op_ps"), 1)

            def route_logits(l, g):
                turn(l.r, g, xlr)
                pe.wait_ge(S(l.r + "_xT"), g + 1)
                for t in range(GT):
                    for kc in range(KC):
                        last = mm(ps[:, 2, t * E:(t + 1) * E], xTr[:, kc, t * P:(t + 1) * P], gate[l.n][:, kc, :], kc == 0, kc == 1)
                last.then_inc(S(l.r + "_lg_ps"), 1)

            def route_positions(l, g):
                pe.wait_ge(S(l.r + "_sel"), g + 1)
                o = ps[:, 3, 0:GT * E]
                mm(o, earlier[:, :], selb[:, :, :].rearrange("p t e -> p (t e)"), True, False)
                mm(o, onesb[:, :], cumb[:, 0:GT, :].rearrange("p t e -> p (t e)"), False, True).then_inc(S(l.r + "_pos_ps"), 1)

            def route_counts(l):
                pe.wait_ge(S(l.r + "_slot"), NG)
                mm(ps[:, 3, 0:E], onesb[:, :], cumb[:, GT, :], True, True).then_inc(S(l.r + "_cnt_ps"), 1)

            turn("a0", 0, xln)
            project_q("a0", 0, w_sb["wq"])
            score_max(0)
            for g in range(NG):
                turn_max(g)
                scores(g)
                if g:
                    route_logits(L[0], g - 1)
                if g + 1 < NG:
                    turn("a0", g + 1, xln)
                    if g:
                        pe.wait_ge(S("r0_lg"), g)
                    project_q("a0", g + 1, w_sb["wq"])
                    score_max(g + 1)
                if g:
                    pe.wait_ge(S("a0_mx"), 12 * min(g + 2, NG))
                    route_positions(L[0], g - 1)
                    pe.wait_ge(S("r0_slot"), g)
                for t in range(GT + 2):
                    if t < GT:
                        weigh_values(g, t)
                    if 1 <= t <= GT:
                        turn_out(g, t - 1)
                    if t >= 2:
                        project_out(g, t - 2)
            pe.wait_ge(S("a0_x"), NT)
            route_logits(L[0], NG - 1)
            route_positions(L[0], NG - 1)
            route_counts(L[0])

            def experts(l):
                r, tb, pairs = l.r, table[l.n], l.pairs

                def turn_block(g):
                    pe.wait_ge(S(r + "_xraw"), g * 16 + 16)
                    for hf in range(2):
                        for part in range(4):
                            last = pe.transpose(psh[:, 6, part * BLK + hf * P:part * BLK + (hf + 1) * P],
                                                x_raw[:, hf, part * P:(part + 1) * P], identh[:, :])
                    last.then_inc(S(r + "_xbT_ps"), 1)

                pe.sem_inc(S(r + "_xbT_ps"), 1)
                pe.sem_inc(S(r + "_down"), 1)
                pe.wait_ge(S(r + "_table"), 1)
                turn_block(0)
                with pe.Fori(0, E // 2) as pr:
                    for slot in range(2):
                        first = pe.value_load(tb[0:1, bass.ds(pr * 2 + slot, 1)], min_val=0, max_val=MAXBLK - 1)
                        end = pe.value_load(tb[0:1, bass.ds(pr * 2 + slot + 1, 1)], min_val=1, max_val=MAXBLK)
                        wait_counted(pe, S(f"w_ready{l.n}"), (pr * 2 + slot + 1) * len(l.chunks))
                        wh, wl = w_hl[slot][:, 0, :], w_hl[slot][:, 1, :]
                        with pe.Fori(first, end) as g:
                            pe.wait_ge(S(r + "_xbT"), g + 1)
                            for j in range(pairs):
                                pe.wait_ge(S(r + "_h32"), g * pairs + j + 1)
                                for which, col in enumerate((l.gate_col, l.up_col)):
                                    for i in range(2):
                                        o = ps[:, 2 * (j % 2) + which, i * BLK:(i + 1) * BLK]
                                        for kc in range(KC):
                                            at = col(kc, 2 * j + i)
                                            mm(o, wh[:, at:at + P], xbT[:, 0, kc, :], kc == 0, False)
                                            mm(o, wh[:, at:at + P], xbT[:, 1, kc, :], False, False)
                                            last = mm(o, wl[:, at:at + P], xbT[:, 0, kc, :], False, kc == 1)
                                    last.then_inc(S(r + "_gu_ps"), 1)
                            turn_block(g + 1)
                            pe.wait_ge(S(r + "_y"), g + 1)
                            for c in range(l.hc):
                                if c % 2 == 0:
                                    pe.wait_ge(S(r + "_h"), g * pairs + c // 2 + 2)
                                at = l.down_at + c * D
                                for hf in range(2):
                                    o, tk = ps[:, 4 + hf, 0:D], slice(hf * P, (hf + 1) * P)
                                    mm(o, h_hi[:, c, tk], wh[:, at:at + D], c == 0, False)
                                    mm(o, h_hi[:, c, tk], wl[:, at:at + D], False, False)
                                    last = mm(o, h_lo[:, c, tk], wh[:, at:at + D], False, c == l.hc - 1)
                            last.then_inc(S(r + "_down"), 1)

            experts(L[0])

            for g in range(NG):
                b = g // 2
                turn("a1", g, xln)
                project_q("a1", g, w_sb["Wq"])
                if g:
                    pe.wait_ge(S("a1_q"), g + 1)
                    route_logits(L[1], g - 1)
                pe.wait_ge(S("a1_q"), g + 1)
                for t in range(GT):
                    for kc in range(KC):
                        last = mm(ps[:, 4 + t // 2, (t % 2) * SK:(t % 2 + 1) * SK], q1T[:, kc, t * P:(t + 1) * P], k1T[:, b, kc, :], kc == 0, kc == 1)
                last.then_inc(S("a1_s_ps"), 1)
                if g:
                    route_positions(L[1], g - 1)
                pe.wait_ge(S("a1_p"), GT * (g + 1))
                for t in range(GT):
                    pe.transpose(ps[:, 6, t * P:(t + 1) * P], att[:, t, 0:KM], ident[:, :])
                for t in range(GT):
                    last = pe.transpose(ps[0:KR, 7, t * P:(t + 1) * P], att[:, t, KM:SK], ident[:, :])
                last.then_inc(S("a1_pT_ps"), 1)
                pe.wait_ge(S("a1_pT"), 2 * (g + 1))
                if g:
                    pe.wait_ge(S("r1_xT"), g)
                for t in range(GT):
                    o = ps[:, t // 2, (t % 2) * D:(t % 2 + 1) * D]
                    mm(o, pT[:, t * P:(t + 1) * P], v1m[:, b, :], True, False)
                    last = mm(o, pTr[0:KR, t * P:(t + 1) * P], v1r[0:KR, b, :], False, True)
                last.then_inc(S("a1_o_ps"), 1)
                pe.wait_ge(S("a1_x"), GT * (g + 1))
            route_logits(L[1], NG - 1)
            route_positions(L[1], NG - 1)
            route_counts(L[1])
            experts(L[1])

        @block.scalar
        def _(act):
            def x_evac(c, g, dst):
                act.wait_ge(S(c + "_xT_ps"), g + 1)
                act.copy(dst[:, :, :], ps[:, 0:2, :]).then_inc(S(c + "_xT"), 1)

            def q_parts(g):
                act.wait_ge(S("a0_q_ps"), g + 1)
                for oc in range(KC):
                    act.activation(q_hi[:, oc, :], ps[:, 2 + oc, :], ACT.Identity, bias=bcol["bq"][:, oc:oc + 1]).then_inc(S("a0_qhi"), 1)

            def gates(l, g):
                act.wait_ge(S(l.r + "_d"), g + 1)
                act.activation(ev[:, :], dv[:, :], ACT.Exp).then_inc(S(l.r + "_e"), 1)

            act.wait_ge(S("ld_kv"), 13 * 16)
            x_evac("a0", 0, xT)
            q_parts(0)
            for g in range(NG):
                act.wait_ge(S("a0_mT_ps"), g + 1)
                act.copy(nmT[:, :], psb[0:32, 0, 0:GW]).then_inc(S("a0_mT"), 1)
                for u in range(21):
                    if u < 20:
                        act.wait_ge(S("a0_st"), 20 * g + u + 1)
                        if 20 * g + u >= 4:
                            act.wait_ge(S("a0_plo"), 20 * g + u - 3)
                        act.activation(e_ring[:, u % 4, :], ps[:, 4 + u % 2, :], ACT.Exp, scale=float(DK) ** -0.5).then_inc(S("a0_exp"), 1)
                    if u:
                        act.wait_ge(S("a0_exp"), 20 * g + u)
                        act.copy(p_hi[:, u - 1, :], e_ring[:, (u - 1) % 4, :]).then_inc(S("a0_phi"), 1)
                if g:
                    x_evac("r0", g - 1, xTr)
                if g + 1 < NG:
                    x_evac("a0", g + 1, xT)
                    q_parts(g + 1)
                if g:
                    gates(L[0], g - 1)
                for t in range(GT + 1):
                    if t < GT:
                        n = 4 * g + t
                        act.wait_ge(S("a0_o_ps"), n + 1)
                        if n:
                            act.wait_ge(S("a0_oev"), n)
                        at = 6 - 2 * (t % 2)
                        act.copy(o_lo[:, :, :, :], ps[:, at:at + 2, 0:8 * VW].rearrange("p b (h v) -> p b h v", v=VW)[:, :, :, DK + 1:VW]).then_inc(S("a0_olo"), 1)
                    if t:
                        n = 4 * g + t - 1
                        act.wait_ge(S("a0_oT_ps"), n + 1)
                        if n >= 2:
                            act.wait_ge(S("a0_op_ps"), n - 1)
                        act.copy(oT[:, (t - 1) % 2, :], ps[:, (t - 1) % 2, 0:D]).then_inc(S("a0_oT"), 1)
            x_evac("r0", NG - 1, xTr)
            gates(L[0], NG - 1)

            def experts(l):
                r, pairs = l.r, l.pairs
                act.sem_inc(S(r + "_y"), 1)
                act.sem_inc(S(r + "_stored"), 16)
                act.wait_ge(S(r + "_table"), 1)
                total = act.value_load(table[l.n][0:1, 8:9], min_val=1, max_val=MAXBLK)
                with act.Fori(0, total) as g:
                    for j in range(pairs):
                        act.wait_ge(S(r + "_h32"), g * pairs + j + 1)
                        act.wait_ge(S(r + "_gu_ps"), (g * pairs + j) * 2 + 1)
                        act.activation(s_act[:, j % 2, :], ps[:, 2 * (j % 2), :], l.act).then_inc(S(r + "_s"), 1)
                    act.wait_ge(S(r + "_down"), g + 2)
                    act.wait_ge(S(r + "_stored"), g * 16 + 16)
                    act.copy(yb[:, :, :], ps[:, 4:6, 0:D]).then_inc(S(r + "_y"), 1)
                    act.wait_ge(S(r + "_y"), g + 2)
                    act.dma_start(results[bass.ds(g * BLK, BLK), :].rearrange("(h p) d -> p h d", p=P), yb[:, :, :]).then_inc(S(r + "_stored"), 16)

            act.wait_ge(S("results_zero"), 16 * (MAXBLK * BLK // (P * 8)))
            experts(L[0])
            for g in range(NG):
                x_evac("a1", g, xT)
                act.wait_ge(S("a1_q_ps"), g + 1)
                for oc in range(KC):
                    last = act.activation(q1T[:, oc, :], ps[:, 2 + oc, :], ACT.Identity, bias=bcol["Bq"][:, oc:oc + 1])
                last.then_inc(S("a1_q"), 1)
                if g:
                    x_evac("r1", g - 1, xTr)
                act.wait_ge(S("a1_nm"), g + 1)
                for t in range(GT):
                    act.activation(att[:, t, :], att[:, t, :], ACT.Exp, bias=mx1[:, t:t + 1], accum_out=den1[:, t:t + 1]).then_inc(S("a1_p"), 1)
                if g:
                    gates(L[1], g - 1)
                act.wait_ge(S("a1_pT_ps"), g + 1)
                act.copy(pT[:, :], ps[:, 6, :]).then_inc(S("a1_pT"), 1)
                act.copy(pTr[0:KR, :], ps[0:KR, 7, :]).then_inc(S("a1_pT"), 1)
            x_evac("r1", NG - 1, xTr)
            gates(L[1], NG - 1)
            experts(L[1])
            total = act.value_load(table[1][0:1, 8:9], min_val=1, max_val=MAXBLK)
            wait_counted(act, S("r1_stored"), total * 16 + 16)

        @block.vector
        def _(dve):
            ch = Chain(dve, S("dve_step"))

            def layernorm(c, g, dst):
                for t in range(GT):
                    ch(dve.bn_stats(stats[:, t, :], x[:, g * GT + t, :]))
                ch.settle()
                for t in range(GT):
                    ch(dve.bn_aggr(mv[:, t, :], stats[:, t, :]))
                ch.settle()
                ch(dve.tensor_scalar(ve[:, :], mv[:, :, 1], EPS, None, ALU.add))
                ch.settle()
                ch(dve.tensor_scalar(ry[:, :].bitcast(I32), ve[:, :].bitcast(I32), -0.5, 1597463007.0, ALU.mult, ALU.add))
                ch.settle()
                for _ in range(4):
                    ch(dve.tensor_tensor(rt[:, :], ry[:, :], ry[:, :], ALU.mult))
                    ch.settle()
                    ch(dve.scalar_tensor_tensor(rt[:, :], rt[:, :], -0.5, ve[:, :], ALU.mult, ALU.mult))
                    ch.settle()
                    ch(dve.scalar_tensor_tensor(ry[:, :], rt[:, :], 1.5, ry[:, :], ALU.add, ALU.mult))
                    ch.settle()
                for t in range(GT):
                    ins = dve.tensor_scalar(dst[:, t, :], x[:, g * GT + t, :], mv[:, t, 0:1], ry[:, t:t + 1], ALU.subtract, ALU.mult)
                    if t < GT - 1:
                        ch(ins)
                ins.then_inc(S(c + "_ln"), 1)

            dve.wait_ge(S("consts"), 1)
            ch(dve.tensor_tensor(le[:, :, :], iota8[:, :].unsqueeze(1).broadcast_to([P, 8, 8]),
                                 iota8[:, :].unsqueeze(2).broadcast_to([P, 8, 8]), ALU.is_le))
            ch(dve.tensor_reduce(head_of[:, :], ident[:, :].rearrange("p (h d) -> p h d", d=DK), AX, ALU.max))
            ch(dve.tensor_reduce(quad_of[:, :], ident[:, :].rearrange("p (a j) -> p a j", j=QW)[:, :, 0:KR], AX, ALU.max))
            ch(dve.tensor_tensor(m16[:, :], ident[0:32, 0:H], ident[0:32, H:2 * H], ALU.add))
            ch(dve.tensor_copy(esel[:, :, :], ident[0:32, 0:QW].unsqueeze(1).broadcast_to([32, 4, QW])))
            ch.settle()
            ch(dve.tensor_copy(msel[:, :, :], m16[:, :].unsqueeze(2).broadcast_to([32, H, P])))
            ch(dve.tensor_copy(mselr[:, :, :], m16[:, :].unsqueeze(2).broadcast_to([32, H, QW])))
            dve.wait_ge(S("blanks"), 1)
            dve.wait_ge(S("ld_kv"), 13 * 16)
            for b in range(B):
                for kc in range(KC):
                    ins = dve.tensor_copy(ctxR[:, b, kc, :, 0:KR], ctxT[:, b, kc, KM:SK].unsqueeze(1).broadcast_to([P, 4, KR]))
                    if (b, kc) != (B - 1, KC - 1):
                        ch(ins)
            ins.then_inc(S("ctx_rep"), 1)
            dve.wait_ge(S("ld_x0"), 16)
            layernorm("a0", 0, xln)
            dve.wait_ge(S("kv_ps"), 1)
            for b in range(B):
                for oc in range(KC):
                    kp, bk = ps[:, 2 * b + oc, 0:SK], bcol["bk"][:, oc:oc + 1]
                    ch(dve.tensor_scalar(k_tmp[:, 0, :], kp, bk, None, ALU.add))
                    ch.settle()
                    ch(dve.scalar_tensor_tensor(k_tmp[:, 1, :], kp, bk, k_tmp[:, 0, :], ALU.add, ALU.subtract))
                    ch.settle()
                    hs = slice(8 * oc, 8 * oc + 8)
                    for i in range(2):
                        ch(dve.tensor_tensor(k_blk[:, b, i, hs, :], k_tmp[:, i, :].unsqueeze(1).broadcast_to([P, 8, SK]),
                                             head_of[:, :].unsqueeze(2).broadcast_to([P, 8, SK]), ALU.mult))
                    ch.settle()
                    for i in range(2):
                        ch(dve.tensor_copy(k_rem[:, b, i, hs, 0:KR], k_blk[:, b, i, hs, KM:SK]))
                for rem in range(2):
                    vh = v_hl[:, :, :].rearrange("p i (h d) -> p i h d", d=DK)
                    ch(dve.tensor_tensor(v_tmp[:, :], ps[:, 4 + 2 * rem + b, 0:D], brow["bv"][:, :], ALU.add))
                    ch.settle()
                    ch(dve.tensor_copy(v_hl[:, 0, :], v_tmp[:, :]))
                    ch.settle()
                    ch(dve.tensor_tensor(v_hl[:, 1, :], v_tmp[:, :], v_hl[:, 0, :], ALU.subtract))
                    ch.settle()
                    for i, at in ((0, 0), (1, DK + 1)):
                        if not rem:
                            ch(dve.tensor_copy(v_ext[:, b, :, at:at + DK], vh[:, i, :, :]))
                            continue
                        for q in range(4):
                            ch(dve.tensor_tensor(v_rem[:, b, q, :, at:at + DK], vh[:, i, 4 * q:4 * q + 4, :],
                                                 quad_of[:, :].unsqueeze(2).broadcast_to([P, 4, DK]), ALU.mult))
                            if i == 0:
                                ch(dve.tensor_copy(v_rem[:, b, q, :, DK:DK + 1], quad_of[:, :].unsqueeze(2)))
                    ch.settle()
            dve.engine_nop().then_inc(S("kv_done"), 1)
            dve.wait_ge(S("kv_ps"), 2)
            for b in range(B):
                for oc in range(KC):
                    ch(dve.tensor_scalar(k1T[:, b, oc, :], ps[:, 2 * b + oc, 0:SK], bcol["Bk"][:, oc:oc + 1], None, ALU.add))
                ch(dve.tensor_tensor(v1m[:, b, :], ps[:, 4 + b, 0:D], brow["Bv"][:, :], ALU.add))
                ins = dve.tensor_tensor(v1r[0:KR, b, :], ps[0:KR, 6 + b, 0:D], brow["Bv"][0:KR, :], ALU.add)
                if b < B - 1:
                    ch(ins)
            ins.then_inc(S("kv_done"), 1)

            def q_low(g):
                for oc in range(KC):
                    dve.wait_ge(S("a0_qhi"), 2 * g + oc + 1)
                    dve.scalar_tensor_tensor(q_lo[:, oc, :], ps[:, 2 + oc, :], bcol["bq"][:, oc:oc + 1], q_hi[:, oc, :],
                                             ALU.add, ALU.subtract).then_inc(S("a0_qlo"), 1)

            def maxima(g):
                for n in range(12):
                    t, h0, at = n // 3, (n % 3) * 6, 2 * (n % 2)
                    dve.wait_ge(S("a0_s_ps"), 12 * g + n + 1)
                    if n % 3 < 2:
                        v = ps[:, at:at + 2, 0:3 * SK].rearrange("p b (h s) -> p b h s", s=SK)
                        dve.tensor_reduce(mx[:, t, h0:h0 + 6].rearrange("p (b h) -> p b h", b=2), v, AX, ALU.max).then_inc(S("a0_mx"), 1)
                    else:
                        ch(dve.tensor_reduce(mx[:, t, h0:h0 + 3], ps[:, at, 0:3 * SK].rearrange("p (h s) -> p h s", s=SK), AX, ALU.max))
                        dve.tensor_reduce(mx[:, t, h0 + 3:h0 + 4], ps[:, at + 1, 0:SK].unsqueeze(1), AX, ALU.max).then_inc(S("a0_mx"), 1)
                dve.wait_ge(S("a0_mx"), 12 * (g + 1))
                ch(dve.tensor_scalar(nm[:, :, 0:H], mx[:, :, :], -1.0, None, ALU.mult))
                ch.settle()
                dve.scalar_tensor_tensor(nm[:, :, H:2 * H], mx[:, :, :], -1.0, nm[:, :, 0:H], ALU.mult, ALU.subtract).then_inc(S("a0_nm"), 1)

            def rows_to_send(l, g):
                if g:
                    dve.wait_ge(S(l.r + "_scattered"), 16 * GT * TOP * g)
                dve.wait_ge(S(l.r + "_ln"), g + 1)
                o = xp[:, :, :]
                ch(dve.tensor_copy(o[:, :, 0:D], xlr[:, :, :]))
                ch.settle()
                dve.tensor_tensor(o[:, :, D:2 * D], xlr[:, :, :], o[:, :, 0:D], ALU.subtract).then_inc(S(l.r + "_xp"), 1)

            def choose(l, g):
                r = l.r
                tg = slice(g * GT, (g + 1) * GT)
                dve.wait_ge(S(r + "_lg_ps"), g + 1)
                dve.tensor_copy(lg[:, :, :].rearrange("p t e -> p (t e)"), ps[:, 2, 0:GT * E]).then_inc(S(r + "_lg"), 1)
                dve.wait_ge(S(r + "_lg"), g + 1)
                for t in range(GT):
                    ch(dve.max(mx8[:, t, :], lg[:, t, :]))
                ch.settle()
                for t in range(GT):
                    ch(dve.max_index(ix8[:, t, :], mx8[:, t, :], lg[:, t, :]))
                dve.tensor_tensor(dv[:, :], mx8[:, :, 1], mx8[:, :, 0], ALU.subtract).then_inc(S(r + "_d"), 1)
                ch.settle()
                ch(dve.tensor_copy(idxf[:, tg, :], ix8[:, :, 0:TOP]))
                ch.settle()
                for t in range(g * GT, (g + 1) * GT):
                    ch(dve.tensor_tensor(oh[:, t, :, :], iota8[:, :].unsqueeze(1).broadcast_to([P, TOP, E]),
                                         idxf[:, t, :].unsqueeze(2).broadcast_to([P, TOP, E]), ALU.is_equal))
                ch.settle()
                ch(dve.tensor_tensor(sel[:, :, :], oh[:, tg, 0, :], oh[:, tg, 1, :], ALU.add))
                if g == 0:
                    ch(dve.memset(cum[:, 0, :], 0.0))
                else:
                    ch(dve.tensor_copy(cum[:, 0, :], cum[:, GT, :]))
                ch.settle()
                ch(dve.tensor_copy(selb[:, :, :], sel[:, :, :]))
                for t in range(GT):
                    ch(dve.tensor_tensor(cum[:, t + 1, :], cum[:, t, :], sel[:, t, :], ALU.add))
                    ch.settle()
                dve.tensor_copy(cumb[:, :, :], cum[:, :, :]).then_inc(S(r + "_sel"), 1)

            def place(l, g):
                r = l.r
                tg = slice(g * GT, (g + 1) * GT)
                dve.wait_ge(S(r + "_pos_ps"), g + 1)
                pos = ps[:, 3, 0:GT * E].rearrange("p (t e) -> p t e", e=E)
                for k in range(TOP):
                    ch(dve.tensor_tensor(ohp[:, tg, k, :], oh[:, tg, k, :], pos, ALU.mult))
                ch.settle()
                ch(dve.tensor_reduce(posk[:, :, :], ohp[:, tg, :, :], AX, ALU.add))
                dve.wait_ge(S(r + "_e"), g + 1)
                ch(dve.tensor_scalar(dn[:, :], ev[:, :], 1.0, None, ALU.add))
                ch.settle()
                ch(dve.reciprocal(weight[:, tg, 0], dn[:, :]))
                ch(dve.tensor_scalar(drop[:, :, :], posk[:, :, :], float(l.cap), None, ALU.is_ge))
                ch(dve.tensor_scalar(pos_kept[:, tg, :], posk[:, :, :], float(l.cap - 1), None, ALU.min))
                ch(dve.scalar_tensor_tensor(slotf[:, tg, :], idxf[:, tg, :], float(REGION), posk[:, :, :], ALU.mult, ALU.add))
                ch.settle()
                ch(dve.tensor_tensor(weight[:, tg, 1], weight[:, tg, 0], ev[:, :], ALU.mult))
                ch.settle()
                ch(dve.tensor_scalar(posk[:, :, :], drop[:, :, :], -1.0, 1.0, ALU.mult, ALU.add))
                ch.settle()
                ch(dve.tensor_tensor(weight[:, tg, :], weight[:, tg, :], posk[:, :, :], ALU.mult))
                dve.scalar_tensor_tensor(slot_s[:, tg, :], drop[:, :, :], float(FAR), slotf[:, tg, :], ALU.mult, ALU.add).then_inc(S(r + "_slot"), 1)

            def count(l):
                r, tb = l.r, table[l.n]
                ch(dve.memset(tb[:, :], 0))
                dve.wait_ge(S(r + "_cnt_ps"), 1)
                ch(dve.tensor_scalar(cnt[:, :], ps[:, 3, 0:E], float(l.cap), None, ALU.min))
                ch.settle()
                ch(dve.tensor_tensor(over[:, :, :], cnt[:, :].unsqueeze(2).broadcast_to([P, E, 7]),
                                     thr[:, :].unsqueeze(1).broadcast_to([P, E, 7]), ALU.is_gt))
                ch.settle()
                ch(dve.tensor_reduce(nblk[:, :], over[:, :, :], AX, ALU.add))
                ch.settle()
                ch(dve.tensor_scalar(nblk[:, :], nblk[:, :], 1.0, None, ALU.add))
                ch.settle()
                ch(dve.tensor_tensor(lem[:, :, :], le[:, :, :], nblk[:, :].unsqueeze(1).broadcast_to([P, E, E]), ALU.mult))
                ch.settle()
                ch(dve.tensor_reduce(blk_end[:, :], lem[:, :, :], AX, ALU.add))
                ch.settle()
                dve.tensor_copy(tb[0:1, 1:9], blk_end[0:1, :]).then_inc(S(r + "_table"), 1)
                ch(dve.tensor_tensor(blk_row[:, :], blk_end[:, :], nblk[:, :], ALU.subtract))
                ch.settle()
                for k in range(TOP):
                    ch(dve.tensor_tensor(ohp[:, :, k, :], oh[:, :, k, :], blk_row[:, :].unsqueeze(1).broadcast_to([P, NT, E]), ALU.mult))
                ch.settle()
                ch(dve.tensor_reduce(slotf[:, :, :], ohp[:, :, :, :], AX, ALU.add))
                ch.settle()
                dve.scalar_tensor_tensor(slot_g[:, :, :], slotf[:, :, :], float(BLK), pos_kept[:, :, :], ALU.mult, ALU.add).then_inc(S(r + "_slotg"), 1)

            q_low(0)
            maxima(0)
            for g in range(NG):
                if g + 1 < NG:
                    dve.wait_ge(S(f"ld_x{g + 1}"), 16)
                    layernorm("a0", g + 1, xln)
                for u in range(20):
                    dve.wait_ge(S("a0_phi"), 20 * g + u + 1)
                    dve.tensor_tensor(p_lo[:, u, :], e_ring[:, u % 4, :], p_hi[:, u, :], ALU.subtract).then_inc(S("a0_plo"), 1)
                if g:
                    choose(L[0], g - 1)
                if g + 1 < NG:
                    q_low(g + 1)
                    maxima(g + 1)
                if g:
                    place(L[0], g - 1)
                for t in range(GT + 2):
                    if t < GT:
                        n = 4 * g + t
                        at = 6 - 2 * (t % 2)
                        o = ps[:, at:at + 2, 0:8 * VW].rearrange("p b (h v) -> p b h v", v=VW)
                        dve.wait_ge(S("a0_olo"), n + 1)
                        if n:
                            dve.wait_ge(S("a0_on"), n)
                        ch(dve.tensor_tensor(o_sum[:, :, :, :], o[:, :, :, 0:DK], o_lo[:, :, :, :], ALU.add))
                        dve.reciprocal(rden[:, :, :], o[:, :, :, DK]).then_inc(S("a0_oev"), 1)
                        dve.wait_ge(S("a0_oev"), n + 1)
                        if n >= 2:
                            dve.wait_ge(S("a0_oT_ps"), n - 1)
                        on = o_n[:, t % 2, :].rearrange("p (h d) -> p h d", d=DK)
                        dve.tensor_tensor(on, o_sum[:, :, :, :].rearrange("p b h d -> p (b h) d"),
                                          rden[:, :, :].rearrange("p b h -> p (b h)").unsqueeze(2).broadcast_to([P, H, DK]), ALU.mult).then_inc(S("a0_on"), 1)
                    if t >= 2:
                        n = 4 * g + t - 2
                        dve.wait_ge(S("a0_op_ps"), n + 1)
                        if n:
                            dve.wait_ge(S("a0_x"), n)
                        ch(dve.tensor_tensor(xo[:, :], ps[:, 2 + t % 2, 0:D], brow["bo"][:, :], ALU.add))
                        ch.settle()
                        dve.tensor_tensor(x[:, n, :], x[:, n, :], xo[:, :], ALU.add).then_inc(S("a0_x"), 1)
                dve.wait_ge(S("a0_x"), 4 * (g + 1))
                if g:
                    dve.wait_ge(S("r0_xT_ps"), g)
                layernorm("r0", g, xlr)
                rows_to_send(L[0], g)
            choose(L[0], NG - 1)
            place(L[0], NG - 1)
            count(L[0])

            def experts(l):
                r, pairs = l.r, l.pairs
                dve.wait_ge(S(r + "_table"), 1)
                total = dve.value_load(table[l.n][0:1, 8:9], min_val=1, max_val=MAXBLK)
                dve.sem_inc(S(r + "_h"), 1)
                dve.sem_inc(S(r + "_h32"), 2)

                def turned(g):
                    dve.wait_ge(S(r + "_xbT_ps"), g + 2)
                    dve.tensor_copy(xbT[:, :, :, :].rearrange("p a b c -> p (a b c)"), psh[:, 6, :]).then_inc(S(r + "_xbT"), 1)

                turned(0)
                with dve.Fori(0, total) as g:
                    dve.wait_ge(S(r + "_down"), g + 1)
                    for j in range(pairs):
                        n = g * pairs + j
                        hh = h_hi[:, 2 * j:2 * j + 2, :].rearrange("p c t -> p (c t)")
                        hl = h_lo[:, 2 * j:2 * j + 2, :].rearrange("p c t -> p (c t)")
                        dve.wait_ge(S(r + "_s"), n + 1)
                        dve.wait_ge(S(r + "_gu_ps"), n * 2 + 2)
                        dve.wait_ge(S(r + "_h"), n + 1)
                        dve.tensor_tensor(h32[:, j % 2, :], s_act[:, j % 2, :], ps[:, 2 * (j % 2) + 1, :], ALU.mult).then_inc(S(r + "_h32"), 1)
                        dve.wait_ge(S(r + "_h32"), n + 3)
                        dve.tensor_copy(hh, h32[:, j % 2, :]).then_inc(S(r + "_hh"), 1)
                        dve.wait_ge(S(r + "_hh"), n + 1)
                        dve.tensor_tensor(hl, h32[:, j % 2, :], hh, ALU.subtract).then_inc(S(r + "_h"), 1)
                    turned(g + 1)

            def combine(l, t):
                r = l.r
                dve.wait_ge(S(f"{r}_gathered{t % 2}"), 32 * (t // 2 + 1))
                ch(dve.scalar_tensor_tensor(x[:, t, :], gb[:, t % 2, 0, :], weight[:, t, 0:1], x[:, t, :], ALU.mult, ALU.add))
                ch.settle()
                dve.scalar_tensor_tensor(x[:, t, :], gb[:, t % 2, 1, :], weight[:, t, 1:2], x[:, t, :], ALU.mult, ALU.add).then_inc(S(r + "_x"), 1)

            experts(L[0])
            for g in range(NG):
                for t in range(g * GT, (g + 1) * GT):
                    combine(L[0], t)
                dve.wait_ge(S("r0_x"), GT * (g + 1))
                layernorm("a1", g, xln)
                if g:
                    choose(L[1], g - 1)
                dve.wait_ge(S("a1_s_ps"), g + 1)
                if g == 0:
                    dve.wait_ge(S("phi_set"), 1)
                for j in range(2):
                    ch(dve.scalar_tensor_tensor(att[:, 2 * j:2 * j + 2, :], ps[:, 4 + j, 0:2 * SK].rearrange("p (t s) -> p t s", s=SK), float(D) ** -0.5,
                                                phi[:, g * GT + 2 * j:g * GT + 2 * j + 2, :], ALU.mult, ALU.add))
                ch.settle()
                ch(dve.tensor_reduce(mx1[:, :], att[:, :, :], AX, ALU.max))
                ch.settle()
                dve.tensor_scalar(mx1[:, :], mx1[:, :], -1.0, None, ALU.mult).then_inc(S("a1_nm"), 1)
                if g:
                    place(L[1], g - 1)
                dve.wait_ge(S("a1_p"), GT * (g + 1))
                ch(dve.reciprocal(rd1[:, :], den1[:, :]))
                ch.settle()
                dve.wait_ge(S("a1_o_ps"), g + 1)
                for t in range(GT):
                    n = g * GT + t
                    dve.scalar_tensor_tensor(x[:, n, :], ps[:, t // 2, (t % 2) * D:(t % 2 + 1) * D], rd1[:, t:t + 1], x[:, n, :],
                                             ALU.mult, ALU.add).then_inc(S("a1_x"), 1)
                dve.wait_ge(S("a1_x"), GT * (g + 1))
                if g:
                    dve.wait_ge(S("r1_xT_ps"), g)
                layernorm("r1", g, xlr)
                rows_to_send(L[1], g)
            choose(L[1], NG - 1)
            place(L[1], NG - 1)
            count(L[1])
            experts(L[1])
            for t in range(NT):
                combine(L[1], t)


def kernel(**inputs):
    import numpy as np
    import concourse.bacc as bacc
    from concourse.bass_utils import run_bass_kernel_spmd

    i = {k: np.asarray(v) for k, v in inputs.items()}

    def by_row_chunk(w):
        e, r, c = w.shape
        return w.reshape(e, r // P, P, c).transpose(0, 2, 1, 3).reshape(e, P, -1)

    def column(b):
        return b.reshape(KC, P).T

    laid = {
        "x": i["x"].reshape(N, D),
        "ctxT": i["ctx_1024"].transpose(0, 2, 1),
        "mask": i["mask_BxSxS2_ik0"].reshape(N, SK),
        "maskT": i["mask_BxSxS2_ik0"].transpose(0, 2, 1),
        "phi": i["fside_BxSxS2_0"].reshape(N, SK),
        "wq": i["L0_xattn_wq"], "wk": i["L0_xattn_wk"], "wv": i["L0_xattn_wv"], "wo": i["L0_xattn_wo"],
        "bq": column(i["L0_xattn_bq"]), "bk": column(i["L0_xattn_bk"]), "bv": i["L0_xattn_bv"], "bo": i["L0_xattn_bo"],
        "Wq": i["L1_xattn_Wq"].T, "Wk": i["L1_xattn_Wk"].T, "Wv": i["L1_xattn_Wv"].T,
        "Bq": column(i["L1_xattn_bq"]), "Bk": column(i["L1_xattn_bk"]), "Bv": i["L1_xattn_bv"],
        "betas": np.stack([i["L1_xattn_beta_risk"].reshape(1), i["L1_xattn_beta_prio"].reshape(1), i["L1_xattn_beta_impl"].reshape(1)]),
        "gate0": i["L0_ffn_gate_w"].T, "gate1": i["L1_ffn_Wg"].T,
        "wg": by_row_chunk(i["L0_ffn_wg"].transpose(0, 2, 1)),
        "wu": by_row_chunk(i["L0_ffn_wu"].transpose(0, 2, 1)),
        "wd": by_row_chunk(i["L0_ffn_wd"].transpose(0, 2, 1)),
        "W1": by_row_chunk(i["L1_ffn_W1"]),
        "W2": by_row_chunk(i["L1_ffn_W2"]),
    }
    nc = bacc.Bacc("TRN2", target_bir_lowering=False, num_devices=1)
    arrays, a = {}, {}
    for name, v in laid.items():
        v = np.ascontiguousarray(v)
        arrays["in_" + name] = v
        a[name] = nc.dram_tensor("in_" + name, v.shape, mybir.dt.from_np(v.dtype), kind="ExternalInput").ap()
    out = nc.dram_tensor("out_x", (N, D), F32, kind="ExternalOutput").ap()
    two_layers(nc, a, out)
    r = run_bass_kernel_spmd(nc, [arrays], core_ids=[0])
    return r.results[0]["out_x"].reshape(i["x"].shape)
```

```python
from contextlib import ExitStack

import concourse.bass as bass
from concourse import mybir

ALU = mybir.AluOpType
ACT = mybir.ActivationFunctionType
AX = mybir.AxisListType.X
F32, F16, BF16 = mybir.dt.float32, mybir.dt.float16, mybir.dt.bfloat16
I32, U32 = mybir.dt.int32, mybir.dt.uint32

P = 128
D = 256
KC = D // P
H = 16
DK = D // H
B = 2
E = 8
TOP = 2
N = 2048
NT = N // P
GT = 4
NG = NT // GT
GW = GT * P
SK = 154
KM = P
KR = SK - KM
QW = 32
VW = 2 * DK + 1
PENALTY = -1e30
BLK = 256
REGION = N + BLK
MAXBLK = N * TOP // BLK + E
AHEAD = MAXBLK + 2
TB_ROW, TB_PAD = 16, 48
CH = 1024
STAGES = 3
FAR = 1 << 20
EPS = 1e-5


class Chain:

    def __init__(self, eng, sem):
        self.eng, self.sem, self.n = eng, sem, 0

    def __call__(self, ins):
        self.n += 1
        ins.then_inc(self.sem, 1)

    def settle(self):
        self.eng.wait_ge(self.sem, self.n)


def two_layers(nc, a, out):
    with ExitStack() as ctx:
        def sb(name, shape, dt=F32):
            return ctx.enter_context(nc.sbuf_tensor(name, shape, dt))

        sems = {}

        def S(name):
            if name not in sems:
                sems[name] = ctx.enter_context(nc.semaphore(name))
            return sems[name]

        ps = ctx.enter_context(nc.psum_tensor("ps", [P, 8, 512], F32))
        psh = ps[:, :, :].bitcast(F16)
        psb = ps[:, :, :].bitcast(BF16)

        rows = nc.dram_tensor("rows", (E * REGION, 2 * D), F16, kind="Internal").ap()
        results = nc.dram_tensor("results", (MAXBLK * BLK, D), F32, kind="Internal").ap()

        WS = 6144
        probs = sb("probs", [P, 2 * 20 * GW], F16)
        keys = sb("keys", [P, B * 2 * H * SK], F16)
        expo = sb("expo", [P, 2 * 4 * GW], F16)
        queries = sb("queries", [P, 2 * KC * GW], F16)
        inbox = sb("inbox", [P, 2 * 2 * 1664], F16)
        heads = sb("heads", [P, 2 * 2048], F16)
        def part(arena, at, shape, dt=F32, rows=P):
            size = 1
            for n in shape[1:]:
                size *= n
            width = size * (1 if dt in (F16, BF16) else 2)
            v = arena[0:rows, at:at + width]
            if dt != F16:
                v = v.bitcast(dt)
            if len(shape) > 2:
                names = "abcdef"[:len(shape) - 1]
                v = v.rearrange("p (" + " ".join(names) + ") -> p " + " ".join(names), **dict(zip(names[1:], shape[2:])))
            return v, at + width

        ident = sb("ident", [P, P])
        identb = sb("identb", [P, P], BF16)
        identh = sb("identh", [P, P], F16)
        earlier = sb("earlier", [P, P], BF16)
        onesb = sb("onesb", [P, P], BF16)
        iota_i = sb("iota_i", [P, AHEAD], I32)
        iota = sb("iota", [P, AHEAD])
        iota8 = iota[:, 0:8]
        head_of = sb("head_of", [P, 8], F16)
        quad_of = sb("quad_of", [P, 4], F16)
        m16 = sb("m16", [32, H], BF16)
        msel = sb("msel", [32, H, P], BF16)
        mselr = sb("mselr", [32, H, QW], BF16)
        esel = sb("esel", [32, 4, QW], BF16)
        zeros = sb("zeros", [P, 512])
        thr = sb("thr", [P, 7])
        le = sb("le", [P, 8, 8])

        x = sb("x", [P, NT, D])
        ctxT, at = part(probs, 0, [P, B, KC, SK])
        ctxR, at = part(probs, at, [P, B, KC, 4, QW])
        w_sb = {n: sb("w_" + n, [P, KC, D]) for n in ("wq", "wo", "Wq")}
        for n in ("wk", "wv", "Wk", "Wv"):
            w_sb[n], at = part(probs, at, [P, KC, D])
        v_tmp, at = part(probs, at, [P, D])
        v_hl, at = part(probs, at, [P, 2, D], F16)
        k_tmp, at = part(probs, at, [P, 2, SK], F16)
        bcol = {n: sb("b_" + n, [P, KC]) for n in ("bq", "bk", "Bq", "Bk")}
        brow = {n: sb("b_" + n, [P, D]) for n in ("bv", "bo", "Bv")}
        gate = [sb("gate0", [P, KC, E]), sb("gate1", [P, KC, E])]
        betas = sb("betas", [P, 4])
        phi, keys_at = part(keys, 0, [P, NT, SK])

        mask_raw, at = part(inbox, 0, [P, GT, SK], I32)
        maskT_raw, at = part(inbox, at, [P, GW], I32)
        maskR_raw, at = part(inbox, at, [QW, GW], I32, rows=QW)
        pen = sb("pen", [P, NT, SK], BF16)
        penT = sb("penT", [P, NG, GW], BF16)
        penR = sb("penR", [QW, NG, GW], BF16)

        k_blk, _ = part(keys, 0, [P, B, 2, H, SK], F16)
        k_rem = sb("k_rem", [P, B, 2, H, QW], F16)
        v_ext = sb("v_ext", [P, B, H, VW], F16)
        v_rem = sb("v_rem", [P, B, 4, 4, VW], F16)
        k1T = sb("k1T", [P, B, KC, SK])
        v1m = sb("v1m", [P, B, D])
        v1r = sb("v1r", [QW, B, D])

        stats = sb("stats", [P, GT, 6])
        mv = sb("mv", [P, GT, 2])
        ve = sb("ve", [P, GT])
        ry = sb("ry", [P, GT])
        rt = sb("rt", [P, GT])
        xln = sb("xln", [P, GT, D])
        xlr = sb("xlr", [P, GT, D])
        xT = sb("xT", [P, KC, GW])
        xTr = sb("xTr", [P, KC, GW])
        q_hi, at = part(queries, 0, [P, KC, GW], F16)
        q_lo, at = part(queries, at, [P, KC, GW], F16)
        mx = sb("mx", [P, GT, H])
        nm = sb("nm", [P, GT, 2 * H], BF16)
        nmT = sb("nmT", [2 * H, GW], BF16)
        e_ring, _ = part(expo, 0, [P, 4, GW])
        p_hi, at = part(probs, 0, [P, 20, GW], F16)
        p_lo, _ = part(probs, at, [P, 20, GW], F16)
        o_lo, at = part(heads, 0, [P, 2, 8, DK])
        o_sum, at = part(heads, at, [P, 2, 8, DK])
        o_n, at = part(heads, at, [P, 2, D])
        rden = sb("rden", [P, 2, 8])
        oT, at = part(heads, at, [P, 2, D])
        xo, at = part(heads, at, [P, D])

        att, at = part(expo, 0, [P, GT, SK])
        pT, at = part(expo, at, [P, GW])
        pTr, at = part(expo, at, [QW, GW], rows=QW)
        mx1 = sb("mx1", [P, GT])
        den1 = sb("den1", [P, GT])
        rd1 = sb("rd1", [P, GT])
        q1T, _ = part(queries, 0, [P, KC, GW])
        passed, at = part(queries, 0, [1, AHEAD, E], rows=1)
        skipped, at = part(queries, at, [1, E], rows=1)
        row_of, at = part(queries, at, [1, AHEAD], rows=1)
        in_use, at = part(queries, at, [1, AHEAD], rows=1)

        xp = sb("xp", [P, GT, 2 * D], F16)
        lg = sb("lg", [P, GT, E])
        mx8 = sb("mx8", [P, GT, 8])
        ix8 = sb("ix8", [P, GT, 8], U32)
        dv = sb("dv", [P, GT])
        ev = sb("ev", [P, GT])
        dn = sb("dn", [P, GT])
        sel = sb("sel", [P, GT, E])
        selb = sb("selb", [P, GT, E], BF16)
        cum = sb("cum", [P, GT + 1, E])
        cumb = sb("cumb", [P, GT + 1, E], BF16)
        ohp = sb("ohp", [P, NT, TOP, E])
        posk = sb("posk", [P, GT, TOP])
        drop = sb("drop", [P, GT, TOP])
        slotf = sb("slotf", [P, NT, TOP])
        idxf = sb("idxf", [P, NT, TOP])
        oh = sb("oh", [P, NT, TOP, E])
        pos_kept = sb("pos_kept", [P, NT, TOP])
        weight = sb("weight", [P, NT, TOP])
        slot_s = sb("slot_s", [P, NT, TOP], I32)
        slot_g = sb("slot_g", [P, NT, TOP], I32)
        cnt = sb("cnt", [P, E])
        over = sb("over", [P, E, 7])
        nblk = sb("nblk", [P, E])
        lem = sb("lem", [P, E, E])
        blk_end = sb("blk_end", [P, E])
        blk_row = sb("blk_row", [P, E])
        table = [sb("table0", [1, 64], I32), sb("table1", [1, 64], I32)]

        stage, _ = part(inbox, 0, [P, STAGES, CH])
        slot0 = sb("slot0", [P, 2, WS], F16)
        slot1, at = part(probs, 0, [P, 2, WS], F16)
        w_hl = [slot0, slot1]
        h_hi, at = part(probs, at, [P, 8, BLK], F16)
        h_lo, at = part(probs, at, [P, 8, BLK], F16)
        s_act, at = part(probs, at, [P, 2, 2 * BLK])
        x_raw, at = part(probs, at, [P, 2, 2 * D], F16)
        h32, keys_at = part(keys, keys_at, [P, 2, 2 * BLK])
        xbT, keys_at = part(keys, keys_at, [P, 2, KC, BLK], F16)
        yb, keys_at = part(keys, keys_at, [P, 2, D])
        gb, _ = part(heads, 0, [P, GT, TOP, D])

        class Layer:
            pass

        L = [Layer(), Layer()]
        for n, l in enumerate(L):
            l.n, l.r = n, f"r{n}"
            l.I = (1024, 512)[n]
            l.hc = l.I // P
            l.pairs = l.hc // 2
            l.cap = (N, N * TOP * 5 // 4 // E)[n]
            l.act = (ACT.Silu, ACT.Gelu)[n]
            l.gate_col = lambda kc, c, n=n: (kc * 1024 + c * P)
            l.up_col = lambda kc, c, n=n: ((2048, 512)[n] + kc * 1024 + c * P)
            l.down_at = (4096, 2048)[n]
            l.beside = (([0], [1], [2], [3], [4, 5]), ([0], [1, 2], []))[n]
        L[0].chunks = [(a[w], 1024 * i, 2048 * n + 1024 * i) for n, w in enumerate(("wg", "wu", "wd")) for i in range(2)]
        L[1].chunks = [(a["W1"], 0, 0), (a["W1"], 1024, 1024), (a["W2"], 0, 2048)]

        def wait_counted(eng, sem, value):
            eng.wait_ge(sem, value)
            eng.sem_inc(S("counted"), 1)

        block = ctx.enter_context(nc.Block())

        @block.sync
        def _(sp):
            for b in range(B):
                sp.dma_start(ctxT[:, b], a["ctxT"][b].rearrange("(k p) s -> p k s", p=P)).then_inc(S("ld_kv"), 16)
            for n in ("wk", "wv", "Wk", "Wv"):
                sp.dma_start(w_sb[n][:, :, :], a[n].rearrange("(k p) n -> p k n", p=P)).then_inc(S("ld_kv"), 16)
            for n in ("bq", "bk", "Bq", "Bk"):
                sp.dma_start(bcol[n][:, :], a[n]).then_inc(S("ld_kv"), 16)
            for n in ("bv", "bo", "Bv"):
                sp.dma_start(brow[n][:, :], a[n].unsqueeze(0).broadcast_to([P, D])).then_inc(S("ld_kv"), 16)
            for g in range(NG):
                sp.dma_start(x[:, g * GT:(g + 1) * GT, :],
                             a["x"][g * GW:(g + 1) * GW, :].rearrange("(t p) d -> p t d", p=P)).then_inc(S(f"ld_x{g}"), 16)
                if g == 0:
                    for n in ("wq", "wo", "Wq"):
                        sp.dma_start(w_sb[n][:, :, :], a[n].rearrange("(k p) n -> p k n", p=P)).then_inc(S("ld_w"), 16)
                    for n in range(2):
                        sp.dma_start(gate[n][:, :, :], a[f"gate{n}"].rearrange("(k p) e -> p k e", p=P)).then_inc(S("ld_w"), 16)
            for g in range(NG):
                if g:
                    sp.wait_ge(S("mask_used"), 3 * g)
                b, q0 = g // 2, (g % 2) * GW
                sp.dma_start(mask_raw[:, :, :], a["mask"][g * GW:(g + 1) * GW, :].rearrange("(t p) s -> p t s", p=P)).then_inc(S("ld_mask"), 16)
                sp.dma_start(maskT_raw[:, :], a["maskT"][b, 0:KM, q0:q0 + GW]).then_inc(S("ld_mask"), 16)
                sp.dma_start(maskR_raw[0:KR, :], a["maskT"][b, KM:SK, q0:q0 + GW]).then_inc(S("ld_mask"), 16)
            for n in range(3):
                sp.dma_start(betas[:, n:n + 1], a["betas"][n].unsqueeze(0).broadcast_to([P, 1])).then_inc(S("ld_phi"), 16)
            sp.wait_ge(S("zeros_set"), 1)
            yz = results.rearrange("(n p r s) d -> n p r (s d)", p=P, r=4, s=2)
            for n in range(MAXBLK * BLK // (P * 8)):
                sp.dma_start(yz[n], zeros[:, :].unsqueeze(1).broadcast_to([P, 4, 512])).then_inc(S("results_zero"), 16)

            def fetch(l, e, n):
                src, col, _ = l.chunks[n]
                k = len(l.chunks)
                if isinstance(e, int):
                    if e * k + n >= STAGES:
                        sp.wait_ge(S(f"w_ready{l.n}"), e * k + n - STAGES + 1)
                    w = src[e]
                else:
                    sp.wait_ge(S(f"w_ready{l.n}"), e * k + n - STAGES + 1)
                    w = src[bass.ds(e, 1), :, :].rearrange("e p n -> (e p) n")
                sp.dma_start(stage[:, n % STAGES, :], w[:, col:col + CH]).then_inc(S(f"staged{l.n}_{n}"), 16)

            def clear_padding(l):
                def clear(e, signal):
                    row = sp.value_load(table[l.n][0:1, bass.ds(e + TB_PAD, 1)], min_val=0, max_val=E * REGION - BLK)
                    sp.dma_start(rows[bass.ds(row, BLK), :].rearrange("(p s) d -> p (s d)", p=P),
                                 zeros[:, :].bitcast(F16)).then_inc(S(signal), 16)

                sp.wait_ge(S(l.r + "_table"), 1)
                clear(0, l.r + "_padded_first")
                with sp.Fori(1, E) as e:
                    clear(e, l.r + "_padded")

            sp.wait_ge(S("mask_used"), 3 * NG)
            k0 = len(L[0].chunks)
            for n in range(k0 + STAGES):
                fetch(L[0], n // k0, n % k0)
            sp.wait_ge(S("a0_st"), 20 * NG)
            sp.dma_start(phi[:, :, :], a["phi"].rearrange("(t p) s -> p t s", p=P)).then_inc(S("ld_phi"), 16)
            clear_padding(L[0])
            for n in range(STAGES, k0):
                fetch(L[0], 1, n)
            with sp.Fori(2, E) as e:
                for n in range(k0):
                    fetch(L[0], e, n)
            sp.wait_ge(S("w_ready0"), E * k0)
            for e in range(2):
                for n in range(len(L[1].chunks)):
                    fetch(L[1], e, n)
            clear_padding(L[1])
            with sp.Fori(2, E) as e:
                for n in range(len(L[1].chunks)):
                    fetch(L[1], e, n)
            for t in range(NT):
                sp.wait_ge(S("r1_x"), t + 1)
                sp.dma_start(out[t * P:(t + 1) * P, :], x[:, t, :]).then_inc(S("stored"), 16)
            sp.wait_ge(S("stored"), 16 * NT)

        @block.gpsimd
        def _(pool):
            ch = Chain(pool, S("pool_step"))
            ch(pool.memset(ident[:, :], 0.0))
            ch(pool.memset(identb[:, :], 1.0))
            ch.settle()
            ch(pool.affine_select(out=ident[:, :], in_=ident[:, :], compare_op=ALU.not_equal, fill=1.0, base=0,
                                  pattern=[[-1, P]], channel_multiplier=1))
            ch(pool.affine_select(out=earlier[:, :], in_=identb[:, :], compare_op=ALU.is_gt, fill=0.0, base=0,
                                  pattern=[[1, P]], channel_multiplier=-1))
            ch.settle()
            ch(pool.tensor_copy(identb[:, :], ident[:, :]))
            ch(pool.tensor_copy(identh[:, :], ident[:, :]))
            ch(pool.memset(onesb[:, :], 1.0))
            ch(pool.iota(iota_i[:, :], pattern=[[1, AHEAD]], base=0, channel_multiplier=0))
            ch.settle()
            ch(pool.tensor_copy(iota[:, :], iota_i[:, :]))
            ch.settle()
            ch(pool.tensor_scalar(thr[:, :], iota8[:, 1:8], float(BLK), None, ALU.mult))
            pool.memset(penR[:, :, :], PENALTY).then_inc(S("consts"), 1)
            ch(pool.memset(ctxR[:, :, :, :, :], 0.0))
            ch(pool.memset(k_rem[:, :, :, :, :], 0.0))
            ch(pool.memset(v_ext[:, :, :, :], 1.0))
            ch.settle()
            pool.memset(v_rem[:, :, :, :, :], 0.0).then_inc(S("blanks"), 1)
            pool.memset(zeros[:, :], 0.0).then_inc(S("zeros_set"), 1)

            for g in range(NG):
                pool.wait_ge(S("ld_mask"), 48 * (g + 1))
                if g == 0:
                    pool.wait_ge(S("consts"), 1)
                pool.tensor_scalar(pen[:, g * GT:(g + 1) * GT, :], mask_raw[:, :, :], 0.0, PENALTY, ALU.is_equal, ALU.mult).then_inc(S("mask_used"), 1)
                pool.tensor_scalar(penT[:, g, :], maskT_raw[:, :], 0.0, PENALTY, ALU.is_equal, ALU.mult).then_inc(S("mask_used"), 1)
                pool.tensor_scalar(penR[0:KR, g, :], maskR_raw[0:KR, :], 0.0, PENALTY, ALU.is_equal, ALU.mult).then_inc(S("mask_used"), 1)

            def low_parts(l, e, slot, chunks):
                k = len(l.chunks)
                for n in chunks:
                    at = l.chunks[n][2]
                    pool.wait_ge(S(f"w_hi{l.n}"), e * k + n + 1)
                    pool.tensor_tensor(w_hl[slot][:, 1, at:at + CH], stage[:, n % STAGES, :], w_hl[slot][:, 0, at:at + CH],
                                       ALU.subtract).then_inc(S(f"w_ready{l.n}"), 1)

            def rest_of_experts(l):
                low_parts(l, 1, 1, range(len(l.chunks)))
                with pool.Fori(1, E // 2) as pr:
                    for slot in range(2):
                        low_parts(l, pr * 2 + slot, slot, range(len(l.chunks)))

            def scatter(l, g):
                r = l.r
                pool.wait_ge(S(r + "_xp"), g + 1)
                pool.wait_ge(S(r + "_slot"), g + 1)
                for t in range(GT):
                    for k in range(TOP):
                        pool.indirect_dma_start(
                            out=rows, out_offset=bass.IndirectOffsetOnAxis(ap=slot_s[:, g * GT + t, k:k + 1], axis=0),
                            in_=xp[:, t, :], in_offset=None, bounds_check=E * REGION - 1,
                            oob_is_err=False).then_inc(S(r + "_scattered"), 16)

            def results_stored(l):
                r = l.r
                total = pool.value_load(table[l.n][0:1, 8:9], min_val=1, max_val=MAXBLK)
                wait_counted(pool, S(r + "_stored"), total * 16 + 16)
                if l.n == 0:
                    pool.wait_ge(S("results_zero"), 16 * (MAXBLK * BLK // (P * 8)))

            def gather(l, g):
                r = l.r
                for t in range(g * GT, (g + 1) * GT):
                    if t >= GT:
                        pool.wait_ge(S(r + "_x"), t - GT + 1)
                    for k in range(TOP):
                        pool.indirect_dma_start(
                            out=gb[:, t % GT, k, :], out_offset=None, in_=results,
                            in_offset=bass.IndirectOffsetOnAxis(ap=slot_g[:, t, k:k + 1], axis=0),
                            bounds_check=MAXBLK * BLK - 1, oob_is_err=False).then_inc(S(f"{r}_gathered{t % GT}"), 16)

            k0 = len(L[0].chunks)
            low_parts(L[0], 0, 0, range(STAGES))
            scatter(L[0], 0)
            low_parts(L[0], 0, 0, range(STAGES, k0))
            for g in range(1, NG):
                scatter(L[0], g)
            rest_of_experts(L[0])
            pool.wait_ge(S("ld_phi"), 64)
            ch(pool.tensor_tensor(betas[:, 3:4], betas[:, 0:1], betas[:, 1:2], ALU.add))
            ch.settle()
            ch(pool.tensor_tensor(betas[:, 3:4], betas[:, 3:4], betas[:, 2:3], ALU.subtract))
            ch.settle()
            pool.tensor_scalar(phi[:, :, :], phi[:, :, :], betas[:, 3:4], None, ALU.mult).then_inc(S("phi_set"), 1)
            results_stored(L[0])
            gather(L[0], 0)
            gather(L[0], 1)
            low_parts(L[1], 0, 0, range(len(L[1].chunks)))
            gather(L[0], 2)
            scatter(L[1], 0)
            gather(L[0], 3)
            for g in range(1, NG):
                scatter(L[1], g)
            rest_of_experts(L[1])
            results_stored(L[1])
            for g in range(NG):
                gather(L[1], g)

        @block.tensor
        def _(pe):
            def mm(o, l, r, start, stop, **kw):
                return pe.matmul(o, l, r, start=start, stop=stop, **kw)

            pe.wait_ge(S("ld_kv"), 13 * 16)
            pe.wait_ge(S("ctx_rep"), 1)
            for b in range(B):
                for oc in range(KC):
                    for kc in range(KC):
                        mm(ps[:, 2 * b + oc, 0:SK], w_sb["wk"][:, kc, oc * P:(oc + 1) * P], ctxT[:, b, kc, :], kc == 0, kc == 1)
                for kc in range(KC):
                    mm(ps[:, 4 + b, 0:D], ctxT[:, b, kc, 0:KM], w_sb["wv"][:, kc, :], kc == 0, kc == 1)
                for kc in range(KC):
                    last = mm(ps[:, 6 + b, 0:D], ctxR[:, b, kc, :, :].rearrange("p a j -> p (a j)"), w_sb["wv"][:, kc, :], kc == 0, kc == 1)
            last.then_inc(S("kv_ps"), 1)
            pe.wait_ge(S("kv_done"), 1)
            for b in range(B):
                for oc in range(KC):
                    for kc in range(KC):
                        mm(ps[:, 2 * b + oc, 0:SK], w_sb["Wk"][:, kc, oc * P:(oc + 1) * P], ctxT[:, b, kc, :], kc == 0, kc == 1)
                for kc in range(KC):
                    mm(ps[:, 4 + b, 0:D], ctxT[:, b, kc, 0:KM], w_sb["Wv"][:, kc, :], kc == 0, kc == 1)
                for kc in range(KC):
                    last = mm(ps[0:KR, 6 + b, 0:D], ctxT[:, b, kc, KM:SK], w_sb["Wv"][:, kc, :], kc == 0, kc == 1)
            last.then_inc(S("kv_ps"), 1)
            pe.wait_ge(S("kv_done"), 2)
            pe.wait_ge(S("ld_w"), 5 * 16)

            def turn(c, g, src, bank=0):
                pe.wait_ge(S(c + "_ln"), g + 1)
                for kc in range(KC):
                    for t in range(GT):
                        last = pe.transpose(ps[:, bank + kc, t * P:(t + 1) * P], src[:, t, kc * P:(kc + 1) * P], ident[:, :])
                last.then_inc(S(c + "_xT_ps"), 1)

            def project_q(c, g, w):
                pe.wait_ge(S(c + "_xT"), g + 1)
                for oc in range(KC):
                    for kc in range(KC):
                        last = mm(ps[:, 2 + oc, :], w[:, kc, oc * P:(oc + 1) * P], xT[:, kc, :], kc == 0, kc == 1)
                last.then_inc(S(c + "_q_ps"), 1)

            def score_max(g):
                b = g // 2
                pe.wait_ge(S("a0_qlo"), 2 * (g + 1))
                pe.wait_ge(S("mask_used"), 3 * (g + 1))
                for n in range(12):
                    t, h0 = n // 3, (n % 3) * 6
                    if n >= 2:
                        pe.wait_ge(S("a0_mx"), 12 * g + n - 1)
                    for j in range(2):
                        heads = range(h0 + 3 * j, min(h0 + 3 * j + 3, H))
                        o = ps[:, 2 * (n % 2) + j, 0:len(heads) * SK].rearrange("p (h s) -> p h s", s=SK)
                        mm(o, identb[:, :], pen[:, g * GT + t, :].unsqueeze(1).broadcast_to([P, len(heads), SK]), True, False)
                        for oc in range(KC):
                            part = [h for h in heads if h // 8 == oc]
                            if part:
                                last = mm(o[:, part[0] - heads[0]:part[-1] - heads[0] + 1, :], q_hi[:, oc, t * P:(t + 1) * P],
                                          k_blk[:, b, 0, part[0]:part[-1] + 1, :], False, part[-1] == heads[-1])
                    last.then_inc(S("a0_s_ps"), 1)

            def turn_max(g):
                pe.wait_ge(S("a0_nm"), g + 1)
                for t in range(GT):
                    last = pe.transpose(psb[0:32, 0, t * P:(t + 1) * P], nm[:, t, :], identb[:, :])
                last.then_inc(S("a0_mT_ps"), 1)

            def scores(g):
                b = g // 2
                pe.wait_ge(S("a0_mT"), g + 1)
                if g:
                    pe.wait_ge(S("a0_oev"), 4 * g)
                for u in range(20):
                    if u >= 2:
                        pe.wait_ge(S("a0_exp"), 20 * g + u - 1)
                    o = ps[:, 4 + u % 2, :]
                    if u < H:
                        kh, kl = (k_blk[:, b, i, u, 0:KM] for i in range(2))
                        oc, who, lp, rp = u // 8, msel[:, u, :], identb[:, :], penT[:, g, :]
                    else:
                        r = u - H
                        kh, kl = (k_rem[:, b, i, 4 * r:4 * r + 4, :].rearrange("p h j -> p (h j)") for i in range(2))
                        oc, who = r // 2, mselr[:, 4 * r:4 * r + 4, :].rearrange("p h j -> p (h j)")
                        lp, rp = esel[:, :, :].rearrange("p a j -> p (a j)"), penR[:, g, :]
                    mm(o, kh, q_hi[:, oc, :], True, False)
                    mm(o, kl, q_hi[:, oc, :], False, False)
                    mm(o, kh, q_lo[:, oc, :], False, False)
                    mm(o, lp, rp, False, False)
                    mm(o, who, nmT[:, :], False, True).then_inc(S("a0_st"), 1)

            def weigh_values(g, t):
                b, at = g // 2, 6 - 2 * (t % 2)
                pe.wait_ge(S("a0_plo"), 20 * (g + 1))
                if t >= 2:
                    pe.wait_ge(S("a0_oev"), 4 * g + t - 1)
                elif t == 0 and g:
                    pe.wait_ge(S("a0_oev"), 4 * g - 1)
                tk = slice(t * P, (t + 1) * P)
                for j in range(2):
                    o = ps[:, at + j, 0:8 * VW].rearrange("p (h v) -> p h v", v=VW)
                    for h in range(8):
                        mm(o[:, h, :], p_hi[:, 8 * j + h, tk], v_ext[:, b, 8 * j + h, :], h == 0, False, skip_group_check=True)
                        mm(o[:, h, 0:DK + 1], p_lo[:, 8 * j + h, tk], v_ext[:, b, 8 * j + h, 0:DK + 1], False, False, skip_group_check=True)
                    for r in range(2):
                        q = 2 * j + r
                        mm(o[:, 4 * r:4 * r + 4, :], p_hi[:, H + q, tk], v_rem[:, b, q, :, :], False, False, skip_group_check=True)
                        last = mm(o[:, 4 * r:4 * r + 4, 0:DK + 1], p_lo[:, H + q, tk], v_rem[:, b, q, :, 0:DK + 1], False, r == 1, skip_group_check=True)
                last.then_inc(S("a0_o_ps"), 1)

            def turn_out(g, t):
                n = 4 * g + t
                pe.wait_ge(S("a0_on"), n + 1)
                if t == 0:
                    pe.wait_ge(S("a0_mx"), 12 * min(g + 2, NG))
                if n >= 2:
                    pe.wait_ge(S("a0_oT"), n - 1)
                for kc in range(KC):
                    last = pe.transpose(ps[:, t % 2, kc * P:(kc + 1) * P], o_n[:, t % 2, kc * P:(kc + 1) * P], ident[:, :])
                last.then_inc(S("a0_oT_ps"), 1)

            def project_out(g, t):
                n = 4 * g + t
                pe.wait_ge(S("a0_oT"), n + 1)
                if n >= 2:
                    pe.wait_ge(S("a0_x"), n - 1)
                for kc in range(KC):
                    last = mm(ps[:, 2 + t % 2, 0:D], oT[:, t % 2, kc * P:(kc + 1) * P], w_sb["wo"][:, kc, :], kc == 0, kc == 1)
                last.then_inc(S("a0_op_ps"), 1)

            def route_logits(l, g):
                turn(l.r, g, xlr)
                pe.wait_ge(S(l.r + "_xT"), g + 1)
                for t in range(GT):
                    for kc in range(KC):
                        last = mm(ps[:, 2, t * E:(t + 1) * E], xTr[:, kc, t * P:(t + 1) * P], gate[l.n][:, kc, :], kc == 0, kc == 1)
                last.then_inc(S(l.r + "_lg_ps"), 1)

            def route_positions(l, g):
                pe.wait_ge(S(l.r + "_sel"), g + 1)
                o = ps[:, 3, 0:GT * E]
                mm(o, earlier[:, :], selb[:, :, :].rearrange("p t e -> p (t e)"), True, False)
                mm(o, onesb[:, :], cumb[:, 0:GT, :].rearrange("p t e -> p (t e)"), False, True).then_inc(S(l.r + "_pos_ps"), 1)

            def route_counts(l):
                pe.wait_ge(S(l.r + "_slot"), NG)
                mm(ps[:, 3, 0:E], onesb[:, :], cumb[:, GT, :], True, True).then_inc(S(l.r + "_cnt_ps"), 1)

            turn("a0", 0, xln)
            project_q("a0", 0, w_sb["wq"])
            score_max(0)
            for g in range(NG):
                turn_max(g)
                scores(g)
                if g:
                    route_logits(L[0], g - 1)
                if g + 1 < NG:
                    turn("a0", g + 1, xln)
                    if g:
                        pe.wait_ge(S("r0_lg"), g)
                    project_q("a0", g + 1, w_sb["wq"])
                    score_max(g + 1)
                if g:
                    pe.wait_ge(S("a0_mx"), 12 * min(g + 2, NG))
                    route_positions(L[0], g - 1)
                    pe.wait_ge(S("r0_slot"), g)
                for t in range(GT + 2):
                    if t < GT:
                        weigh_values(g, t)
                    if 1 <= t <= GT:
                        turn_out(g, t - 1)
                    if t >= 2:
                        project_out(g, t - 2)
            pe.wait_ge(S("a0_x"), NT)
            route_logits(L[0], NG - 1)
            route_positions(L[0], NG - 1)
            route_counts(L[0])

            def experts(l):
                r, tb, pairs = l.r, table[l.n], l.pairs

                def turn_block(g):
                    pe.wait_ge(S(r + "_xraw"), g * 16 + 16)
                    for hf in range(2):
                        for part in range(4):
                            last = pe.transpose(psh[:, 6, part * BLK + hf * P:part * BLK + (hf + 1) * P],
                                                x_raw[:, hf, part * P:(part + 1) * P], identh[:, :])
                    last.then_inc(S(r + "_xbT_ps"), 1)

                pe.sem_inc(S(r + "_xbT_ps"), 1)
                pe.sem_inc(S(r + "_down"), 1)
                pe.wait_ge(S(r + "_table"), 1)
                turn_block(0)
                with pe.Fori(0, E // 2) as pr:
                    for slot in range(2):
                        first = pe.value_load(tb[0:1, bass.ds(pr * 2 + slot, 1)], min_val=0, max_val=MAXBLK - 1)
                        end = pe.value_load(tb[0:1, bass.ds(pr * 2 + slot + 1, 1)], min_val=1, max_val=MAXBLK)
                        wait_counted(pe, S(f"w_ready{l.n}"), (pr * 2 + slot + 1) * len(l.chunks))
                        wh, wl = w_hl[slot][:, 0, :], w_hl[slot][:, 1, :]
                        with pe.Fori(first, end) as g:
                            pe.wait_ge(S(r + "_xbT"), g + 1)
                            for j in range(pairs):
                                pe.wait_ge(S(r + "_h32"), g * pairs + j + 1)
                                for which, col in enumerate((l.gate_col, l.up_col)):
                                    for i in range(2):
                                        o = ps[:, 2 * (j % 2) + which, i * BLK:(i + 1) * BLK]
                                        for kc in range(KC):
                                            at = col(kc, 2 * j + i)
                                            mm(o, wh[:, at:at + P], xbT[:, 0, kc, :], kc == 0, False)
                                            mm(o, wh[:, at:at + P], xbT[:, 1, kc, :], False, False)
                                            last = mm(o, wl[:, at:at + P], xbT[:, 0, kc, :], False, kc == 1)
                                    last.then_inc(S(r + "_gu_ps"), 1)
                            turn_block(g + 1)
                            pe.wait_ge(S(r + "_y"), g + 1)
                            for c in range(l.hc):
                                if c % 2 == 0:
                                    pe.wait_ge(S(r + "_h"), g * pairs + c // 2 + 2)
                                at = l.down_at + c * D
                                for hf in range(2):
                                    o, tk = ps[:, 4 + hf, 0:D], slice(hf * P, (hf + 1) * P)
                                    mm(o, h_hi[:, c, tk], wh[:, at:at + D], c == 0, False)
                                    mm(o, h_hi[:, c, tk], wl[:, at:at + D], False, False)
                                    last = mm(o, h_lo[:, c, tk], wh[:, at:at + D], False, c == l.hc - 1)
                            last.then_inc(S(r + "_down"), 1)

            experts(L[0])

            turn("a1", 0, xln, 6)
            project_q("a1", 0, w_sb["Wq"])
            for g in range(NG):
                b = g // 2
                pe.wait_ge(S("a1_q"), g + 1)
                for t in range(GT):
                    for kc in range(KC):
                        last = mm(ps[:, 4 + t // 2, (t % 2) * SK:(t % 2 + 1) * SK], q1T[:, kc, t * P:(t + 1) * P], k1T[:, b, kc, :], kc == 0, kc == 1)
                last.then_inc(S("a1_s_ps"), 1)
                if g:
                    route_logits(L[1], g - 1)
                pe.wait_ge(S("a1_p"), GT * (g + 1))
                for t in range(GT):
                    pe.transpose(ps[:, 6, t * P:(t + 1) * P], att[:, t, 0:KM], ident[:, :])
                for t in range(GT):
                    last = pe.transpose(ps[0:KR, 7, t * P:(t + 1) * P], att[:, t, KM:SK], ident[:, :])
                last.then_inc(S("a1_pT_ps"), 1)
                pe.wait_ge(S("a1_pT"), 2 * (g + 1))
                for t in range(GT):
                    o = ps[:, t // 2, (t % 2) * D:(t % 2 + 1) * D]
                    mm(o, pT[:, t * P:(t + 1) * P], v1m[:, b, :], True, False)
                    last = mm(o, pTr[0:KR, t * P:(t + 1) * P], v1r[0:KR, b, :], False, True)
                last.then_inc(S("a1_o_ps"), 1)
                if g + 1 < NG:
                    turn("a1", g + 1, xln, 6)
                    if g:
                        pe.wait_ge(S("r1_lg"), g)
                    if g >= 2:
                        pe.wait_ge(S("r1_slot"), g - 1)
                    project_q("a1", g + 1, w_sb["Wq"])
                if g:
                    pe.wait_ge(S("a1_q"), min(g + 2, NG))
                    route_positions(L[1], g - 1)
            pe.wait_ge(S("r1_slot"), NG - 1)
            route_logits(L[1], NG - 1)
            route_positions(L[1], NG - 1)
            route_counts(L[1])
            experts(L[1])

        @block.scalar
        def _(act):
            def x_evac(c, g, dst, bank=0):
                act.wait_ge(S(c + "_xT_ps"), g + 1)
                act.copy(dst[:, :, :], ps[:, bank:bank + 2, :]).then_inc(S(c + "_xT"), 1)

            def q_parts(g):
                act.wait_ge(S("a0_q_ps"), g + 1)
                for oc in range(KC):
                    act.activation(q_hi[:, oc, :], ps[:, 2 + oc, :], ACT.Identity, bias=bcol["bq"][:, oc:oc + 1]).then_inc(S("a0_qhi"), 1)

            def gates(l, g):
                act.wait_ge(S(l.r + "_d"), g + 1)
                act.activation(ev[:, :], dv[:, :], ACT.Exp).then_inc(S(l.r + "_e"), 1)

            def high_part(l, e, slot, n):
                at = l.chunks[n][2]
                act.wait_ge(S(f"staged{l.n}_{n}"), (e + 1) * 16)
                act.copy(w_hl[slot][:, 0, at:at + CH], stage[:, n % STAGES, :]).then_inc(S(f"w_hi{l.n}"), 1)

            act.wait_ge(S("ld_kv"), 13 * 16)
            x_evac("a0", 0, xT)
            q_parts(0)
            for g in range(NG):
                act.wait_ge(S("a0_mT_ps"), g + 1)
                act.copy(nmT[:, :], psb[0:32, 0, 0:GW]).then_inc(S("a0_mT"), 1)
                for u in range(21):
                    if u < 20:
                        act.wait_ge(S("a0_st"), 20 * g + u + 1)
                        if 20 * g + u >= 4:
                            act.wait_ge(S("a0_plo"), 20 * g + u - 3)
                        act.activation(e_ring[:, u % 4, :], ps[:, 4 + u % 2, :], ACT.Exp, scale=float(DK) ** -0.5).then_inc(S("a0_exp"), 1)
                    if u:
                        act.wait_ge(S("a0_exp"), 20 * g + u)
                        act.copy(p_hi[:, u - 1, :], e_ring[:, (u - 1) % 4, :]).then_inc(S("a0_phi"), 1)
                if g:
                    x_evac("r0", g - 1, xTr)
                if g + 1 < NG:
                    x_evac("a0", g + 1, xT)
                    q_parts(g + 1)
                if g:
                    gates(L[0], g - 1)
                for t in range(GT + 1):
                    if t < GT:
                        n = 4 * g + t
                        act.wait_ge(S("a0_o_ps"), n + 1)
                        if n:
                            act.wait_ge(S("a0_oev"), n)
                        at = 6 - 2 * (t % 2)
                        act.copy(o_lo[:, :, :, :], ps[:, at:at + 2, 0:8 * VW].rearrange("p b (h v) -> p b h v", v=VW)[:, :, :, DK + 1:VW]).then_inc(S("a0_olo"), 1)
                    if t:
                        n = 4 * g + t - 1
                        act.wait_ge(S("a0_oT_ps"), n + 1)
                        if n >= 2:
                            act.wait_ge(S("a0_op_ps"), n - 1)
                        act.copy(oT[:, (t - 1) % 2, :], ps[:, (t - 1) % 2, 0:D]).then_inc(S("a0_oT"), 1)
                if g < 2:
                    for n in range(STAGES):
                        high_part(L[0], 0, 0, g * STAGES + n)
            x_evac("r0", NG - 1, xTr)
            gates(L[0], NG - 1)

            def experts(l):
                r, pairs = l.r, l.pairs
                act.sem_inc(S(r + "_y"), 1)
                act.sem_inc(S(r + "_stored"), 16)
                act.wait_ge(S(r + "_table"), 1)

                tb = table[l.n]

                def load(g):
                    row = act.value_load(tb[0:1, bass.ds(g + TB_ROW, 1)], min_val=0, max_val=E * REGION - BLK)
                    act.dma_start(x_raw[:, :, :], rows[bass.ds(row, BLK), :].rearrange("(h p) d -> p h d", p=P)).then_inc(S(r + "_xraw"), 16)

                def one_block(g, coming=None):
                    def split(step):
                        if coming:
                            for n in l.beside[step]:
                                high_part(l, *coming, n)

                    for j in range(pairs):
                        act.wait_ge(S(r + "_h32"), g * pairs + j + 1)
                        act.wait_ge(S(r + "_gu_ps"), (g * pairs + j) * 2 + 1)
                        act.activation(s_act[:, j % 2, :], ps[:, 2 * (j % 2), :], l.act).then_inc(S(r + "_s"), 1)
                        split(j)
                    act.wait_ge(S(r + "_xbT_ps"), g + 3)
                    load(g + 2)
                    act.wait_ge(S(r + "_down"), g + 2)
                    act.wait_ge(S(r + "_stored"), g * 16 + 16)
                    act.copy(yb[:, :, :], ps[:, 4:6, 0:D]).then_inc(S(r + "_y"), 1)
                    act.wait_ge(S(r + "_y"), g + 2)
                    act.dma_start(results[bass.ds(g * BLK, BLK), :].rearrange("(h p) d -> p h d", p=P), yb[:, :, :]).then_inc(S(r + "_stored"), 16)
                    split(pairs)

                def blocks_of(e, coming=None):
                    first = act.value_load(tb[0:1, bass.ds(e, 1)], min_val=0, max_val=MAXBLK - 1)
                    end = act.value_load(tb[0:1, bass.ds(e + 1, 1)], min_val=1, max_val=MAXBLK)
                    if coming:
                        one_block(first, coming)
                        with act.If(end - first - 1):
                            with act.Fori(first + 1, end) as g:
                                one_block(g)
                    else:
                        with act.Fori(first, end) as g:
                            one_block(g)

                act.wait_ge(S(r + "_padded_first"), 16)
                act.wait_ge(S(r + "_scattered"), 16 * NT * TOP)
                load(0)
                act.wait_ge(S(r + "_padded"), 16 * (E - 1))
                act.wait_ge(S(r + "_xbT_ps"), 2)
                load(1)
                with act.Fori(0, E // 2 - 1) as pr:
                    blocks_of(pr * 2, (pr * 2 + 1, 1))
                    blocks_of(pr * 2 + 1, (pr * 2 + 2, 0))
                blocks_of(E - 2, (E - 1, 1))
                blocks_of(E - 1)
                total = act.value_load(tb[0:1, 8:9], min_val=1, max_val=MAXBLK)
                wait_counted(act, S(r + "_xraw"), total * 16 + 32)
                wait_counted(act, S(r + "_stored"), total * 16 + 16)

            act.wait_ge(S("results_zero"), 16 * (MAXBLK * BLK // (P * 8)))
            experts(L[0])
            for n in range(len(L[1].chunks)):
                high_part(L[1], 0, 0, n)

            def queries_of(g):
                x_evac("a1", g, xT, 6)
                act.wait_ge(S("a1_q_ps"), g + 1)
                for oc in range(KC):
                    last = act.activation(q1T[:, oc, :], ps[:, 2 + oc, :], ACT.Identity, bias=bcol["Bq"][:, oc:oc + 1])
                last.then_inc(S("a1_q"), 1)

            queries_of(0)
            for g in range(NG):
                if g:
                    x_evac("r1", g - 1, xTr)
                act.wait_ge(S("a1_nm"), g + 1)
                for t in range(GT):
                    act.activation(att[:, t, :], att[:, t, :], ACT.Exp, bias=mx1[:, t:t + 1], accum_out=den1[:, t:t + 1]).then_inc(S("a1_p"), 1)
                act.wait_ge(S("a1_pT_ps"), g + 1)
                act.copy(pT[:, :], ps[:, 6, :]).then_inc(S("a1_pT"), 1)
                act.copy(pTr[0:KR, :], ps[0:KR, 7, :]).then_inc(S("a1_pT"), 1)
                if g + 1 < NG:
                    queries_of(g + 1)
                if g:
                    gates(L[1], g - 1)
            x_evac("r1", NG - 1, xTr)
            gates(L[1], NG - 1)
            experts(L[1])

        @block.vector
        def _(dve):
            ch = Chain(dve, S("dve_step"))

            def layernorm(c, g, dst):
                for t in range(GT):
                    ch(dve.bn_stats(stats[:, t, :], x[:, g * GT + t, :]))
                ch.settle()
                for t in range(GT):
                    ch(dve.bn_aggr(mv[:, t, :], stats[:, t, :]))
                ch.settle()
                ch(dve.tensor_scalar(ve[:, :], mv[:, :, 1], EPS, None, ALU.add))
                ch.settle()
                ch(dve.tensor_scalar(ry[:, :].bitcast(I32), ve[:, :].bitcast(I32), -0.5, 1597463007.0, ALU.mult, ALU.add))
                ch.settle()
                for _ in range(3):
                    ch(dve.tensor_tensor(rt[:, :], ry[:, :], ry[:, :], ALU.mult))
                    ch.settle()
                    ch(dve.scalar_tensor_tensor(rt[:, :], rt[:, :], -0.5, ve[:, :], ALU.mult, ALU.mult))
                    ch.settle()
                    ch(dve.scalar_tensor_tensor(ry[:, :], rt[:, :], 1.5, ry[:, :], ALU.add, ALU.mult))
                    ch.settle()
                for t in range(GT):
                    ins = dve.tensor_scalar(dst[:, t, :], x[:, g * GT + t, :], mv[:, t, 0:1], ry[:, t:t + 1], ALU.subtract, ALU.mult)
                    if t < GT - 1:
                        ch(ins)
                ins.then_inc(S(c + "_ln"), 1)

            dve.wait_ge(S("consts"), 1)
            ch(dve.tensor_tensor(le[:, :, :], iota8[:, :].unsqueeze(1).broadcast_to([P, 8, 8]),
                                 iota8[:, :].unsqueeze(2).broadcast_to([P, 8, 8]), ALU.is_le))
            ch(dve.tensor_reduce(head_of[:, :], ident[:, :].rearrange("p (h d) -> p h d", d=DK), AX, ALU.max))
            ch(dve.tensor_reduce(quad_of[:, :], ident[:, :].rearrange("p (a j) -> p a j", j=QW)[:, :, 0:KR], AX, ALU.max))
            ch(dve.tensor_tensor(m16[:, :], ident[0:32, 0:H], ident[0:32, H:2 * H], ALU.add))
            ch(dve.tensor_copy(esel[:, :, :], ident[0:32, 0:QW].unsqueeze(1).broadcast_to([32, 4, QW])))
            ch.settle()
            ch(dve.tensor_copy(msel[:, :, :], m16[:, :].unsqueeze(2).broadcast_to([32, H, P])))
            ch(dve.tensor_copy(mselr[:, :, :], m16[:, :].unsqueeze(2).broadcast_to([32, H, QW])))
            dve.wait_ge(S("blanks"), 1)
            dve.wait_ge(S("ld_kv"), 13 * 16)
            for b in range(B):
                for kc in range(KC):
                    ins = dve.tensor_copy(ctxR[:, b, kc, :, 0:KR], ctxT[:, b, kc, KM:SK].unsqueeze(1).broadcast_to([P, 4, KR]))
                    if (b, kc) != (B - 1, KC - 1):
                        ch(ins)
            ins.then_inc(S("ctx_rep"), 1)
            dve.wait_ge(S("ld_x0"), 16)
            layernorm("a0", 0, xln)
            dve.wait_ge(S("kv_ps"), 1)
            for b in range(B):
                for oc in range(KC):
                    kp, bk = ps[:, 2 * b + oc, 0:SK], bcol["bk"][:, oc:oc + 1]
                    ch(dve.tensor_scalar(k_tmp[:, 0, :], kp, bk, None, ALU.add))
                    ch.settle()
                    ch(dve.scalar_tensor_tensor(k_tmp[:, 1, :], kp, bk, k_tmp[:, 0, :], ALU.add, ALU.subtract))
                    ch.settle()
                    hs = slice(8 * oc, 8 * oc + 8)
                    for i in range(2):
                        ch(dve.tensor_tensor(k_blk[:, b, i, hs, :], k_tmp[:, i, :].unsqueeze(1).broadcast_to([P, 8, SK]),
                                             head_of[:, :].unsqueeze(2).broadcast_to([P, 8, SK]), ALU.mult))
                    ch.settle()
                    for i in range(2):
                        ch(dve.tensor_copy(k_rem[:, b, i, hs, 0:KR], k_blk[:, b, i, hs, KM:SK]))
                for rem in range(2):
                    vh = v_hl[:, :, :].rearrange("p i (h d) -> p i h d", d=DK)
                    ch(dve.tensor_tensor(v_tmp[:, :], ps[:, 4 + 2 * rem + b, 0:D], brow["bv"][:, :], ALU.add))
                    ch.settle()
                    ch(dve.tensor_copy(v_hl[:, 0, :], v_tmp[:, :]))
                    ch.settle()
                    ch(dve.tensor_tensor(v_hl[:, 1, :], v_tmp[:, :], v_hl[:, 0, :], ALU.subtract))
                    ch.settle()
                    for i, at in ((0, 0), (1, DK + 1)):
                        if not rem:
                            ch(dve.tensor_copy(v_ext[:, b, :, at:at + DK], vh[:, i, :, :]))
                            continue
                        for q in range(4):
                            ch(dve.tensor_tensor(v_rem[:, b, q, :, at:at + DK], vh[:, i, 4 * q:4 * q + 4, :],
                                                 quad_of[:, :].unsqueeze(2).broadcast_to([P, 4, DK]), ALU.mult))
                            if i == 0:
                                ch(dve.tensor_copy(v_rem[:, b, q, :, DK:DK + 1], quad_of[:, :].unsqueeze(2)))
                    ch.settle()
            dve.engine_nop().then_inc(S("kv_done"), 1)
            dve.wait_ge(S("kv_ps"), 2)
            for b in range(B):
                for oc in range(KC):
                    ch(dve.tensor_scalar(k1T[:, b, oc, :], ps[:, 2 * b + oc, 0:SK], bcol["Bk"][:, oc:oc + 1], None, ALU.add))
                ch(dve.tensor_tensor(v1m[:, b, :], ps[:, 4 + b, 0:D], brow["Bv"][:, :], ALU.add))
                ins = dve.tensor_tensor(v1r[0:KR, b, :], ps[0:KR, 6 + b, 0:D], brow["Bv"][0:KR, :], ALU.add)
                if b < B - 1:
                    ch(ins)
            ins.then_inc(S("kv_done"), 1)

            def q_low(g):
                for oc in range(KC):
                    dve.wait_ge(S("a0_qhi"), 2 * g + oc + 1)
                    dve.scalar_tensor_tensor(q_lo[:, oc, :], ps[:, 2 + oc, :], bcol["bq"][:, oc:oc + 1], q_hi[:, oc, :],
                                             ALU.add, ALU.subtract).then_inc(S("a0_qlo"), 1)

            def maxima(g):
                for n in range(12):
                    t, h0, at = n // 3, (n % 3) * 6, 2 * (n % 2)
                    dve.wait_ge(S("a0_s_ps"), 12 * g + n + 1)
                    if n % 3 < 2:
                        v = ps[:, at:at + 2, 0:3 * SK].rearrange("p b (h s) -> p b h s", s=SK)
                        dve.tensor_reduce(mx[:, t, h0:h0 + 6].rearrange("p (b h) -> p b h", b=2), v, AX, ALU.max).then_inc(S("a0_mx"), 1)
                    else:
                        ch(dve.tensor_reduce(mx[:, t, h0:h0 + 3], ps[:, at, 0:3 * SK].rearrange("p (h s) -> p h s", s=SK), AX, ALU.max))
                        dve.tensor_reduce(mx[:, t, h0 + 3:h0 + 4], ps[:, at + 1, 0:SK].unsqueeze(1), AX, ALU.max).then_inc(S("a0_mx"), 1)
                dve.wait_ge(S("a0_mx"), 12 * (g + 1))
                ch(dve.tensor_scalar(nm[:, :, 0:H], mx[:, :, :], -1.0, None, ALU.mult))
                ch.settle()
                dve.scalar_tensor_tensor(nm[:, :, H:2 * H], mx[:, :, :], -1.0, nm[:, :, 0:H], ALU.mult, ALU.subtract).then_inc(S("a0_nm"), 1)

            def rows_to_send(l, g):
                if g:
                    dve.wait_ge(S(l.r + "_scattered"), 16 * GT * TOP * g)
                dve.wait_ge(S(l.r + "_ln"), g + 1)
                o = xp[:, :, :]
                ch(dve.tensor_copy(o[:, :, 0:D], xlr[:, :, :]))
                ch.settle()
                dve.tensor_tensor(o[:, :, D:2 * D], xlr[:, :, :], o[:, :, 0:D], ALU.subtract).then_inc(S(l.r + "_xp"), 1)

            def choose(l, g):
                r = l.r
                tg = slice(g * GT, (g + 1) * GT)
                dve.wait_ge(S(r + "_lg_ps"), g + 1)
                dve.tensor_copy(lg[:, :, :].rearrange("p t e -> p (t e)"), ps[:, 2, 0:GT * E]).then_inc(S(r + "_lg"), 1)
                dve.wait_ge(S(r + "_lg"), g + 1)
                for t in range(GT):
                    ch(dve.max(mx8[:, t, :], lg[:, t, :]))
                ch.settle()
                for t in range(GT):
                    ch(dve.max_index(ix8[:, t, :], mx8[:, t, :], lg[:, t, :]))
                dve.tensor_tensor(dv[:, :], mx8[:, :, 1], mx8[:, :, 0], ALU.subtract).then_inc(S(r + "_d"), 1)
                ch.settle()
                ch(dve.tensor_copy(idxf[:, tg, :], ix8[:, :, 0:TOP]))
                ch.settle()
                for t in range(g * GT, (g + 1) * GT):
                    ch(dve.tensor_tensor(oh[:, t, :, :], iota8[:, :].unsqueeze(1).broadcast_to([P, TOP, E]),
                                         idxf[:, t, :].unsqueeze(2).broadcast_to([P, TOP, E]), ALU.is_equal))
                ch.settle()
                ch(dve.tensor_tensor(sel[:, :, :], oh[:, tg, 0, :], oh[:, tg, 1, :], ALU.add))
                if g == 0:
                    ch(dve.memset(cum[:, 0, :], 0.0))
                else:
                    ch(dve.tensor_copy(cum[:, 0, :], cum[:, GT, :]))
                ch.settle()
                ch(dve.tensor_copy(selb[:, :, :], sel[:, :, :]))
                for t in range(GT):
                    ch(dve.tensor_tensor(cum[:, t + 1, :], cum[:, t, :], sel[:, t, :], ALU.add))
                    ch.settle()
                dve.tensor_copy(cumb[:, :, :], cum[:, :, :]).then_inc(S(r + "_sel"), 1)

            def place(l, g):
                r = l.r
                tg = slice(g * GT, (g + 1) * GT)
                dve.wait_ge(S(r + "_pos_ps"), g + 1)
                pos = ps[:, 3, 0:GT * E].rearrange("p (t e) -> p t e", e=E)
                for k in range(TOP):
                    ch(dve.tensor_tensor(ohp[:, tg, k, :], oh[:, tg, k, :], pos, ALU.mult))
                ch.settle()
                ch(dve.tensor_reduce(posk[:, :, :], ohp[:, tg, :, :], AX, ALU.add))
                dve.wait_ge(S(r + "_e"), g + 1)
                ch(dve.tensor_scalar(dn[:, :], ev[:, :], 1.0, None, ALU.add))
                ch.settle()
                ch(dve.reciprocal(weight[:, tg, 0], dn[:, :]))
                ch(dve.tensor_scalar(drop[:, :, :], posk[:, :, :], float(l.cap), None, ALU.is_ge))
                ch(dve.tensor_scalar(pos_kept[:, tg, :], posk[:, :, :], float(l.cap - 1), None, ALU.min))
                ch(dve.scalar_tensor_tensor(slotf[:, tg, :], idxf[:, tg, :], float(REGION), posk[:, :, :], ALU.mult, ALU.add))
                ch.settle()
                ch(dve.tensor_tensor(weight[:, tg, 1], weight[:, tg, 0], ev[:, :], ALU.mult))
                ch.settle()
                ch(dve.tensor_scalar(posk[:, :, :], drop[:, :, :], -1.0, 1.0, ALU.mult, ALU.add))
                ch.settle()
                ch(dve.tensor_tensor(weight[:, tg, :], weight[:, tg, :], posk[:, :, :], ALU.mult))
                dve.scalar_tensor_tensor(slot_s[:, tg, :], drop[:, :, :], float(FAR), slotf[:, tg, :], ALU.mult, ALU.add).then_inc(S(r + "_slot"), 1)

            def count(l):
                r, tb = l.r, table[l.n]
                ch(dve.memset(tb[:, :], 0))
                dve.wait_ge(S(r + "_cnt_ps"), 1)
                ch(dve.tensor_scalar(cnt[:, :], ps[:, 3, 0:E], float(l.cap), None, ALU.min))
                ch.settle()
                ch(dve.tensor_tensor(over[:, :, :], cnt[:, :].unsqueeze(2).broadcast_to([P, E, 7]),
                                     thr[:, :].unsqueeze(1).broadcast_to([P, E, 7]), ALU.is_gt))
                ch.settle()
                ch(dve.tensor_reduce(nblk[:, :], over[:, :, :], AX, ALU.add))
                ch.settle()
                ch(dve.tensor_scalar(nblk[:, :], nblk[:, :], 1.0, None, ALU.add))
                ch.settle()
                ch(dve.tensor_tensor(lem[:, :, :], le[:, :, :], nblk[:, :].unsqueeze(1).broadcast_to([P, E, E]), ALU.mult))
                ch.settle()
                ch(dve.tensor_reduce(blk_end[:, :], lem[:, :, :], AX, ALU.add))
                ch.settle()
                be = blk_end[0:1, :]
                ch(dve.tensor_copy(tb[0:1, 1:9], be))
                ch(dve.tensor_tensor(passed[:, :, :], iota[0:1, :].unsqueeze(2).broadcast_to([1, AHEAD, E]),
                                     be.unsqueeze(1).broadcast_to([1, AHEAD, E]), ALU.is_ge))
                ch(dve.tensor_scalar(skipped[:, :], nblk[0:1, :], float(-BLK), float(REGION), ALU.mult, ALU.add))
                ch(dve.tensor_scalar(in_use[:, :], iota[0:1, :], blk_end[0:1, 7:8], None, ALU.is_lt))
                ch(dve.scalar_tensor_tensor(tb[0:1, TB_PAD:TB_PAD + E], iota8[0:1, :], float(REGION), cnt[0:1, :], ALU.mult, ALU.add))
                ch.settle()
                ch(dve.tensor_tensor(passed[:, :, :], passed[:, :, :], skipped[:, :].unsqueeze(1).broadcast_to([1, AHEAD, E]), ALU.mult))
                ch.settle()
                ch(dve.tensor_reduce(row_of[:, :], passed[:, :, :], AX, ALU.add))
                ch.settle()
                ch(dve.scalar_tensor_tensor(row_of[:, :], iota[0:1, :], float(BLK), row_of[:, :], ALU.mult, ALU.add))
                ch.settle()
                dve.tensor_tensor(tb[0:1, TB_ROW:TB_ROW + AHEAD], row_of[:, :], in_use[:, :], ALU.mult).then_inc(S(r + "_table"), 1)
                ch(dve.tensor_tensor(blk_row[:, :], blk_end[:, :], nblk[:, :], ALU.subtract))
                ch.settle()
                for k in range(TOP):
                    ch(dve.tensor_tensor(ohp[:, :, k, :], oh[:, :, k, :], blk_row[:, :].unsqueeze(1).broadcast_to([P, NT, E]), ALU.mult))
                ch.settle()
                ch(dve.tensor_reduce(slotf[:, :, :], ohp[:, :, :, :], AX, ALU.add))
                ch.settle()
                dve.scalar_tensor_tensor(slot_g[:, :, :], slotf[:, :, :], float(BLK), pos_kept[:, :, :], ALU.mult, ALU.add).then_inc(S(r + "_slotg"), 1)

            q_low(0)
            maxima(0)
            for g in range(NG):
                if g + 1 < NG:
                    dve.wait_ge(S(f"ld_x{g + 1}"), 16)
                    layernorm("a0", g + 1, xln)
                for u in range(20):
                    dve.wait_ge(S("a0_phi"), 20 * g + u + 1)
                    dve.tensor_tensor(p_lo[:, u, :], e_ring[:, u % 4, :], p_hi[:, u, :], ALU.subtract).then_inc(S("a0_plo"), 1)
                if g:
                    choose(L[0], g - 1)
                if g + 1 < NG:
                    q_low(g + 1)
                    maxima(g + 1)
                if g:
                    place(L[0], g - 1)
                for t in range(GT + 2):
                    if t < GT:
                        n = 4 * g + t
                        at = 6 - 2 * (t % 2)
                        o = ps[:, at:at + 2, 0:8 * VW].rearrange("p b (h v) -> p b h v", v=VW)
                        dve.wait_ge(S("a0_olo"), n + 1)
                        if n:
                            dve.wait_ge(S("a0_on"), n)
                        ch(dve.tensor_tensor(o_sum[:, :, :, :], o[:, :, :, 0:DK], o_lo[:, :, :, :], ALU.add))
                        dve.reciprocal(rden[:, :, :], o[:, :, :, DK]).then_inc(S("a0_oev"), 1)
                        dve.wait_ge(S("a0_oev"), n + 1)
                        if n >= 2:
                            dve.wait_ge(S("a0_oT_ps"), n - 1)
                        on = o_n[:, t % 2, :].rearrange("p (h d) -> p h d", d=DK)
                        dve.tensor_tensor(on, o_sum[:, :, :, :].rearrange("p b h d -> p (b h) d"),
                                          rden[:, :, :].rearrange("p b h -> p (b h)").unsqueeze(2).broadcast_to([P, H, DK]), ALU.mult).then_inc(S("a0_on"), 1)
                    if t >= 2:
                        n = 4 * g + t - 2
                        dve.wait_ge(S("a0_op_ps"), n + 1)
                        if n:
                            dve.wait_ge(S("a0_x"), n)
                        ch(dve.tensor_tensor(xo[:, :], ps[:, 2 + t % 2, 0:D], brow["bo"][:, :], ALU.add))
                        ch.settle()
                        dve.tensor_tensor(x[:, n, :], x[:, n, :], xo[:, :], ALU.add).then_inc(S("a0_x"), 1)
                dve.wait_ge(S("a0_x"), 4 * (g + 1))
                if g:
                    dve.wait_ge(S("r0_xT_ps"), g)
                layernorm("r0", g, xlr)
                rows_to_send(L[0], g)
            choose(L[0], NG - 1)
            place(L[0], NG - 1)
            count(L[0])

            def experts(l):
                r, pairs = l.r, l.pairs
                dve.wait_ge(S(r + "_table"), 1)
                total = dve.value_load(table[l.n][0:1, 8:9], min_val=1, max_val=MAXBLK)
                dve.sem_inc(S(r + "_h"), 1)
                dve.sem_inc(S(r + "_h32"), 2)

                def turned(g):
                    dve.wait_ge(S(r + "_xbT_ps"), g + 2)
                    dve.tensor_copy(xbT[:, :, :, :].rearrange("p a b c -> p (a b c)"), psh[:, 6, :]).then_inc(S(r + "_xbT"), 1)

                turned(0)
                with dve.Fori(0, total) as g:
                    dve.wait_ge(S(r + "_down"), g + 1)
                    for j in range(pairs):
                        n = g * pairs + j
                        hh = h_hi[:, 2 * j:2 * j + 2, :].rearrange("p c t -> p (c t)")
                        hl = h_lo[:, 2 * j:2 * j + 2, :].rearrange("p c t -> p (c t)")
                        dve.wait_ge(S(r + "_s"), n + 1)
                        dve.wait_ge(S(r + "_gu_ps"), n * 2 + 2)
                        dve.wait_ge(S(r + "_h"), n + 1)
                        dve.tensor_tensor(h32[:, j % 2, :], s_act[:, j % 2, :], ps[:, 2 * (j % 2) + 1, :], ALU.mult).then_inc(S(r + "_h32"), 1)
                        dve.wait_ge(S(r + "_h32"), n + 3)
                        dve.tensor_copy(hh, h32[:, j % 2, :]).then_inc(S(r + "_hh"), 1)
                        dve.wait_ge(S(r + "_hh"), n + 1)
                        dve.tensor_tensor(hl, h32[:, j % 2, :], hh, ALU.subtract).then_inc(S(r + "_h"), 1)
                    turned(g + 1)

            def combine(l, t):
                r = l.r
                dve.wait_ge(S(f"{r}_gathered{t % GT}"), 32 * (t // GT + 1))
                ch(dve.scalar_tensor_tensor(x[:, t, :], gb[:, t % GT, 0, :], weight[:, t, 0:1], x[:, t, :], ALU.mult, ALU.add))
                ch.settle()
                dve.scalar_tensor_tensor(x[:, t, :], gb[:, t % GT, 1, :], weight[:, t, 1:2], x[:, t, :], ALU.mult, ALU.add).then_inc(S(r + "_x"), 1)

            experts(L[0])

            def combine_group(g):
                for t in range(g * GT, (g + 1) * GT):
                    combine(L[0], t)
                dve.wait_ge(S("r0_x"), GT * (g + 1))
                layernorm("a1", g, xln)

            combine_group(0)
            dve.wait_ge(S("phi_set"), 1)
            for g in range(NG):
                dve.wait_ge(S("a1_s_ps"), g + 1)
                for j in range(2):
                    ch(dve.scalar_tensor_tensor(att[:, 2 * j:2 * j + 2, :], ps[:, 4 + j, 0:2 * SK].rearrange("p (t s) -> p t s", s=SK), float(D) ** -0.5,
                                                phi[:, g * GT + 2 * j:g * GT + 2 * j + 2, :], ALU.mult, ALU.add))
                ch.settle()
                ch(dve.tensor_reduce(mx1[:, :], att[:, :, :], AX, ALU.max))
                ch.settle()
                dve.tensor_scalar(mx1[:, :], mx1[:, :], -1.0, None, ALU.mult).then_inc(S("a1_nm"), 1)
                if g:
                    rows_to_send(L[1], g - 1)
                if g + 1 < NG:
                    combine_group(g + 1)
                if g:
                    choose(L[1], g - 1)
                dve.wait_ge(S("a1_p"), GT * (g + 1))
                ch(dve.reciprocal(rd1[:, :], den1[:, :]))
                ch.settle()
                dve.wait_ge(S("a1_o_ps"), g + 1)
                for t in range(GT):
                    n = g * GT + t
                    dve.scalar_tensor_tensor(x[:, n, :], ps[:, t // 2, (t % 2) * D:(t % 2 + 1) * D], rd1[:, t:t + 1], x[:, n, :],
                                             ALU.mult, ALU.add).then_inc(S("a1_x"), 1)
                dve.wait_ge(S("a1_x"), GT * (g + 1))
                if g:
                    dve.wait_ge(S("r1_xT_ps"), g)
                layernorm("r1", g, xlr)
                if g:
                    place(L[1], g - 1)
            rows_to_send(L[1], NG - 1)
            choose(L[1], NG - 1)
            place(L[1], NG - 1)
            count(L[1])
            experts(L[1])
            for t in range(NT):
                combine(L[1], t)


def kernel(**inputs):
    import numpy as np
    import concourse.bacc as bacc
    from concourse.bass_utils import run_bass_kernel_spmd

    i = {k: np.asarray(v) for k, v in inputs.items()}

    def by_row_chunk(w):
        e, r, c = w.shape
        return w.reshape(e, r // P, P, c).transpose(0, 2, 1, 3).reshape(e, P, -1)

    def column(b):
        return b.reshape(KC, P).T

    laid = {
        "x": i["x"].reshape(N, D),
        "ctxT": i["ctx_1024"].transpose(0, 2, 1),
        "mask": i["mask_BxSxS2_ik0"].reshape(N, SK),
        "maskT": i["mask_BxSxS2_ik0"].transpose(0, 2, 1),
        "phi": i["fside_BxSxS2_0"].reshape(N, SK),
        "wq": i["L0_xattn_wq"], "wk": i["L0_xattn_wk"], "wv": i["L0_xattn_wv"], "wo": i["L0_xattn_wo"],
        "bq": column(i["L0_xattn_bq"]), "bk": column(i["L0_xattn_bk"]), "bv": i["L0_xattn_bv"], "bo": i["L0_xattn_bo"],
        "Wq": i["L1_xattn_Wq"].T, "Wk": i["L1_xattn_Wk"].T, "Wv": i["L1_xattn_Wv"].T,
        "Bq": column(i["L1_xattn_bq"]), "Bk": column(i["L1_xattn_bk"]), "Bv": i["L1_xattn_bv"],
        "betas": np.stack([i["L1_xattn_beta_risk"].reshape(1), i["L1_xattn_beta_prio"].reshape(1), i["L1_xattn_beta_impl"].reshape(1)]),
        "gate0": i["L0_ffn_gate_w"].T, "gate1": i["L1_ffn_Wg"].T,
        "wg": by_row_chunk(i["L0_ffn_wg"].transpose(0, 2, 1)),
        "wu": by_row_chunk(i["L0_ffn_wu"].transpose(0, 2, 1)),
        "wd": by_row_chunk(i["L0_ffn_wd"].transpose(0, 2, 1)),
        "W1": by_row_chunk(i["L1_ffn_W1"]),
        "W2": by_row_chunk(i["L1_ffn_W2"]),
    }
    nc = bacc.Bacc("TRN2", target_bir_lowering=False, num_devices=1)
    arrays, a = {}, {}
    for name, v in laid.items():
        v = np.ascontiguousarray(v)
        arrays["in_" + name] = v
        a[name] = nc.dram_tensor("in_" + name, v.shape, mybir.dt.from_np(v.dtype), kind="ExternalInput").ap()
    out = nc.dram_tensor("out_x", (N, D), F32, kind="ExternalOutput").ap()
    two_layers(nc, a, out)
    r = run_bass_kernel_spmd(nc, [arrays], core_ids=[0])
    return r.results[0]["out_x"].reshape(i["x"].shape)
```

```python
from contextlib import ExitStack

import concourse.bass as bass
from concourse import mybir

ALU = mybir.AluOpType
ACT = mybir.ActivationFunctionType
AX = mybir.AxisListType.X
F32, F16, BF16 = mybir.dt.float32, mybir.dt.float16, mybir.dt.bfloat16
I32, U32 = mybir.dt.int32, mybir.dt.uint32

P = 128
D = 256
KC = D // P
H = 16
DK = D // H
B = 2
E = 8
TOP = 2
N = 2048
NT = N // P
GT = 4
NG = NT // GT
GW = GT * P
SK = 154
KM = P
KR = SK - KM
QW = 32
VW = 2 * DK + 1
PENALTY = -1e30
BLK = 256
REGION = N + BLK
MAXBLK = N * TOP // BLK + E
AHEAD = MAXBLK + 2
TB_ROW, TB_PAD = 16, 48
TB_PACKED = 64
PACK = 32
CH = 1024
STAGES = 3
FAR = 1 << 20
EPS = 1e-5


class Chain:

    def __init__(self, eng, sem):
        self.eng, self.sem, self.n = eng, sem, 0

    def __call__(self, ins):
        self.n += 1
        ins.then_inc(self.sem, 1)

    def settle(self):
        self.eng.wait_ge(self.sem, self.n)


def two_layers(nc, a, out):
    with ExitStack() as ctx:
        def sb(name, shape, dt=F32):
            return ctx.enter_context(nc.sbuf_tensor(name, shape, dt))

        sems = {}

        def S(name):
            if name not in sems:
                sems[name] = ctx.enter_context(nc.semaphore(name))
            return sems[name]

        ps = ctx.enter_context(nc.psum_tensor("ps", [P, 8, 512], F32))
        psh = ps[:, :, :].bitcast(F16)
        psb = ps[:, :, :].bitcast(BF16)

        rows = nc.dram_tensor("rows", (E * REGION, 2 * D), F16, kind="Internal").ap()
        results = nc.dram_tensor("results", (MAXBLK * BLK, D), F32, kind="Internal").ap()

        WS = 6144
        probs = sb("probs", [P, 2 * 20 * GW], F16)
        keys = sb("keys", [P, B * 2 * H * SK], F16)
        expo = sb("expo", [P, 2 * 4 * GW], F16)
        queries = sb("queries", [P, 2 * KC * GW], F16)
        inbox = sb("inbox", [P, 2 * 2 * 1664], F16)
        heads = sb("heads", [P, 2 * 2048], F16)
        def part(arena, at, shape, dt=F32, rows=P):
            size = 1
            for n in shape[1:]:
                size *= n
            width = size * (1 if dt in (F16, BF16) else 2)
            v = arena[0:rows, at:at + width]
            if dt != F16:
                v = v.bitcast(dt)
            if len(shape) > 2:
                names = "abcdef"[:len(shape) - 1]
                v = v.rearrange("p (" + " ".join(names) + ") -> p " + " ".join(names), **dict(zip(names[1:], shape[2:])))
            return v, at + width

        ident = sb("ident", [P, P])
        identb = sb("identb", [P, P], BF16)
        identh = sb("identh", [P, P], F16)
        earlier = sb("earlier", [P, P], BF16)
        onesb = sb("onesb", [P, P], BF16)
        iota_i = sb("iota_i", [P, AHEAD], I32)
        iota = sb("iota", [P, AHEAD])
        iota8 = iota[:, 0:8]
        head_of = sb("head_of", [P, 8], F16)
        quad_of = sb("quad_of", [P, 4], F16)
        m16 = sb("m16", [32, H], BF16)
        msel = sb("msel", [32, H, P], BF16)
        mselr = sb("mselr", [32, H, QW], BF16)
        esel = sb("esel", [32, 4, QW], BF16)
        zeros = sb("zeros", [P, 512])
        thr = sb("thr", [P, 7])
        le = sb("le", [P, 8, 8])

        x = sb("x", [P, NT, D])
        ctxT, at = part(probs, 0, [P, B, KC, SK])
        ctxR, at = part(probs, at, [P, B, KC, 4, QW])
        w_sb = {n: sb("w_" + n, [P, KC, D]) for n in ("wq", "wo", "Wq")}
        for n in ("wk", "wv", "Wk", "Wv"):
            w_sb[n], at = part(probs, at, [P, KC, D])
        v_tmp, at = part(probs, at, [P, D])
        v_hl, at = part(probs, at, [P, 2, D], F16)
        k_parts = [part(probs, at, [P, KC, 2, SK], F16)[0], part(heads, 0, [P, KC, 2, SK], F16)[0]]
        bcol = {n: sb("b_" + n, [P, KC]) for n in ("bq", "bk", "Bq", "Bk")}
        brow = {n: sb("b_" + n, [P, D]) for n in ("bv", "bo", "Bv")}
        gate = [sb("gate0", [P, KC, E]), sb("gate1", [P, KC, E])]
        betas = sb("betas", [P, 4])
        phi, keys_at = part(keys, 0, [P, NT, SK])

        mask_raw, at = part(inbox, 0, [P, GT, SK], I32)
        maskT_raw, at = part(inbox, at, [P, GW], I32)
        maskR_raw, at = part(inbox, at, [QW, GW], I32, rows=QW)
        penalties = sb("penalties", [P, NT * SK], F16)
        pen, _ = part(penalties, 0, [P, NT, SK], BF16)
        penT = sb("penT", [P, NG, GW], BF16)
        penR = sb("penR", [QW, NG, GW], BF16)

        k_blk, _ = part(keys, 0, [P, B, 2, H, SK], F16)
        k_rem = sb("k_rem", [P, B, 2, H, QW], F16)
        v_ext = sb("v_ext", [P, B, H, VW], F16)
        v_rem = sb("v_rem", [P, B, 4, 4, VW], F16)
        k1T = sb("k1T", [P, B, KC, SK])
        v1m = sb("v1m", [P, B, D])
        v1r = sb("v1r", [QW, B, D])

        stats = sb("stats", [P, GT, 6])
        mv = {c: sb("mv_" + c, [P, GT, 2]) for c in ("a0", "r0", "a1", "r1")}
        ve = sb("ve", [P, GT])
        ry = {c: sb("ry_" + c, [P, GT]) for c in ("a0", "r0", "a1", "r1")}
        rt = sb("rt", [P, GT])
        xln = sb("xln", [P, GT, D])
        xlr = sb("xlr", [P, GT, D])
        xT = sb("xT", [P, KC, GW])
        xTr = sb("xTr", [P, KC, GW])
        q_hi, at = part(queries, 0, [P, KC, GW], F16)
        q_lo, at = part(queries, at, [P, KC, GW], F16)
        mx = sb("mx", [P, GT, H])
        nm = sb("nm", [P, GT, 2 * H], BF16)
        nmT = sb("nmT", [2 * H, GW], BF16)
        e_ring, _ = part(expo, 0, [P, 4, GW])
        p_hi, at = part(probs, 0, [P, 20, GW], F16)
        p_lo, _ = part(probs, at, [P, 20, GW], F16)
        o_lo, at = part(heads, 0, [P, 2, 8, DK])
        o_sum, at = part(heads, at, [P, 2, 8, DK])
        o_n, at = part(heads, at, [P, GT, D])
        rden = sb("rden", [P, 2, 8])
        xo, at = part(heads, at, [P, D])
        oT, _ = part(expo, 0, [P, 2, D])

        att, at = part(expo, 0, [P, GT, SK])
        pT, at = part(expo, at, [P, GW])
        pTr, at = part(expo, at, [QW, GW], rows=QW)
        mx1 = sb("mx1", [P, GT])
        den1 = sb("den1", [P, GT])
        rd1 = sb("rd1", [P, GT])
        q1T, _ = part(queries, 0, [P, KC, GW])
        passed, at = part(queries, 0, [1, AHEAD, E], rows=1)
        skipped, at = part(queries, at, [1, E], rows=1)
        row_of, at = part(queries, at, [1, AHEAD], rows=1)
        in_use, at = part(queries, at, [1, AHEAD], rows=1)
        first_block, at = part(queries, at, [1, E], rows=1)
        room, at = part(queries, at, [1, E], rows=1)

        xp = sb("xp", [P, GT, 2 * D], F16)
        xps = [xp, part(penalties, 0, [P, GT, 2 * D], F16)[0]]
        lg = sb("lg", [P, GT, E])
        mx8 = sb("mx8", [P, GT, 8])
        ix8 = sb("ix8", [P, GT, 8], U32)
        dv = sb("dv", [P, GT])
        ev = sb("ev", [P, GT])
        dn = sb("dn", [P, GT])
        sel = sb("sel", [P, GT, E])
        selb = sb("selb", [P, GT, E], BF16)
        cum = sb("cum", [P, GT + 1, E])
        cumb = sb("cumb", [P, GT + 1, E], BF16)
        ohp = sb("ohp", [P, NT, TOP, E])
        posk = sb("posk", [P, GT, TOP])
        drop = sb("drop", [P, GT, TOP])
        slotf = sb("slotf", [P, NT, TOP])
        idxf = sb("idxf", [P, NT, TOP])
        oh = sb("oh", [P, NT, TOP, E])
        pos_kept = sb("pos_kept", [P, NT, TOP])
        weight = sb("weight", [P, NT, TOP])
        slot_s = sb("slot_s", [P, NT, TOP], I32)
        slot_g = sb("slot_g", [P, NT, TOP], I32)
        cnt = sb("cnt", [P, E])
        over = sb("over", [P, E, 7])
        nblk = sb("nblk", [P, E])
        lem = sb("lem", [P, E, E])
        blk_end = sb("blk_end", [P, E])
        blk_row = sb("blk_row", [P, E])
        table = [sb("table0", [1, 96], I32), sb("table1", [1, 96], I32)]

        stage, _ = part(inbox, 0, [P, STAGES, CH])
        slot0 = sb("slot0", [P, 2, WS], F16)
        slot1, at = part(probs, 0, [P, 2, WS], F16)
        w_hl = [slot0, slot1]
        h_hi, at = part(probs, at, [P, 8, BLK], F16)
        h_lo, at = part(probs, at, [P, 8, BLK], F16)
        s_act, at = part(probs, at, [P, 2, 2 * BLK])
        x_raw, at = part(probs, at, [P, 2, 2 * D], F16)
        h32, keys_at = part(keys, keys_at, [P, 2, 2 * BLK])
        xbT, keys_at = part(keys, keys_at, [P, 2, KC, BLK], F16)
        yb, keys_at = part(keys, keys_at, [P, 2, D])
        gb, _ = part(heads, 0, [P, GT, TOP, D])

        class Layer:
            pass

        L = [Layer(), Layer()]
        for n, l in enumerate(L):
            l.n, l.r = n, f"r{n}"
            l.I = (1024, 512)[n]
            l.bank = (6, 2)[n]
            l.hc = l.I // P
            l.pairs = l.hc // 2
            l.cap = (N, N * TOP * 5 // 4 // E)[n]
            l.act = (ACT.Silu, ACT.Gelu)[n]
            l.gate_col = lambda kc, c, n=n: (kc * 1024 + c * P)
            l.up_col = lambda kc, c, n=n: ((2048, 512)[n] + kc * 1024 + c * P)
            l.down_at = (4096, 2048)[n]
            l.beside = (([0], [1], [2], [3], [4, 5]), ([0], [1, 2], []))[n]
        L[0].chunks = [(a[w], 1024 * i, 2048 * n + 1024 * i) for n, w in enumerate(("wg", "wu", "wd")) for i in range(2)]
        L[1].chunks = [(a["W1"], 0, 0), (a["W1"], 1024, 1024), (a["W2"], 0, 2048)]

        def wait_counted(eng, sem, value):
            eng.wait_ge(sem, value)
            eng.sem_inc(S("counted"), 1)

        block = ctx.enter_context(nc.Block())

        @block.sync
        def _(sp):
            for b in range(B):
                sp.dma_start(ctxT[:, b], a["ctxT"][b].rearrange("(k p) s -> p k s", p=P)).then_inc(S("ld_kv"), 16)
            for n in ("wk", "wv", "Wk", "Wv"):
                sp.dma_start(w_sb[n][:, :, :], a[n].rearrange("(k p) n -> p k n", p=P)).then_inc(S("ld_kv"), 16)
            for n in ("bq", "bk", "Bq", "Bk"):
                sp.dma_start(bcol[n][:, :], a[n]).then_inc(S("ld_kv"), 16)
            for n in ("bv", "bo", "Bv"):
                sp.dma_start(brow[n][:, :], a[n].unsqueeze(0).broadcast_to([P, D])).then_inc(S("ld_kv"), 16)
            for g in range(NG):
                sp.dma_start(x[:, g * GT:(g + 1) * GT, :],
                             a["x"][g * GW:(g + 1) * GW, :].rearrange("(t p) d -> p t d", p=P)).then_inc(S(f"ld_x{g}"), 16)
                if g == 0:
                    for n in ("wq", "wo", "Wq"):
                        sp.dma_start(w_sb[n][:, :, :], a[n].rearrange("(k p) n -> p k n", p=P)).then_inc(S("ld_w"), 16)
                    for n in range(2):
                        sp.dma_start(gate[n][:, :, :], a[f"gate{n}"].rearrange("(k p) e -> p k e", p=P)).then_inc(S("ld_w"), 16)
            for g in range(NG):
                if g:
                    sp.wait_ge(S("mask_used"), 3 * g)
                b, q0 = g // 2, (g % 2) * GW
                sp.dma_start(mask_raw[:, :, :], a["mask"][g * GW:(g + 1) * GW, :].rearrange("(t p) s -> p t s", p=P)).then_inc(S("ld_mask"), 16)
                sp.dma_start(maskT_raw[:, :], a["maskT"][b, 0:KM, q0:q0 + GW]).then_inc(S("ld_mask"), 16)
                sp.dma_start(maskR_raw[0:KR, :], a["maskT"][b, KM:SK, q0:q0 + GW]).then_inc(S("ld_mask"), 16)
            for n in range(3):
                sp.dma_start(betas[:, n:n + 1], a["betas"][n].unsqueeze(0).broadcast_to([P, 1])).then_inc(S("ld_phi"), 16)
            sp.wait_ge(S("zeros_set"), 1)
            yz = results.rearrange("(n p r s) d -> n p r (s d)", p=P, r=4, s=2)
            for n in range(MAXBLK * BLK // (P * 8)):
                sp.dma_start(yz[n], zeros[:, :].unsqueeze(1).broadcast_to([P, 4, 512])).then_inc(S("results_zero"), 16)

            def fetch(l, e, n):
                src, col, _ = l.chunks[n]
                k = len(l.chunks)
                if isinstance(e, int):
                    if e * k + n >= STAGES:
                        sp.wait_ge(S(f"w_ready{l.n}"), e * k + n - STAGES + 1)
                    w = src[e]
                else:
                    sp.wait_ge(S(f"w_ready{l.n}"), e * k + n - STAGES + 1)
                    w = src[bass.ds(e, 1), :, :].rearrange("e p n -> (e p) n")
                sp.dma_start(stage[:, n % STAGES, :], w[:, col:col + CH]).then_inc(S(f"staged{l.n}_{n}"), 16)

            def clear_padding(l):
                def clear(e, signal):
                    row = sp.value_load(table[l.n][0:1, bass.ds(e + TB_PAD, 1)], min_val=0, max_val=E * REGION - BLK)
                    sp.dma_start(rows[bass.ds(row, BLK), :].rearrange("(p s) d -> p (s d)", p=P),
                                 zeros[:, :].bitcast(F16)).then_inc(S(signal), 16)

                sp.wait_ge(S(l.r + "_table"), 1)
                clear(0, l.r + "_padded_first")
                with sp.Fori(1, E) as e:
                    clear(e, l.r + "_padded")

            sp.wait_ge(S("mask_used"), 3 * NG)
            k0 = len(L[0].chunks)
            for n in range(k0 + STAGES):
                fetch(L[0], n // k0, n % k0)
            sp.wait_ge(S("a0_st"), 20 * NG)
            sp.dma_start(phi[:, :, :], a["phi"].rearrange("(t p) s -> p t s", p=P)).then_inc(S("ld_phi"), 16)
            clear_padding(L[0])
            for n in range(STAGES, k0):
                fetch(L[0], 1, n)
            with sp.Fori(2, E) as e:
                for n in range(k0):
                    fetch(L[0], e, n)
            sp.wait_ge(S("w_ready0"), E * k0)
            for e in range(2):
                for n in range(len(L[1].chunks)):
                    fetch(L[1], e, n)
            clear_padding(L[1])
            with sp.Fori(2, E) as e:
                for n in range(len(L[1].chunks)):
                    fetch(L[1], e, n)
            for t in range(NT):
                sp.wait_ge(S("r1_x"), t + 1)
                sp.dma_start(out[t * P:(t + 1) * P, :], x[:, t, :]).then_inc(S("stored"), 16)
            sp.wait_ge(S("stored"), 16 * NT)

        @block.gpsimd
        def _(pool):
            ch = Chain(pool, S("pool_step"))
            ch(pool.memset(ident[:, :], 0.0))
            ch(pool.memset(identb[:, :], 1.0))
            ch.settle()
            ch(pool.affine_select(out=ident[:, :], in_=ident[:, :], compare_op=ALU.not_equal, fill=1.0, base=0,
                                  pattern=[[-1, P]], channel_multiplier=1))
            ch(pool.affine_select(out=earlier[:, :], in_=identb[:, :], compare_op=ALU.is_gt, fill=0.0, base=0,
                                  pattern=[[1, P]], channel_multiplier=-1))
            ch.settle()
            ch(pool.tensor_copy(identb[:, :], ident[:, :]))
            ch(pool.tensor_copy(identh[:, :], ident[:, :]))
            ch(pool.memset(onesb[:, :], 1.0))
            ch(pool.iota(iota_i[:, :], pattern=[[1, AHEAD]], base=0, channel_multiplier=0))
            ch.settle()
            ch(pool.tensor_copy(iota[:, :], iota_i[:, :]))
            ch.settle()
            ch(pool.tensor_scalar(thr[:, :], iota8[:, 1:8], float(BLK), None, ALU.mult))
            pool.memset(penR[:, :, :], PENALTY).then_inc(S("consts"), 1)
            ch(pool.memset(ctxR[:, :, :, :, :], 0.0))
            ch(pool.memset(k_rem[:, :, :, :, :], 0.0))
            ch(pool.memset(v_ext[:, :, :, :], 1.0))
            ch.settle()
            pool.memset(v_rem[:, :, :, :, :], 0.0).then_inc(S("blanks"), 1)
            pool.memset(zeros[:, :], 0.0).then_inc(S("zeros_set"), 1)

            for g in range(NG):
                pool.wait_ge(S("ld_mask"), 48 * (g + 1))
                if g == 0:
                    pool.wait_ge(S("consts"), 1)
                pool.tensor_scalar(pen[:, g * GT:(g + 1) * GT, :], mask_raw[:, :, :], 0.0, PENALTY, ALU.is_equal, ALU.mult).then_inc(S("mask_used"), 1)
                pool.tensor_scalar(penT[:, g, :], maskT_raw[:, :], 0.0, PENALTY, ALU.is_equal, ALU.mult).then_inc(S("mask_used"), 1)
                pool.tensor_scalar(penR[0:KR, g, :], maskR_raw[0:KR, :], 0.0, PENALTY, ALU.is_equal, ALU.mult).then_inc(S("mask_used"), 1)

            def low_parts(l, e, slot, chunks):
                k = len(l.chunks)
                for n in chunks:
                    at = l.chunks[n][2]
                    pool.wait_ge(S(f"w_hi{l.n}"), e * k + n + 1)
                    pool.tensor_tensor(w_hl[slot][:, 1, at:at + CH], stage[:, n % STAGES, :], w_hl[slot][:, 0, at:at + CH],
                                       ALU.subtract).then_inc(S(f"w_ready{l.n}"), 1)

            def rest_of_experts(l):
                low_parts(l, 1, 1, range(len(l.chunks)))
                with pool.Fori(1, E // 2) as pr:
                    for slot in range(2):
                        low_parts(l, pr * 2 + slot, slot, range(len(l.chunks)))

            def scatter(l, g):
                r = l.r
                pool.wait_ge(S(r + "_xp"), g + 1)
                pool.wait_ge(S(r + "_slot"), g + 1)
                for t in range(GT):
                    for k in range(TOP):
                        pool.indirect_dma_start(
                            out=rows, out_offset=bass.IndirectOffsetOnAxis(ap=slot_s[:, g * GT + t, k:k + 1], axis=0),
                            in_=xps[g % 2 if l.n else 0][:, t, :], in_offset=None, bounds_check=E * REGION - 1,
                            oob_is_err=False).then_inc(S(f"{r}_scattered{g % 2}"), 16)

            def results_stored(l):
                r = l.r
                total = pool.value_load(table[l.n][0:1, 8:9], min_val=1, max_val=MAXBLK)
                wait_counted(pool, S(r + "_stored"), total * 16 + 16)
                if l.n == 0:
                    pool.wait_ge(S("results_zero"), 16 * (MAXBLK * BLK // (P * 8)))

            def gather(l, g):
                r = l.r
                for t in range(g * GT, (g + 1) * GT):
                    if t >= GT:
                        pool.wait_ge(S(r + "_x"), t - GT + 1)
                    for k in range(TOP):
                        pool.indirect_dma_start(
                            out=gb[:, t % GT, k, :], out_offset=None, in_=results,
                            in_offset=bass.IndirectOffsetOnAxis(ap=slot_g[:, t, k:k + 1], axis=0),
                            bounds_check=MAXBLK * BLK - 1, oob_is_err=False).then_inc(S(f"{r}_gathered{t % GT}"), 16)

            def normalise(c, g, dst, roots):
                pool.wait_ge(S(c + "_root"), roots)
                for t in range(GT):
                    ins = pool.tensor_scalar(dst[:, t, :], x[:, g * GT + t, :], mv[c][:, t, 0:1], ry[c][:, t:t + 1], ALU.subtract, ALU.mult)
                    if t < GT - 1:
                        ch(ins)
                ins.then_inc(S(c + "_ln"), 1)

            def split_rows(g):
                pool.wait_ge(S("r0_ln"), g + 1)
                if g:
                    pool.wait_ge(S(f"r0_scattered{(g - 1) % 2}"), 16 * GT * TOP * ((g + 1) // 2))
                ch(pool.tensor_copy(xp[:, :, 0:D], xlr[:, :, :]))
                ch.settle()
                pool.tensor_tensor(xp[:, :, D:2 * D], xlr[:, :, :], xp[:, :, 0:D], ALU.subtract).then_inc(S("r0_xp"), 1)

            k0 = len(L[0].chunks)
            for g in range(NG):
                if g:
                    if g >= 2:
                        pool.wait_ge(S("r0_xT_ps"), g - 1)
                        pool.wait_ge(S("r0_xp"), g - 1)
                    normalise("r0", g - 1, xlr, g)
                if g + 1 < NG:
                    pool.wait_ge(S("a0_xT_ps"), g + 1)
                    normalise("a0", g + 1, xln, g + 2)
                if g:
                    split_rows(g - 1)
                if 1 <= g <= 2:
                    low_parts(L[0], 0, 0, range((g - 1) * STAGES, g * STAGES))
                if g:
                    scatter(L[0], g - 1)
            split_rows(NG - 1)
            scatter(L[0], NG - 1)
            rest_of_experts(L[0])
            pool.wait_ge(S("ld_phi"), 64)
            ch(pool.tensor_tensor(betas[:, 3:4], betas[:, 0:1], betas[:, 1:2], ALU.add))
            ch.settle()
            ch(pool.tensor_tensor(betas[:, 3:4], betas[:, 3:4], betas[:, 2:3], ALU.subtract))
            ch.settle()
            pool.tensor_scalar(phi[:, :, :], phi[:, :, :], betas[:, 3:4], None, ALU.mult).then_inc(S("phi_set"), 1)
            results_stored(L[0])
            gather(L[0], 0)
            gather(L[0], 1)
            low_parts(L[1], 0, 0, range(len(L[1].chunks)))
            gather(L[0], 2)
            gather(L[0], 3)
            for g in range(NG):
                scatter(L[1], g)
            rest_of_experts(L[1])
            results_stored(L[1])
            for g in range(NG):
                gather(L[1], g)

        @block.tensor
        def _(pe):
            def mm(o, l, r, start, stop, **kw):
                return pe.matmul(o, l, r, start=start, stop=stop, **kw)

            pe.wait_ge(S("ld_kv"), 13 * 16)
            pe.wait_ge(S("ctx_rep"), 1)
            for bank, wn in ((0, "wk"), (2, "Wk")):
                for b in range(B):
                    for oc in range(KC):
                        for kc in range(KC):
                            last = mm(ps[:, bank + b, oc * SK:(oc + 1) * SK], w_sb[wn][:, kc, oc * P:(oc + 1) * P], ctxT[:, b, kc, :], kc == 0, kc == 1)
                last.then_inc(S("kv_ps"), 1)
            for bank, wn in ((4, "wv"), (6, "Wv")):
                for b in range(B):
                    for kc in range(KC):
                        mm(ps[:, bank, b * D:(b + 1) * D], ctxT[:, b, kc, 0:KM], w_sb[wn][:, kc, :], kc == 0, kc == 1)
                    for kc in range(KC):
                        rest, rows_of = (ctxR[:, b, kc, :, :].rearrange("p a j -> p (a j)"), P) if bank == 4 else (ctxT[:, b, kc, KM:SK], KR)
                        last = mm(ps[0:rows_of, bank + 1, b * D:(b + 1) * D], rest, w_sb[wn][:, kc, :], kc == 0, kc == 1)
                last.then_inc(S("kv_ps"), 1)
            pe.wait_ge(S("ld_w"), 5 * 16)

            def turn(c, g, src, bank=0):
                pe.wait_ge(S(c + "_ln"), g + 1)
                for kc in range(KC):
                    for t in range(GT):
                        last = pe.transpose(ps[:, bank + kc, t * P:(t + 1) * P], src[:, t, kc * P:(kc + 1) * P], ident[:, :])
                last.then_inc(S(c + "_xT_ps"), 1)

            def project_q(c, g, w):
                pe.wait_ge(S(c + "_xT"), g + 1)
                for oc in range(KC):
                    for kc in range(KC):
                        last = mm(ps[:, 2 + oc, :], w[:, kc, oc * P:(oc + 1) * P], xT[:, kc, :], kc == 0, kc == 1)
                last.then_inc(S(c + "_q_ps"), 1)

            def score_max(g):
                b = g // 2
                pe.wait_ge(S("a0_qhi"), 2 * (g + 1))
                pe.wait_ge(S("mask_used"), 3 * (g + 1))
                pe.wait_ge(S("keys_set"), b + 1)
                for n in range(12):
                    t, h0 = n // 3, (n % 3) * 6
                    if n and n % 3 == 0 and g:
                        weigh_values(g - 1, n // 3)
                    if n == 1:
                        pe.wait_ge(S("a0_qlo"), 2 * (g + 1))
                    if n >= 2:
                        pe.wait_ge(S("a0_mx"), 12 * g + n - 1)
                    for j in range(2):
                        heads = range(h0 + 3 * j, min(h0 + 3 * j + 3, H))
                        o = ps[:, 2 * (n % 2) + j, 0:len(heads) * SK].rearrange("p (h s) -> p h s", s=SK)
                        mm(o, identb[:, :], pen[:, g * GT + t, :].unsqueeze(1).broadcast_to([P, len(heads), SK]), True, False)
                        for oc in range(KC):
                            part = [h for h in heads if h // 8 == oc]
                            if part:
                                last = mm(o[:, part[0] - heads[0]:part[-1] - heads[0] + 1, :], q_hi[:, oc, t * P:(t + 1) * P],
                                          k_blk[:, b, 0, part[0]:part[-1] + 1, :], False, part[-1] == heads[-1])
                    last.then_inc(S("a0_s_ps"), 1)

            def turn_max(g):
                pe.wait_ge(S("a0_nm"), g + 1)
                for t in range(GT):
                    last = pe.transpose(psb[0:32, 0, t * P:(t + 1) * P], nm[:, t, :], identb[:, :])
                last.then_inc(S("a0_mT_ps"), 1)

            def scores(g):
                b = g // 2
                pe.wait_ge(S("a0_mT"), g + 1)
                if g:
                    pe.wait_ge(S("a0_oev"), 4 * g)
                for u in range(20):
                    if g and u == 9:
                        turn("r0", g - 1, xlr)
                    if g and u == 12:
                        route_logits(L[0], g - 1)
                    if g + 1 < NG and u == 15:
                        turn("a0", g + 1, xln)
                    if u >= 2:
                        pe.wait_ge(S("a0_exp"), 20 * g + u - 1)
                    o = ps[:, 4 + u % 2, :]
                    if u < H:
                        kh, kl = (k_blk[:, b, i, u, 0:KM] for i in range(2))
                        oc, who, lp, rp = u // 8, msel[:, u, :], identb[:, :], penT[:, g, :]
                    else:
                        r = u - H
                        kh, kl = (k_rem[:, b, i, 4 * r:4 * r + 4, :].rearrange("p h j -> p (h j)") for i in range(2))
                        oc, who = r // 2, mselr[:, 4 * r:4 * r + 4, :].rearrange("p h j -> p (h j)")
                        lp, rp = esel[:, :, :].rearrange("p a j -> p (a j)"), penR[:, g, :]
                    mm(o, kh, q_hi[:, oc, :], True, False)
                    mm(o, kl, q_hi[:, oc, :], False, False)
                    mm(o, kh, q_lo[:, oc, :], False, False)
                    mm(o, lp, rp, False, False)
                    mm(o, who, nmT[:, :], False, True).then_inc(S("a0_st"), 1)

            def weigh_values(g, t):
                b, at = g // 2, 4 + 2 * (t % 2)
                pe.wait_ge(S("a0_plo"), 20 * (g + 1))
                if t >= 2:
                    pe.wait_ge(S("a0_oev"), 4 * g + t - 1)
                elif t == 1 and g:
                    pe.wait_ge(S("r0_slot"), g)
                tk = slice(t * P, (t + 1) * P)
                for j in range(2):
                    o = ps[:, at + j, 0:8 * VW].rearrange("p (h v) -> p h v", v=VW)
                    for h in range(8):
                        mm(o[:, h, :], p_hi[:, 8 * j + h, tk], v_ext[:, b, 8 * j + h, :], h == 0, False, skip_group_check=True)
                        mm(o[:, h, 0:DK + 1], p_lo[:, 8 * j + h, tk], v_ext[:, b, 8 * j + h, 0:DK + 1], False, False, skip_group_check=True)
                    for r in range(2):
                        q = 2 * j + r
                        mm(o[:, 4 * r:4 * r + 4, :], p_hi[:, H + q, tk], v_rem[:, b, q, :, :], False, False, skip_group_check=True)
                        last = mm(o[:, 4 * r:4 * r + 4, 0:DK + 1], p_lo[:, H + q, tk], v_rem[:, b, q, :, 0:DK + 1], False, r == 1, skip_group_check=True)
                last.then_inc(S("a0_o_ps"), 1)

            def turn_out(g, t):
                n = 4 * g + t
                pe.wait_ge(S("a0_on"), n + 1)
                if t == 0:
                    pe.wait_ge(S("a0_mx"), 12 * min(g + 2, NG))
                if n >= 2:
                    pe.wait_ge(S("a0_oT"), n - 1)
                for kc in range(KC):
                    last = pe.transpose(ps[:, t % 2, kc * P:(kc + 1) * P], o_n[:, t, kc * P:(kc + 1) * P], ident[:, :])
                last.then_inc(S("a0_oT_ps"), 1)

            def project_out(g, t):
                n = 4 * g + t
                pe.wait_ge(S("a0_oT"), n + 1)
                if n >= 2:
                    pe.wait_ge(S("a0_x"), n - 1)
                for kc in range(KC):
                    last = mm(ps[:, 2 + t % 2, 0:D], oT[:, t % 2, kc * P:(kc + 1) * P], w_sb["wo"][:, kc, :], kc == 0, kc == 1)
                last.then_inc(S("a0_op_ps"), 1)

            def route_logits(l, g):
                pe.wait_ge(S(l.r + "_xT"), g + 1)
                for t in range(GT):
                    for kc in range(KC):
                        last = mm(ps[:, l.bank, t * E:(t + 1) * E], xTr[:, kc, t * P:(t + 1) * P], gate[l.n][:, kc, :], kc == 0, kc == 1)
                last.then_inc(S(l.r + "_lg_ps"), 1)

            def route_positions(l, g):
                pe.wait_ge(S(l.r + "_sel"), g + 1)
                o = ps[:, l.bank + 1, 0:GT * E]
                mm(o, earlier[:, :], selb[:, :, :].rearrange("p t e -> p (t e)"), True, False)
                mm(o, onesb[:, :], cumb[:, 0:GT, :].rearrange("p t e -> p (t e)"), False, True).then_inc(S(l.r + "_pos_ps"), 1)

            def route_counts(l):
                pe.wait_ge(S(l.r + "_slot"), NG)
                mm(ps[:, l.bank + 1, 0:E], onesb[:, :], cumb[:, GT, :], True, True).then_inc(S(l.r + "_cnt_ps"), 1)

            pe.wait_ge(S("keys_out"), 1)
            turn("a0", 0, xln)
            pe.wait_ge(S("keys_out"), 2)
            project_q("a0", 0, w_sb["wq"])
            score_max(0)
            pe.wait_ge(S("kv_done"), 1)
            for g in range(NG):
                turn_max(g)
                scores(g)
                if g + 1 < NG:
                    project_q("a0", g + 1, w_sb["wq"])
                weigh_values(g, 0)
                if g:
                    route_positions(L[0], g - 1)
                if g + 1 < NG:
                    score_max(g + 1)
                else:
                    for t in range(1, GT):
                        weigh_values(g, t)
                for t in range(GT + 1):
                    if t < GT:
                        turn_out(g, t)
                    if t:
                        project_out(g, t - 1)
            pe.wait_ge(S("a0_x"), NT)
            turn("r0", NG - 1, xlr)
            route_logits(L[0], NG - 1)
            route_positions(L[0], NG - 1)
            route_counts(L[0])

            def experts(l):
                r, tb, pairs = l.r, table[l.n], l.pairs

                def turn_block(g):
                    pe.wait_ge(S(r + "_xraw"), g * 16 + 16)
                    for hf in range(2):
                        for part in range(4):
                            last = pe.transpose(psh[:, 6, part * BLK + hf * P:part * BLK + (hf + 1) * P],
                                                x_raw[:, hf, part * P:(part + 1) * P], identh[:, :])
                    last.then_inc(S(r + "_xbT_ps"), 1)

                def one_block(g, wh, wl, width):
                    pe.wait_ge(S(r + "_xbT"), g + 1)
                    for j in range(pairs):
                        pe.wait_ge(S(r + "_h32"), g * pairs + j + 1)
                        for which, col in enumerate((l.gate_col, l.up_col)):
                            for i in range(2):
                                o = ps[:, 2 * (j % 2) + which, i * BLK:i * BLK + width]
                                for kc in range(KC):
                                    at = col(kc, 2 * j + i)
                                    mm(o, wh[:, at:at + P], xbT[:, 0, kc, 0:width], kc == 0, False)
                                    mm(o, wh[:, at:at + P], xbT[:, 1, kc, 0:width], False, False)
                                    last = mm(o, wl[:, at:at + P], xbT[:, 0, kc, 0:width], False, kc == 1)
                            last.then_inc(S(r + "_gu_ps"), 1)
                    turn_block(g + 1)
                    pe.wait_ge(S(r + "_y"), g + 1)
                    for c in range(l.hc):
                        if c % 2 == 0:
                            pe.wait_ge(S(r + "_h"), g * pairs + c // 2 + 3)
                        at = l.down_at + c * D
                        for hf in range(width // P):
                            o, tk = ps[:, 4 + hf, 0:D], slice(hf * P, (hf + 1) * P)
                            mm(o, h_hi[:, c, tk], wh[:, at:at + D], c == 0, False)
                            mm(o, h_hi[:, c, tk], wl[:, at:at + D], False, False)
                            last = mm(o, h_lo[:, c, tk], wh[:, at:at + D], False, c == l.hc - 1)
                    last.then_inc(S(r + "_down"), 1)

                pe.sem_inc(S(r + "_xbT_ps"), 1)
                pe.sem_inc(S(r + "_down"), 1)
                pe.wait_ge(S(r + "_table"), 1)
                turn_block(0)
                with pe.Fori(0, E // 2) as pr:
                    for slot in range(2):
                        packed = pe.value_load(tb[0:1, bass.ds(pr * 2 + slot + TB_PACKED, 1)], min_val=0, max_val=PACK * 2 * PACK)
                        first, end, half = packed // (2 * PACK), packed // 2 % PACK, packed % 2
                        wait_counted(pe, S(f"w_ready{l.n}"), (pr * 2 + slot + 1) * len(l.chunks))
                        wh, wl = w_hl[slot][:, 0, :], w_hl[slot][:, 1, :]
                        with pe.Fori(first, end) as g:
                            with pe.If(g + half >= end):
                                one_block(g, wh, wl, P)
                            with pe.If(g + half < end):
                                one_block(g, wh, wl, BLK)

            experts(L[0])

            turn("a1", 0, xln, 6)
            project_q("a1", 0, w_sb["Wq"])
            for g in range(NG):
                b = g // 2
                pe.wait_ge(S("a1_q"), g + 1)
                for t in range(GT):
                    for kc in range(KC):
                        last = mm(ps[:, 4 + t // 2, (t % 2) * SK:(t % 2 + 1) * SK], q1T[:, kc, t * P:(t + 1) * P], k1T[:, b, kc, :], kc == 0, kc == 1)
                last.then_inc(S("a1_s_ps"), 1)
                if g:
                    turn("r1", g - 1, xlr)
                    route_logits(L[1], g - 1)
                pe.wait_ge(S("a1_p"), GT * (g + 1))
                for t in range(GT):
                    pe.transpose(ps[:, 6, t * P:(t + 1) * P], att[:, t, 0:KM], ident[:, :])
                for t in range(GT):
                    last = pe.transpose(ps[0:KR, 7, t * P:(t + 1) * P], att[:, t, KM:SK], ident[:, :])
                last.then_inc(S("a1_pT_ps"), 1)
                if g == NG - 1:
                    route_positions(L[1], g - 1)
                pe.wait_ge(S("a1_pT"), 2 * (g + 1))
                for t in range(GT):
                    o = ps[:, t // 2, (t % 2) * D:(t % 2 + 1) * D]
                    mm(o, pT[:, t * P:(t + 1) * P], v1m[:, b, :], True, False)
                    last = mm(o, pTr[0:KR, t * P:(t + 1) * P], v1r[0:KR, b, :], False, True)
                last.then_inc(S("a1_o_ps"), 1)
                if g + 1 < NG:
                    turn("a1", g + 1, xln, 6)
                    if g:
                        pe.wait_ge(S("r1_lg"), g)
                    if g >= 2:
                        pe.wait_ge(S("r1_slot"), g - 1)
                    project_q("a1", g + 1, w_sb["Wq"])
                if 1 <= g < NG - 1:
                    pe.wait_ge(S("a1_q"), g + 2)
                    route_positions(L[1], g - 1)
            pe.wait_ge(S("r1_slot"), NG - 1)
            turn("r1", NG - 1, xlr)
            route_logits(L[1], NG - 1)
            route_positions(L[1], NG - 1)
            route_counts(L[1])
            experts(L[1])

        @block.scalar
        def _(act):
            def x_evac(c, g, dst, bank=0):
                act.wait_ge(S(c + "_xT_ps"), g + 1)
                act.copy(dst[:, :, :], ps[:, bank:bank + 2, :]).then_inc(S(c + "_xT"), 1)

            def q_parts(g):
                act.wait_ge(S("a0_q_ps"), g + 1)
                for oc in range(KC):
                    act.activation(q_hi[:, oc, :], ps[:, 2 + oc, :], ACT.Identity, bias=bcol["bq"][:, oc:oc + 1]).then_inc(S("a0_qhi"), 1)

            def gates(l, g):
                act.wait_ge(S(l.r + "_d"), g + 1)
                act.activation(ev[:, :], dv[:, :], ACT.Exp).then_inc(S(l.r + "_e"), 1)

            def high_part(l, e, slot, n):
                at = l.chunks[n][2]
                act.wait_ge(S(f"staged{l.n}_{n}"), (e + 1) * 16)
                act.copy(w_hl[slot][:, 0, at:at + CH], stage[:, n % STAGES, :]).then_inc(S(f"w_hi{l.n}"), 1)

            act.wait_ge(S("ld_kv"), 13 * 16)
            x_evac("a0", 0, xT)
            q_parts(0)
            for g in range(NG):
                act.wait_ge(S("a0_mT_ps"), g + 1)
                act.copy(nmT[:, :], psb[0:32, 0, 0:GW]).then_inc(S("a0_mT"), 1)
                for u in range(21):
                    if u < 20:
                        act.wait_ge(S("a0_st"), 20 * g + u + 1)
                        if 20 * g + u >= 4:
                            act.wait_ge(S("a0_plo"), 20 * g + u - 3)
                        act.activation(e_ring[:, u % 4, :], ps[:, 4 + u % 2, :], ACT.Exp, scale=float(DK) ** -0.5).then_inc(S("a0_exp"), 1)
                    if u:
                        act.wait_ge(S("a0_exp"), 20 * g + u)
                        act.copy(p_hi[:, u - 1, :], e_ring[:, (u - 1) % 4, :]).then_inc(S("a0_phi"), 1)
                    if g and u == 10:
                        x_evac("r0", g - 1, xTr)
                    if g + 1 < NG and u == 16:
                        x_evac("a0", g + 1, xT)
                if g + 1 < NG:
                    q_parts(g + 1)
                if g:
                    gates(L[0], g - 1)
                for t in range(GT):
                    n = 4 * g + t
                    act.wait_ge(S("a0_o_ps"), n + 1)
                    if n:
                        act.wait_ge(S("a0_oev"), n)
                    at = 4 + 2 * (t % 2)
                    act.copy(o_lo[:, :, :, :], ps[:, at:at + 2, 0:8 * VW].rearrange("p b (h v) -> p b h v", v=VW)[:, :, :, DK + 1:VW]).then_inc(S("a0_olo"), 1)
                for t in range(GT):
                    n = 4 * g + t
                    act.wait_ge(S("a0_oT_ps"), n + 1)
                    if n >= 2:
                        act.wait_ge(S("a0_op_ps"), n - 1)
                    act.copy(oT[:, t % 2, :], ps[:, t % 2, 0:D]).then_inc(S("a0_oT"), 1)
                if g < 2:
                    for n in range(STAGES):
                        high_part(L[0], 0, 0, g * STAGES + n)
            x_evac("r0", NG - 1, xTr)
            gates(L[0], NG - 1)

            def experts(l):
                r, pairs = l.r, l.pairs
                act.sem_inc(S(r + "_y"), 1)
                act.sem_inc(S(r + "_stored"), 16)
                act.wait_ge(S(r + "_table"), 1)

                tb = table[l.n]

                def load(g):
                    row = act.value_load(tb[0:1, bass.ds(g + TB_ROW, 1)], min_val=0, max_val=E * REGION - BLK)
                    act.dma_start(x_raw[:, :, :], rows[bass.ds(row, BLK), :].rearrange("(h p) d -> p h d", p=P)).then_inc(S(r + "_xraw"), 16)

                def one_block(g, coming=None):
                    def split(step):
                        if coming:
                            for n in l.beside[step]:
                                high_part(l, *coming, n)

                    for j in range(pairs + 1):
                        n = g * pairs + j
                        if j < pairs:
                            act.wait_ge(S(r + "_h32"), n + 1)
                            act.wait_ge(S(r + "_gu_ps"), n * 2 + 1)
                            act.activation(s_act[:, j % 2, :], ps[:, 2 * (j % 2), :], l.act).then_inc(S(r + "_s"), 1)
                        if j:
                            act.wait_ge(S(r + "_h32"), n + 2)
                            act.copy(h_hi[:, 2 * j - 2:2 * j, :].rearrange("p c t -> p (c t)"), h32[:, (j - 1) % 2, :]).then_inc(S(r + "_hh"), 1)
                            split(j - 1)
                    act.wait_ge(S(r + "_xbT_ps"), g + 3)
                    load(g + 2)
                    act.wait_ge(S(r + "_down"), g + 2)
                    act.wait_ge(S(r + "_stored"), g * 16 + 16)
                    act.copy(yb[:, :, :], ps[:, 4:6, 0:D]).then_inc(S(r + "_y"), 1)
                    act.wait_ge(S(r + "_y"), g + 2)
                    act.dma_start(results[bass.ds(g * BLK, BLK), :].rearrange("(h p) d -> p h d", p=P), yb[:, :, :]).then_inc(S(r + "_stored"), 16)
                    split(pairs)

                def blocks_of(e, coming=None):
                    first = act.value_load(tb[0:1, bass.ds(e, 1)], min_val=0, max_val=MAXBLK - 1)
                    end = act.value_load(tb[0:1, bass.ds(e + 1, 1)], min_val=1, max_val=MAXBLK)
                    if coming:
                        one_block(first, coming)
                        with act.If(end - first - 1):
                            with act.Fori(first + 1, end) as g:
                                one_block(g)
                    else:
                        with act.Fori(first, end) as g:
                            one_block(g)

                act.wait_ge(S(r + "_padded_first"), 16)
                for n in range(2):
                    act.wait_ge(S(f"{r}_scattered{n}"), 16 * NT * TOP // 2)
                load(0)
                act.wait_ge(S(r + "_padded"), 16 * (E - 1))
                act.wait_ge(S(r + "_xbT_ps"), 2)
                load(1)
                with act.Fori(0, E // 2 - 1) as pr:
                    blocks_of(pr * 2, (pr * 2 + 1, 1))
                    blocks_of(pr * 2 + 1, (pr * 2 + 2, 0))
                blocks_of(E - 2, (E - 1, 1))
                blocks_of(E - 1)
                total = act.value_load(tb[0:1, 8:9], min_val=1, max_val=MAXBLK)
                wait_counted(act, S(r + "_xraw"), total * 16 + 32)
                wait_counted(act, S(r + "_stored"), total * 16 + 16)

            act.wait_ge(S("results_zero"), 16 * (MAXBLK * BLK // (P * 8)))
            experts(L[0])
            for n in range(len(L[1].chunks)):
                high_part(L[1], 0, 0, n)

            def queries_of(g):
                x_evac("a1", g, xT, 6)
                act.wait_ge(S("a1_q_ps"), g + 1)
                for oc in range(KC):
                    last = act.activation(q1T[:, oc, :], ps[:, 2 + oc, :], ACT.Identity, bias=bcol["Bq"][:, oc:oc + 1])
                last.then_inc(S("a1_q"), 1)

            queries_of(0)
            for g in range(NG):
                if g:
                    x_evac("r1", g - 1, xTr)
                act.wait_ge(S("a1_nm"), g + 1)
                for t in range(GT):
                    act.activation(att[:, t, :], att[:, t, :], ACT.Exp, bias=mx1[:, t:t + 1], accum_out=den1[:, t:t + 1]).then_inc(S("a1_p"), 1)
                act.wait_ge(S("a1_pT_ps"), g + 1)
                act.copy(pT[:, :], ps[:, 6, :]).then_inc(S("a1_pT"), 1)
                act.copy(pTr[0:KR, :], ps[0:KR, 7, :]).then_inc(S("a1_pT"), 1)
                if g + 1 < NG:
                    queries_of(g + 1)
                if g:
                    gates(L[1], g - 1)
            x_evac("r1", NG - 1, xTr)
            gates(L[1], NG - 1)
            experts(L[1])

        @block.vector
        def _(dve):
            ch = Chain(dve, S("dve_step"))

            def row_stats(c, g):
                for t in range(GT):
                    ch(dve.bn_stats(stats[:, t, :], x[:, g * GT + t, :]))
                ch.settle()
                for t in range(GT):
                    ch(dve.bn_aggr(mv[c][:, t, :], stats[:, t, :]))
                ch.settle()

            def inverse_root(c):
                y = ry[c][:, :]
                ch(dve.tensor_scalar(ve[:, :], mv[c][:, :, 1], EPS, None, ALU.add))
                ch.settle()
                ch(dve.tensor_scalar(y.bitcast(I32), ve[:, :].bitcast(I32), -0.5, 1597463007.0, ALU.mult, ALU.add))
                ch.settle()
                for step in range(3):
                    ch(dve.tensor_tensor(rt[:, :], y, y, ALU.mult))
                    ch.settle()
                    ch(dve.scalar_tensor_tensor(rt[:, :], rt[:, :], -0.5, ve[:, :], ALU.mult, ALU.mult))
                    ch.settle()
                    last = dve.scalar_tensor_tensor(y, rt[:, :], 1.5, y, ALU.add, ALU.mult)
                    if step < 2:
                        ch(last)
                        ch.settle()
                last.then_inc(S(c + "_root"), 1)

            def layernorm(c, g, dst, roots):
                row_stats(c, g)
                inverse_root(c)
                dve.wait_ge(S(c + "_root"), roots + 1)
                for t in range(GT):
                    ins = dve.tensor_scalar(dst[:, t, :], x[:, g * GT + t, :], mv[c][:, t, 0:1], ry[c][:, t:t + 1], ALU.subtract, ALU.mult)
                    if t < GT - 1:
                        ch(ins)
                ins.then_inc(S(c + "_ln"), 1)

            dve.wait_ge(S("consts"), 1)
            ch(dve.tensor_tensor(le[:, :, :], iota8[:, :].unsqueeze(1).broadcast_to([P, 8, 8]),
                                 iota8[:, :].unsqueeze(2).broadcast_to([P, 8, 8]), ALU.is_le))
            ch(dve.tensor_reduce(head_of[:, :], ident[:, :].rearrange("p (h d) -> p h d", d=DK), AX, ALU.max))
            ch(dve.tensor_reduce(quad_of[:, :], ident[:, :].rearrange("p (a j) -> p a j", j=QW)[:, :, 0:KR], AX, ALU.max))
            ch(dve.tensor_tensor(m16[:, :], ident[0:32, 0:H], ident[0:32, H:2 * H], ALU.add))
            ch(dve.tensor_copy(esel[:, :, :], ident[0:32, 0:QW].unsqueeze(1).broadcast_to([32, 4, QW])))
            ch.settle()
            ch(dve.tensor_copy(msel[:, :, :], m16[:, :].unsqueeze(2).broadcast_to([32, H, P])))
            ch(dve.tensor_copy(mselr[:, :, :], m16[:, :].unsqueeze(2).broadcast_to([32, H, QW])))
            dve.wait_ge(S("blanks"), 1)
            dve.wait_ge(S("ld_kv"), 13 * 16)
            for b in range(B):
                for kc in range(KC):
                    ins = dve.tensor_copy(ctxR[:, b, kc, :, 0:KR], ctxT[:, b, kc, KM:SK].unsqueeze(1).broadcast_to([P, 4, KR]))
                    if (b, kc) != (B - 1, KC - 1):
                        ch(ins)
            ins.then_inc(S("ctx_rep"), 1)
            dve.wait_ge(S("ld_x0"), 16)
            layernorm("a0", 0, xln, 0)

            def key_parts(b):
                for oc in range(KC):
                    kp, bk, kt = ps[:, b, oc * SK:(oc + 1) * SK], bcol["bk"][:, oc:oc + 1], k_parts[b]
                    ch(dve.tensor_scalar(kt[:, oc, 0, :], kp, bk, None, ALU.add))
                    ch.settle()
                    ch(dve.scalar_tensor_tensor(kt[:, oc, 1, :], kp, bk, kt[:, oc, 0, :], ALU.add, ALU.subtract))
                ch.settle()

            def key_blocks(b, oc, i):
                hs = slice(8 * oc, 8 * oc + 8)
                ch(dve.tensor_tensor(k_blk[:, b, i, hs, :], k_parts[b][:, oc, i, :].unsqueeze(1).broadcast_to([P, 8, SK]),
                                     head_of[:, :].unsqueeze(2).broadcast_to([P, 8, SK]), ALU.mult))
                ch.settle()
                last = dve.tensor_copy(k_rem[:, b, i, hs, 0:KR], k_blk[:, b, i, hs, KM:SK])
                if (oc, i) == (KC - 1, 1):
                    last.then_inc(S("keys_set"), 1)
                else:
                    ch(last)

            dve.wait_ge(S("kv_ps"), 1)
            key_parts(0)
            key_parts(1)
            dve.engine_nop().then_inc(S("keys_out"), 1)
            dve.wait_ge(S("kv_ps"), 2)
            for b in range(B):
                for oc in range(KC):
                    ins = dve.tensor_scalar(k1T[:, b, oc, :], ps[:, 2 + b, oc * SK:(oc + 1) * SK], bcol["Bk"][:, oc:oc + 1], None, ALU.add)
                    if (b, oc) != (B - 1, KC - 1):
                        ch(ins)
            ins.then_inc(S("keys_out"), 1)
            for oc in range(KC):
                for i in range(2):
                    key_blocks(0, oc, i)
            dve.wait_ge(S("kv_ps"), 4)
            for b in range(B):
                for rem in range(2):
                    vh = v_hl[:, :, :].rearrange("p i (h d) -> p i h d", d=DK)
                    ch(dve.tensor_tensor(v_tmp[:, :], ps[:, 4 + rem, b * D:(b + 1) * D], brow["bv"][:, :], ALU.add))
                    ch.settle()
                    ch(dve.tensor_copy(v_hl[:, 0, :], v_tmp[:, :]))
                    ch.settle()
                    ch(dve.tensor_tensor(v_hl[:, 1, :], v_tmp[:, :], v_hl[:, 0, :], ALU.subtract))
                    ch.settle()
                    for i, at in ((0, 0), (1, DK + 1)):
                        if not rem:
                            ch(dve.tensor_copy(v_ext[:, b, :, at:at + DK], vh[:, i, :, :]))
                            continue
                        for q in range(4):
                            ch(dve.tensor_tensor(v_rem[:, b, q, :, at:at + DK], vh[:, i, 4 * q:4 * q + 4, :],
                                                 quad_of[:, :].unsqueeze(2).broadcast_to([P, 4, DK]), ALU.mult))
                            if i == 0:
                                ch(dve.tensor_copy(v_rem[:, b, q, :, DK:DK + 1], quad_of[:, :].unsqueeze(2)))
                    ch.settle()
            for b in range(B):
                ch(dve.tensor_tensor(v1m[:, b, :], ps[:, 6, b * D:(b + 1) * D], brow["Bv"][:, :], ALU.add))
                ins = dve.tensor_tensor(v1r[0:KR, b, :], ps[0:KR, 7, b * D:(b + 1) * D], brow["Bv"][0:KR, :], ALU.add)
                if b < B - 1:
                    ch(ins)
            ins.then_inc(S("kv_done"), 1)

            def q_low(g):
                for oc in range(KC):
                    dve.wait_ge(S("a0_qhi"), 2 * g + oc + 1)
                    dve.scalar_tensor_tensor(q_lo[:, oc, :], ps[:, 2 + oc, :], bcol["bq"][:, oc:oc + 1], q_hi[:, oc, :],
                                             ALU.add, ALU.subtract).then_inc(S("a0_qlo"), 1)

            def head_outputs(g, t):
                n, at = 4 * g + t, 4 + 2 * (t % 2)
                o = ps[:, at:at + 2, 0:8 * VW].rearrange("p b (h v) -> p b h v", v=VW)
                dve.wait_ge(S("a0_olo"), n + 1)
                if n:
                    dve.wait_ge(S("a0_on"), n)
                ch(dve.tensor_tensor(o_sum[:, :, :, :], o[:, :, :, 0:DK], o_lo[:, :, :, :], ALU.add))
                dve.reciprocal(rden[:, :, :], o[:, :, :, DK]).then_inc(S("a0_oev"), 1)
                dve.wait_ge(S("a0_oev"), n + 1)
                on = o_n[:, t, :].rearrange("p (h d) -> p h d", d=DK)
                dve.tensor_tensor(on, o_sum[:, :, :, :].rearrange("p b h d -> p (b h) d"),
                                  rden[:, :, :].rearrange("p b h -> p (b h)").unsqueeze(2).broadcast_to([P, H, DK]), ALU.mult).then_inc(S("a0_on"), 1)

            def maxima(g):
                for n in range(12):
                    t, h0, at = n // 3, (n % 3) * 6, 2 * (n % 2)
                    if n % 3 == 0 and g:
                        head_outputs(g - 1, n // 3)
                    dve.wait_ge(S("a0_s_ps"), 12 * g + n + 1)
                    if n % 3 < 2:
                        v = ps[:, at:at + 2, 0:3 * SK].rearrange("p b (h s) -> p b h s", s=SK)
                        dve.tensor_reduce(mx[:, t, h0:h0 + 6].rearrange("p (b h) -> p b h", b=2), v, AX, ALU.max).then_inc(S("a0_mx"), 1)
                    else:
                        ch(dve.tensor_reduce(mx[:, t, h0:h0 + 3], ps[:, at, 0:3 * SK].rearrange("p (h s) -> p h s", s=SK), AX, ALU.max))
                        dve.tensor_reduce(mx[:, t, h0 + 3:h0 + 4], ps[:, at + 1, 0:SK].unsqueeze(1), AX, ALU.max).then_inc(S("a0_mx"), 1)
                dve.wait_ge(S("a0_mx"), 12 * (g + 1))
                ch(dve.tensor_scalar(nm[:, :, 0:H], mx[:, :, :], -1.0, None, ALU.mult))
                ch.settle()
                dve.scalar_tensor_tensor(nm[:, :, H:2 * H], mx[:, :, :], -1.0, nm[:, :, 0:H], ALU.mult, ALU.subtract).then_inc(S("a0_nm"), 1)

            def rows_to_send(g):
                if g >= 2:
                    dve.wait_ge(S(f"r1_scattered{g % 2}"), 16 * GT * TOP * (g // 2))
                dve.wait_ge(S("r1_ln"), g + 1)
                o = xps[g % 2]
                ch(dve.tensor_copy(o[:, :, 0:D], xlr[:, :, :]))
                ch.settle()
                dve.tensor_tensor(o[:, :, D:2 * D], xlr[:, :, :], o[:, :, 0:D], ALU.subtract).then_inc(S("r1_xp"), 1)

            def choose(l, g):
                r = l.r
                tg = slice(g * GT, (g + 1) * GT)
                dve.wait_ge(S(r + "_lg_ps"), g + 1)
                dve.tensor_copy(lg[:, :, :].rearrange("p t e -> p (t e)"), ps[:, l.bank, 0:GT * E]).then_inc(S(r + "_lg"), 1)
                dve.wait_ge(S(r + "_lg"), g + 1)
                for t in range(GT):
                    ch(dve.max(mx8[:, t, :], lg[:, t, :]))
                ch.settle()
                for t in range(GT):
                    ch(dve.max_index(ix8[:, t, :], mx8[:, t, :], lg[:, t, :]))
                dve.tensor_tensor(dv[:, :], mx8[:, :, 1], mx8[:, :, 0], ALU.subtract).then_inc(S(r + "_d"), 1)
                ch.settle()
                ch(dve.tensor_copy(idxf[:, tg, :], ix8[:, :, 0:TOP]))
                ch.settle()
                for t in range(g * GT, (g + 1) * GT):
                    ch(dve.tensor_tensor(oh[:, t, :, :], iota8[:, :].unsqueeze(1).broadcast_to([P, TOP, E]),
                                         idxf[:, t, :].unsqueeze(2).broadcast_to([P, TOP, E]), ALU.is_equal))
                ch.settle()
                ch(dve.tensor_tensor(sel[:, :, :], oh[:, tg, 0, :], oh[:, tg, 1, :], ALU.add))
                if g == 0:
                    ch(dve.memset(cum[:, 0, :], 0.0))
                else:
                    ch(dve.tensor_copy(cum[:, 0, :], cum[:, GT, :]))
                ch.settle()
                ch(dve.tensor_copy(selb[:, :, :], sel[:, :, :]))
                for t in range(GT):
                    ch(dve.tensor_tensor(cum[:, t + 1, :], cum[:, t, :], sel[:, t, :], ALU.add))
                    ch.settle()
                dve.tensor_copy(cumb[:, :, :], cum[:, :, :]).then_inc(S(r + "_sel"), 1)

            def place(l, g):
                r = l.r
                tg = slice(g * GT, (g + 1) * GT)
                dve.wait_ge(S(r + "_pos_ps"), g + 1)
                pos = ps[:, l.bank + 1, 0:GT * E].rearrange("p (t e) -> p t e", e=E)
                for k in range(TOP):
                    ch(dve.tensor_tensor(ohp[:, tg, k, :], oh[:, tg, k, :], pos, ALU.mult))
                ch.settle()
                ch(dve.tensor_reduce(posk[:, :, :], ohp[:, tg, :, :], AX, ALU.add))
                dve.wait_ge(S(r + "_e"), g + 1)
                ch(dve.tensor_scalar(dn[:, :], ev[:, :], 1.0, None, ALU.add))
                ch.settle()
                ch(dve.reciprocal(weight[:, tg, 0], dn[:, :]))
                ch(dve.tensor_scalar(drop[:, :, :], posk[:, :, :], float(l.cap), None, ALU.is_ge))
                ch(dve.tensor_scalar(pos_kept[:, tg, :], posk[:, :, :], float(l.cap - 1), None, ALU.min))
                ch(dve.scalar_tensor_tensor(slotf[:, tg, :], idxf[:, tg, :], float(REGION), posk[:, :, :], ALU.mult, ALU.add))
                ch.settle()
                ch(dve.tensor_tensor(weight[:, tg, 1], weight[:, tg, 0], ev[:, :], ALU.mult))
                ch.settle()
                ch(dve.tensor_scalar(posk[:, :, :], drop[:, :, :], -1.0, 1.0, ALU.mult, ALU.add))
                ch.settle()
                ch(dve.tensor_tensor(weight[:, tg, :], weight[:, tg, :], posk[:, :, :], ALU.mult))
                dve.scalar_tensor_tensor(slot_s[:, tg, :], drop[:, :, :], float(FAR), slotf[:, tg, :], ALU.mult, ALU.add).then_inc(S(r + "_slot"), 1)

            def count(l):
                r, tb = l.r, table[l.n]
                ch(dve.memset(tb[:, :], 0))
                dve.wait_ge(S(r + "_cnt_ps"), 1)
                ch(dve.tensor_scalar(cnt[:, :], ps[:, l.bank + 1, 0:E], float(l.cap), None, ALU.min))
                ch.settle()
                ch(dve.tensor_tensor(over[:, :, :], cnt[:, :].unsqueeze(2).broadcast_to([P, E, 7]),
                                     thr[:, :].unsqueeze(1).broadcast_to([P, E, 7]), ALU.is_gt))
                ch.settle()
                ch(dve.tensor_reduce(nblk[:, :], over[:, :, :], AX, ALU.add))
                ch.settle()
                ch(dve.tensor_scalar(nblk[:, :], nblk[:, :], 1.0, None, ALU.add))
                ch.settle()
                ch(dve.tensor_tensor(lem[:, :, :], le[:, :, :], nblk[:, :].unsqueeze(1).broadcast_to([P, E, E]), ALU.mult))
                ch.settle()
                ch(dve.tensor_reduce(blk_end[:, :], lem[:, :, :], AX, ALU.add))
                ch.settle()
                be = blk_end[0:1, :]
                ch(dve.tensor_copy(tb[0:1, 1:9], be))
                ch(dve.tensor_tensor(passed[:, :, :], iota[0:1, :].unsqueeze(2).broadcast_to([1, AHEAD, E]),
                                     be.unsqueeze(1).broadcast_to([1, AHEAD, E]), ALU.is_ge))
                ch(dve.tensor_scalar(skipped[:, :], nblk[0:1, :], float(-BLK), float(REGION), ALU.mult, ALU.add))
                ch(dve.tensor_tensor(first_block[:, :], be, nblk[0:1, :], ALU.subtract))
                ch(dve.scalar_tensor_tensor(room[:, :], nblk[0:1, :], float(BLK), cnt[0:1, :], ALU.mult, ALU.subtract))
                ch(dve.tensor_scalar(in_use[:, :], iota[0:1, :], blk_end[0:1, 7:8], None, ALU.is_lt))
                ch(dve.scalar_tensor_tensor(tb[0:1, TB_PAD:TB_PAD + E], iota8[0:1, :], float(REGION), cnt[0:1, :], ALU.mult, ALU.add))
                ch.settle()
                ch(dve.tensor_tensor(passed[:, :, :], passed[:, :, :], skipped[:, :].unsqueeze(1).broadcast_to([1, AHEAD, E]), ALU.mult))
                ch.settle()
                ch(dve.tensor_scalar(room[:, :], room[:, :], float(P), None, ALU.is_ge))
                ch(dve.scalar_tensor_tensor(first_block[:, :], first_block[:, :], float(PACK), be, ALU.mult, ALU.add))
                ch(dve.tensor_reduce(row_of[:, :], passed[:, :, :], AX, ALU.add))
                ch.settle()
                ch(dve.scalar_tensor_tensor(row_of[:, :], iota[0:1, :], float(BLK), row_of[:, :], ALU.mult, ALU.add))
                ch.settle()
                ch(dve.scalar_tensor_tensor(tb[0:1, TB_PACKED:TB_PACKED + E], first_block[:, :], 2.0, room[:, :], ALU.mult, ALU.add))
                dve.tensor_tensor(tb[0:1, TB_ROW:TB_ROW + AHEAD], row_of[:, :], in_use[:, :], ALU.mult).then_inc(S(r + "_table"), 1)
                ch(dve.tensor_tensor(blk_row[:, :], blk_end[:, :], nblk[:, :], ALU.subtract))
                ch.settle()
                for k in range(TOP):
                    ch(dve.tensor_tensor(ohp[:, :, k, :], oh[:, :, k, :], blk_row[:, :].unsqueeze(1).broadcast_to([P, NT, E]), ALU.mult))
                ch.settle()
                ch(dve.tensor_reduce(slotf[:, :, :], ohp[:, :, :, :], AX, ALU.add))
                ch.settle()
                dve.scalar_tensor_tensor(slot_g[:, :, :], slotf[:, :, :], float(BLK), pos_kept[:, :, :], ALU.mult, ALU.add).then_inc(S(r + "_slotg"), 1)

            q_low(0)
            maxima(0)
            for g in range(NG):
                if g:
                    row_stats("r0", g - 1)
                    inverse_root("r0")
                for u in range(20):
                    dve.wait_ge(S("a0_phi"), 20 * g + u + 1)
                    dve.tensor_tensor(p_lo[:, u, :], e_ring[:, u % 4, :], p_hi[:, u, :], ALU.subtract).then_inc(S("a0_plo"), 1)
                    if g + 1 < NG and u == 4:
                        dve.wait_ge(S(f"ld_x{g + 1}"), 16)
                        dve.wait_ge(S("a0_ln"), g + 1)
                        row_stats("a0", g + 1)
                    if g + 1 < NG and u == 7:
                        inverse_root("a0")
                    if g == 0 and 9 <= u < 13:
                        key_blocks(1, (u - 9) // 2, (u - 9) % 2)
                if g:
                    choose(L[0], g - 1)
                if g + 1 < NG:
                    q_low(g + 1)
                if g:
                    place(L[0], g - 1)
                if g + 1 < NG:
                    maxima(g + 1)
                else:
                    for t in range(GT):
                        head_outputs(g, t)
                for t in range(GT):
                    n = 4 * g + t
                    dve.wait_ge(S("a0_op_ps"), n + 1)
                    if n:
                        dve.wait_ge(S("a0_x"), n)
                    ch(dve.tensor_tensor(xo[:, :], ps[:, 2 + t % 2, 0:D], brow["bo"][:, :], ALU.add))
                    ch.settle()
                    dve.tensor_tensor(x[:, n, :], x[:, n, :], xo[:, :], ALU.add).then_inc(S("a0_x"), 1)
                dve.wait_ge(S("a0_x"), 4 * (g + 1))
            dve.wait_ge(S("r0_xT_ps"), NG - 1)
            dve.wait_ge(S("r0_xp"), NG - 1)
            layernorm("r0", NG - 1, xlr, NG - 1)
            choose(L[0], NG - 1)
            place(L[0], NG - 1)
            count(L[0])

            def experts(l):
                r, pairs = l.r, l.pairs
                dve.wait_ge(S(r + "_table"), 1)
                total = dve.value_load(table[l.n][0:1, 8:9], min_val=1, max_val=MAXBLK)
                dve.sem_inc(S(r + "_h"), 2)
                dve.sem_inc(S(r + "_h32"), 2)

                def turned(g):
                    dve.wait_ge(S(r + "_xbT_ps"), g + 2)
                    dve.tensor_copy(xbT[:, :, :, :].rearrange("p a b c -> p (a b c)"), psh[:, 6, :]).then_inc(S(r + "_xbT"), 1)

                turned(0)
                with dve.Fori(0, total) as g:
                    for j in range(pairs + 1):
                        n = g * pairs + j
                        if j < pairs:
                            dve.wait_ge(S(r + "_s"), n + 1)
                            dve.wait_ge(S(r + "_gu_ps"), n * 2 + 2)
                            dve.wait_ge(S(r + "_h"), n + 1)
                            dve.tensor_tensor(h32[:, j % 2, :], s_act[:, j % 2, :], ps[:, 2 * (j % 2) + 1, :], ALU.mult).then_inc(S(r + "_h32"), 1)
                        if j:
                            if j == 1:
                                dve.wait_ge(S(r + "_down"), g + 1)
                            dve.wait_ge(S(r + "_hh"), n)
                            dve.tensor_tensor(h_lo[:, 2 * j - 2:2 * j, :].rearrange("p c t -> p (c t)"), h32[:, (j - 1) % 2, :],
                                              h_hi[:, 2 * j - 2:2 * j, :].rearrange("p c t -> p (c t)"), ALU.subtract).then_inc(S(r + "_h"), 1)
                    turned(g + 1)

            def combine(l, t):
                r = l.r
                dve.wait_ge(S(f"{r}_gathered{t % GT}"), 32 * (t // GT + 1))
                ch(dve.scalar_tensor_tensor(x[:, t, :], gb[:, t % GT, 0, :], weight[:, t, 0:1], x[:, t, :], ALU.mult, ALU.add))
                ch.settle()
                dve.scalar_tensor_tensor(x[:, t, :], gb[:, t % GT, 1, :], weight[:, t, 1:2], x[:, t, :], ALU.mult, ALU.add).then_inc(S(r + "_x"), 1)

            experts(L[0])

            def combine_group(g):
                for t in range(g * GT, (g + 1) * GT):
                    combine(L[0], t)
                dve.wait_ge(S("r0_x"), GT * (g + 1))
                layernorm("a1", g, xln, g)

            combine_group(0)
            dve.wait_ge(S("phi_set"), 1)
            for g in range(NG):
                dve.wait_ge(S("a1_s_ps"), g + 1)
                for j in range(2):
                    ch(dve.scalar_tensor_tensor(att[:, 2 * j:2 * j + 2, :], ps[:, 4 + j, 0:2 * SK].rearrange("p (t s) -> p t s", s=SK), float(D) ** -0.5,
                                                phi[:, g * GT + 2 * j:g * GT + 2 * j + 2, :], ALU.mult, ALU.add))
                ch.settle()
                ch(dve.tensor_reduce(mx1[:, :], att[:, :, :], AX, ALU.max))
                ch.settle()
                dve.tensor_scalar(mx1[:, :], mx1[:, :], -1.0, None, ALU.mult).then_inc(S("a1_nm"), 1)
                if g + 1 < NG:
                    combine_group(g + 1)
                if g:
                    choose(L[1], g - 1)
                if g == NG - 1:
                    place(L[1], g - 1)
                dve.wait_ge(S("a1_p"), GT * (g + 1))
                ch(dve.reciprocal(rd1[:, :], den1[:, :]))
                ch.settle()
                dve.wait_ge(S("a1_o_ps"), g + 1)
                for t in range(GT):
                    n = g * GT + t
                    dve.scalar_tensor_tensor(x[:, n, :], ps[:, t // 2, (t % 2) * D:(t % 2 + 1) * D], rd1[:, t:t + 1], x[:, n, :],
                                             ALU.mult, ALU.add).then_inc(S("a1_x"), 1)
                dve.wait_ge(S("a1_x"), GT * (g + 1))
                if g:
                    dve.wait_ge(S("r1_xT_ps"), g)
                layernorm("r1", g, xlr, g)
                rows_to_send(g)
                if 1 <= g < NG - 1:
                    place(L[1], g - 1)
            choose(L[1], NG - 1)
            place(L[1], NG - 1)
            count(L[1])
            experts(L[1])
            for t in range(NT):
                combine(L[1], t)


def kernel(**inputs):
    import numpy as np
    import concourse.bacc as bacc
    from concourse.bass_utils import run_bass_kernel_spmd

    i = {k: np.asarray(v) for k, v in inputs.items()}

    def by_row_chunk(w):
        e, r, c = w.shape
        return w.reshape(e, r // P, P, c).transpose(0, 2, 1, 3).reshape(e, P, -1)

    def column(b):
        return b.reshape(KC, P).T

    laid = {
        "x": i["x"].reshape(N, D),
        "ctxT": i["ctx_1024"].transpose(0, 2, 1),
        "mask": i["mask_BxSxS2_ik0"].reshape(N, SK),
        "maskT": i["mask_BxSxS2_ik0"].transpose(0, 2, 1),
        "phi": i["fside_BxSxS2_0"].reshape(N, SK),
        "wq": i["L0_xattn_wq"], "wk": i["L0_xattn_wk"], "wv": i["L0_xattn_wv"], "wo": i["L0_xattn_wo"],
        "bq": column(i["L0_xattn_bq"]), "bk": column(i["L0_xattn_bk"]), "bv": i["L0_xattn_bv"], "bo": i["L0_xattn_bo"],
        "Wq": i["L1_xattn_Wq"].T, "Wk": i["L1_xattn_Wk"].T, "Wv": i["L1_xattn_Wv"].T,
        "Bq": column(i["L1_xattn_bq"]), "Bk": column(i["L1_xattn_bk"]), "Bv": i["L1_xattn_bv"],
        "betas": np.stack([i["L1_xattn_beta_risk"].reshape(1), i["L1_xattn_beta_prio"].reshape(1), i["L1_xattn_beta_impl"].reshape(1)]),
        "gate0": i["L0_ffn_gate_w"].T, "gate1": i["L1_ffn_Wg"].T,
        "wg": by_row_chunk(i["L0_ffn_wg"].transpose(0, 2, 1)),
        "wu": by_row_chunk(i["L0_ffn_wu"].transpose(0, 2, 1)),
        "wd": by_row_chunk(i["L0_ffn_wd"].transpose(0, 2, 1)),
        "W1": by_row_chunk(i["L1_ffn_W1"]),
        "W2": by_row_chunk(i["L1_ffn_W2"]),
    }
    nc = bacc.Bacc("TRN2", target_bir_lowering=False, num_devices=1)
    arrays, a = {}, {}
    for name, v in laid.items():
        v = np.ascontiguousarray(v)
        arrays["in_" + name] = v
        a[name] = nc.dram_tensor("in_" + name, v.shape, mybir.dt.from_np(v.dtype), kind="ExternalInput").ap()
    out = nc.dram_tensor("out_x", (N, D), F32, kind="ExternalOutput").ap()
    two_layers(nc, a, out)
    r = run_bass_kernel_spmd(nc, [arrays], core_ids=[0])
    return r.results[0]["out_x"].reshape(i["x"].shape)
```
